# Optimizing a Trainium2 kernel written in Bass

```python
import numpy as np
import jax
import jax.numpy as jnp

def _softmax(x, axis=-1):
    return jax.nn.softmax(x, axis=axis)
def _gelu(x):
    return jax.nn.gelu(x, approximate=True)
def _silu(x):
    return jax.nn.silu(x)
def _sigmoid(x):
    return jax.nn.sigmoid(x)
def _layernorm(x, axis=-1, eps=1e-5):
    m = jnp.mean(x, axis=axis, keepdims=True)
    v = jnp.var(x, axis=axis, keepdims=True)
    return (x - m) / jnp.sqrt(v + eps)
def _scatter_add(tgt, idx, src, axis=0):
    return tgt.at[idx].add(src)
def _segment_sum(src, seg, n):
    return jax.ops.segment_sum(src, seg, n)

kernel_name = 'mk_conv_preact_d4_conv_nchw384_ccd8ad'

def setup_inputs(seed: int = 0):
    np.random.seed(seed)
    _w = jnp.asarray
    def _rec_inputs():
        import jax
        import jax.numpy as jnp
        _gk = jax.random.key(seed)
        x = -0.0005963 + 1.001 * jax.random.normal(jax.random.fold_in(_gk, 1), (8, 384, 32, 32), jnp.float32)
        return x
    x = _rec_inputs()
    def _L0_conv_setup():
        import jax, jax.numpy as jnp
        import numpy as np
        from jax import lax
        DIM = 384
        NUM_HEADS = 12
        HEAD_DIM = DIM // NUM_HEADS
        SCALE = HEAD_DIM ** (-0.5)
        key = jax.random.key(seed)
        ks = jax.random.split(key, 7)
        B, H, W = (8, 32, 32)
        s = 0.02
        return {'x': jax.random.normal(ks[0], (B, DIM, H, W), jnp.float32), 'qkvo_w': jax.random.normal(ks[1], (4 * DIM, DIM, 1, 1), jnp.float32) * s, 'qkvo_b': jax.random.normal(ks[2], (4 * DIM,), jnp.float32) * s, 'lepe_w': jax.random.normal(ks[3], (DIM, 1, 5, 5), jnp.float32) * s, 'lepe_b': jax.random.normal(ks[4], (DIM,), jnp.float32) * s, 'proj_w': jax.random.normal(ks[5], (DIM, DIM, 1, 1), jnp.float32) * s, 'proj_b': jax.random.normal(ks[6], (DIM,), jnp.float32) * s}
    _L0_conv_all = _L0_conv_setup()
    _L0_conv_in = {k: v for k, v in _L0_conv_all.items() if k in ('qkvo_w', 'qkvo_b', 'lepe_w', 'lepe_b', 'proj_w', 'proj_b', )}
    del _L0_conv_all

    def _L1_conv_setup():
        import jax, jax.numpy as jnp
        import numpy as np
        D_MODEL = 192
        D_STATE = 16
        SSM_RATIO = 2.0
        D_INNER = int(SSM_RATIO * D_MODEL)
        DT_RANK = int(np.ceil(D_MODEL / 16))
        K_GROUP = 4
        BATCH, HH, WW = (4, 32, 32)
        DT_MIN, DT_MAX = (0.001, 0.1)
        LN_EPS = 1e-05

        def _cross_scan(x):
            B, D, H, W = x.shape
            x0 = x.reshape(B, D, H * W)
            x1 = jnp.transpose(x, (0, 1, 3, 2)).reshape(B, D, H * W)
            return jnp.stack([x0, x1, x0[..., ::-1], x1[..., ::-1]], axis=1)

        def _cross_merge(ys, H, W):
            B, K, D, L = ys.shape
            y0 = ys[:, 0]
            y2 = ys[:, 2][..., ::-1]
            yt = ys[:, 1] + ys[:, 3][..., ::-1]
            yt = jnp.transpose(yt.reshape(B, D, W, H), (0, 1, 3, 2)).reshape(B, D, L)
            return y0 + y2 + yt

        def _selective_scan(u, dt, A, Bs, Cs):
            dt_l = jnp.moveaxis(dt, -1, 0)
            u_l = jnp.moveaxis(u, -1, 0)
            B_l = jnp.moveaxis(Bs, -1, 0)
            C_l = jnpp_move = jnp.moveaxis(Cs, -1, 0)

            def step(h, inp):
                dtt, ut, bt, ct = inp
                dA = jnp.exp(dtt[..., None] * A)
                h = h * dA + (dtt * ut)[..., None] * bt[:, :, None, :]
                y = jnp.einsum('bkdn,bkn->bkd', h, ct)
                return (h, y)
            h0 = jnp.zeros(u.shape[:3] + (A.shape[-1],), dtype=u.dtype)
            _, ys = jax.lax.scan(step, h0, (dt_l, u_l, B_l, C_l))
            return jnp.moveaxis(ys, 0, -1)
        key = jax.random.key(seed)
        ks = jax.random.split(key, 6)
        x = jax.random.normal(ks[0], (BATCH, D_INNER, HH, WW), dtype=jnp.float32)
        x_proj_weight = jax.random.normal(ks[1], (K_GROUP, DT_RANK + 2 * D_STATE, D_INNER), dtype=jnp.float32) * D_INNER ** (-0.5)
        dt_projs_weight = jax.random.normal(ks[2], (K_GROUP, D_INNER, DT_RANK), dtype=jnp.float32) * DT_RANK ** (-0.5)
        dt = jnp.exp(jax.random.uniform(ks[3], (K_GROUP, D_INNER)) * (np.log(DT_MAX) - np.log(DT_MIN)) + np.log(DT_MIN))
        dt = jnp.clip(dt, 0.0001, None)
        dt_projs_bias = dt + jnp.log(-jnp.expm1(-dt))
        A = jnp.tile(jnp.arange(1, D_STATE + 1, dtype=jnp.float32)[None, :], (K_GROUP * D_INNER, 1))
        A_logs = jnp.log(A)
        Ds = jnp.ones((K_GROUP * D_INNER,), dtype=jnp.float32)
        ln_weight = jnp.ones((D_INNER,), dtype=jnp.float32)
        ln_bias = jnp.zeros((D_INNER,), dtype=jnp.float32)
        return {'x': x, 'x_proj_weight': x_proj_weight, 'dt_projs_weight': dt_projs_weight, 'dt_projs_bias': dt_projs_bias, 'A_logs': A_logs, 'Ds': Ds, 'ln_weight': ln_weight, 'ln_bias': ln_bias}
    _L1_conv_all = _L1_conv_setup()
    _L1_conv_in = {k: v for k, v in _L1_conv_all.items() if k in ('x_proj_weight', 'dt_projs_weight', 'dt_projs_bias', 'A_logs', 'Ds', 'ln_weight', 'ln_bias', )}
    del _L1_conv_all

    def _L2_conv_setup():
        import jax, jax.numpy as jnp
        from jax import lax
        import numpy as np
        H, W = (64, 64)
        K = 5
        SIGMA = 0.5
        CHAN_PER_POS = 8
        INIT_STRIDE = 16
        BATCH = 32

        def _num_offsets(h, w, s):
            ny = (h - s) // s * 2 + 1
            nx = (w - s) // s * 2 + 1
            return (ny, nx, ny * nx - 1)

        def _displace(x, off_int):
            _, _, _, h, w = x.shape

            def shift_one(xp, dxy):
                dx, dy = (dxy[0], dxy[1])
                ys = jnp.arange(h) - dy
                xs = jnp.arange(w) - dx
                ym = (ys >= 0) & (ys < h)
                xm = (xs >= 0) & (xs < w)
                ysc = jnp.clip(ys, 0, h - 1)
                xsc = jnp.clip(xs, 0, w - 1)
                out = xp[:, :, ysc][:, :, :, xsc]
                return out * (ym[:, None] & xm[None, :]).astype(xp.dtype)
            return jax.vmap(shift_one, in_axes=(1, 0), out_axes=1)(x, off_int)
        key = jax.random.key(seed)
        k1, k2 = jax.random.split(key)
        ny, nx, npos = _num_offsets(H, W, INIT_STRIDE)
        C = npos * CHAN_PER_POS
        x = jax.random.normal(k1, (BATCH, C, H, W), dtype=jnp.float32)
        offs = []
        for ih in range(-(ny // 2), ny // 2 + 1):
            for iw in range(-(nx // 2), nx // 2 + 1):
                if ih == 0 and iw == 0:
                    continue
                offs.append([iw * INIT_STRIDE, ih * INIT_STRIDE])
        offset = jnp.asarray(np.array(offs, dtype=np.float32))
        offset = offset + jax.random.uniform(k2, offset.shape, dtype=jnp.float32, minval=-0.4, maxval=0.4)
        return {'x': x, 'offset': offset}
    _L2_conv_all = _L2_conv_setup()
    _L2_conv_in = {k: v for k, v in _L2_conv_all.items() if k in ('offset', )}
    del _L2_conv_all

    def _L3_conv_setup():
        import jax, jax.numpy as jnp
        import numpy as np
        DIM = 384
        QK_DIM = max(16, DIM // 2)
        SE_DIM = DIM // 4
        BN_EPS = 1e-05
        key = jax.random.key(seed)
        ks = jax.random.split(key, 12)
        B, C, H, W = (8, DIM, 48, 48)
        s = lambda fan_in: (2.0 / fan_in) ** 0.5
        return {'x': jax.random.normal(ks[0], (B, C, H, W), jnp.float32), 'wq': jax.random.normal(ks[1], (QK_DIM, C), jnp.float32) * s(C), 'bq': jnp.zeros((QK_DIM,), jnp.float32), 'wk': jax.random.normal(ks[2], (QK_DIM, C), jnp.float32) * s(C), 'bk': jnp.zeros((QK_DIM,), jnp.float32), 'wv': jax.random.normal(ks[3], (C, C), jnp.float32) * s(C), 'bv': jnp.zeros((C,), jnp.float32), 'w_proj': jax.random.normal(ks[4], (C, C), jnp.float32) * s(C), 'b_proj': jnp.zeros((C,), jnp.float32), 'bn_gamma': jnp.ones((C,), jnp.float32), 'bn_beta': jnp.zeros((C,), jnp.float32), 'bn_mean': jnp.zeros((C,), jnp.float32), 'bn_var': jnp.ones((C,), jnp.float32), 'w_se1': jax.random.normal(ks[5], (SE_DIM, C), jnp.float32) * s(C), 'b_se1': jnp.zeros((SE_DIM,), jnp.float32), 'w_se2': jax.random.normal(ks[6], (C, SE_DIM), jnp.float32) * s(SE_DIM), 'b_se2': jnp.zeros((C,), jnp.float32)}
    _L3_conv_all = _L3_conv_setup()
    _L3_conv_in = {k: v for k, v in _L3_conv_all.items() if k in ('wq', 'bq', 'wk', 'bk', 'wv', 'bv', 'w_proj', 'b_proj', 'bn_gamma', 'bn_beta', 'bn_mean', 'bn_var', 'w_se1', 'b_se1', 'w_se2', 'b_se2', )}
    del _L3_conv_all

    return {
        "x": x,
        "L0_conv_qkvo_w": _L0_conv_in["qkvo_w"],
        "L0_conv_qkvo_b": _L0_conv_in["qkvo_b"],
        "L0_conv_lepe_w": _L0_conv_in["lepe_w"],
        "L0_conv_lepe_b": _L0_conv_in["lepe_b"],
        "L0_conv_proj_w": _L0_conv_in["proj_w"],
        "L0_conv_proj_b": _L0_conv_in["proj_b"],
        "L1_conv_x_proj_weight": _L1_conv_in["x_proj_weight"],
        "L1_conv_dt_projs_weight": _L1_conv_in["dt_projs_weight"],
        "L1_conv_dt_projs_bias": _L1_conv_in["dt_projs_bias"],
        "L1_conv_A_logs": _L1_conv_in["A_logs"],
        "L1_conv_Ds": _L1_conv_in["Ds"],
        "L1_conv_ln_weight": _L1_conv_in["ln_weight"],
        "L1_conv_ln_bias": _L1_conv_in["ln_bias"],
        "L2_conv_offset": _L2_conv_in["offset"],
        "L3_conv_wq": _L3_conv_in["wq"],
        "L3_conv_bq": _L3_conv_in["bq"],
        "L3_conv_wk": _L3_conv_in["wk"],
        "L3_conv_bk": _L3_conv_in["bk"],
        "L3_conv_wv": _L3_conv_in["wv"],
        "L3_conv_bv": _L3_conv_in["bv"],
        "L3_conv_w_proj": _L3_conv_in["w_proj"],
        "L3_conv_b_proj": _L3_conv_in["b_proj"],
        "L3_conv_bn_gamma": _L3_conv_in["bn_gamma"],
        "L3_conv_bn_beta": _L3_conv_in["bn_beta"],
        "L3_conv_bn_mean": _L3_conv_in["bn_mean"],
        "L3_conv_bn_var": _L3_conv_in["bn_var"],
        "L3_conv_w_se1": _L3_conv_in["w_se1"],
        "L3_conv_b_se1": _L3_conv_in["b_se1"],
        "L3_conv_w_se2": _L3_conv_in["w_se2"],
        "L3_conv_b_se2": _L3_conv_in["b_se2"],
    }

def reference(x, L0_conv_qkvo_w, L0_conv_qkvo_b, L0_conv_lepe_w, L0_conv_lepe_b, L0_conv_proj_w, L0_conv_proj_b, L1_conv_x_proj_weight, L1_conv_dt_projs_weight, L1_conv_dt_projs_bias, L1_conv_A_logs, L1_conv_Ds, L1_conv_ln_weight, L1_conv_ln_bias, L2_conv_offset, L3_conv_wq, L3_conv_bq, L3_conv_wk, L3_conv_bk, L3_conv_wv, L3_conv_bv, L3_conv_w_proj, L3_conv_b_proj, L3_conv_bn_gamma, L3_conv_bn_beta, L3_conv_bn_mean, L3_conv_bn_var, L3_conv_w_se1, L3_conv_b_se1, L3_conv_w_se2, L3_conv_b_se2):
    import jax
    import jax.numpy as jnp
    def _L0_conv_ref(x, qkvo_w, qkvo_b, lepe_w, lepe_b, proj_w, proj_b):
        import jax, jax.numpy as jnp
        import numpy as np
        from jax import lax
        DIM = 384
        NUM_HEADS = 12
        HEAD_DIM = DIM // NUM_HEADS
        SCALE = HEAD_DIM ** (-0.5)
        B, C, H, W = x.shape
        n, d = (NUM_HEADS, HEAD_DIM)
        HW = H * W
        qkvo = jnp.einsum('oc,bchw->bohw', qkvo_w[:, :, 0, 0], x) + qkvo_b[:, None, None]
        qkv = qkvo[:, :3 * C]
        o = qkvo[:, 3 * C:]
        v_ch = qkv[:, 2 * C:]
        lepe = lax.conv_general_dilated(v_ch, lepe_w, window_strides=(1, 1), padding='SAME', feature_group_count=C, dimension_numbers=('NCHW', 'OIHW', 'NCHW')) + lepe_b[:, None, None]
        q, k, v = jnp.transpose(qkv.reshape(B, 3, n, d, HW), (1, 0, 2, 4, 3))
        attn = jax.nn.softmax(SCALE * jnp.einsum('bnqd,bnkd->bnqk', q, k), axis=-1)
        res = jnp.einsum('bnqk,bnkd->bnqd', attn, v)
        res = jnp.transpose(res, (0, 1, 3, 2)).reshape(B, C, H, W)
        res = res + lepe
        out = jnp.einsum('oc,bchw->bohw', proj_w[:, :, 0, 0], res * o) + proj_b[:, None, None]
        return out

    def _L1_conv_ref(x, x_proj_weight, dt_projs_weight, dt_projs_bias, A_logs, Ds, ln_weight, ln_bias):
        import jax, jax.numpy as jnp
        import numpy as np
        D_MODEL = 192
        D_STATE = 16
        SSM_RATIO = 2.0
        D_INNER = int(SSM_RATIO * D_MODEL)
        DT_RANK = int(np.ceil(D_MODEL / 16))
        K_GROUP = 4
        BATCH, HH, WW = (4, 32, 32)
        DT_MIN, DT_MAX = (0.001, 0.1)
        LN_EPS = 1e-05

        def _cross_scan(x):
            B, D, H, W = x.shape
            x0 = x.reshape(B, D, H * W)
            x1 = jnp.transpose(x, (0, 1, 3, 2)).reshape(B, D, H * W)
            return jnp.stack([x0, x1, x0[..., ::-1], x1[..., ::-1]], axis=1)

        def _cross_merge(ys, H, W):
            B, K, D, L = ys.shape
            y0 = ys[:, 0]
            y2 = ys[:, 2][..., ::-1]
            yt = ys[:, 1] + ys[:, 3][..., ::-1]
            yt = jnp.transpose(yt.reshape(B, D, W, H), (0, 1, 3, 2)).reshape(B, D, L)
            return y0 + y2 + yt

        def _selective_scan(u, dt, A, Bs, Cs):
            dt_l = jnp.moveaxis(dt, -1, 0)
            u_l = jnp.moveaxis(u, -1, 0)
            B_l = jnp.moveaxis(Bs, -1, 0)
            C_l = jnpp_move = jnp.moveaxis(Cs, -1, 0)

            def step(h, inp):
                dtt, ut, bt, ct = inp
                dA = jnp.exp(dtt[..., None] * A)
                h = h * dA + (dtt * ut)[..., None] * bt[:, :, None, :]
                y = jnp.einsum('bkdn,bkn->bkd', h, ct)
                return (h, y)
            h0 = jnp.zeros(u.shape[:3] + (A.shape[-1],), dtype=u.dtype)
            _, ys = jax.lax.scan(step, h0, (dt_l, u_l, B_l, C_l))
            return jnp.moveaxis(ys, 0, -1)
        B, D, H, W = x.shape
        K = x_proj_weight.shape[0]
        N = D_STATE
        R = dt_projs_weight.shape[-1]
        L = H * W
        xs = _cross_scan(x)
        x_dbl = jnp.einsum('bkdl,kcd->bkcl', xs, x_proj_weight)
        dts, Bs, Cs = (x_dbl[:, :, :R], x_dbl[:, :, R:R + N], x_dbl[:, :, R + N:])
        dts = jnp.einsum('bkrl,kdr->bkdl', dts, dt_projs_weight)
        A = -jnp.exp(A_logs.astype(jnp.float32)).reshape(K, D, N)
        dt = jax.nn.softplus(dts.astype(jnp.float32) + dt_projs_bias.astype(jnp.float32)[None, :, :, None])
        u = xs.astype(jnp.float32)
        Bs = Bs.astype(jnp.float32)
        Cs = Cs.astype(jnp.float32)
        ys = _selective_scan(u, dt, A, Bs, Cs)
        ys = ys + Ds.astype(jnp.float32).reshape(K, D)[None, :, :, None] * u
        y = _cross_merge(ys, H, W).reshape(B, D, H, W)
        yc = jnp.transpose(y, (0, 2, 3, 1))
        mu = jnp.mean(yc, axis=-1, keepdims=True)
        var = jnp.mean((yc - mu) ** 2, axis=-1, keepdims=True)
        yc = (yc - mu) * jax.lax.rsqrt(var + LN_EPS) * ln_weight + ln_bias
        y = jnp.transpose(yc, (0, 3, 1, 2)).astype(x.dtype)
        return jax.nn.gelu(y, approximate=False)

    def _L2_conv_ref(x, offset):
        import jax, jax.numpy as jnp
        from jax import lax
        import numpy as np
        H, W = (64, 64)
        K = 5
        SIGMA = 0.5
        CHAN_PER_POS = 8
        INIT_STRIDE = 16
        BATCH = 32

        def _num_offsets(h, w, s):
            ny = (h - s) // s * 2 + 1
            nx = (w - s) // s * 2 + 1
            return (ny, nx, ny * nx - 1)

        def _displace(x, off_int):
            _, _, _, h, w = x.shape

            def shift_one(xp, dxy):
                dx, dy = (dxy[0], dxy[1])
                ys = jnp.arange(h) - dy
                xs = jnp.arange(w) - dx
                ym = (ys >= 0) & (ys < h)
                xm = (xs >= 0) & (xs < w)
                ysc = jnp.clip(ys, 0, h - 1)
                xsc = jnp.clip(xs, 0, w - 1)
                out = xp[:, :, ysc][:, :, :, xsc]
                return out * (ym[:, None] & xm[None, :]).astype(xp.dtype)
            return jax.vmap(shift_one, in_axes=(1, 0), out_axes=1)(x, off_int)
        B, C, h, w = x.shape
        P = offset.shape[0]
        cpp = C // P
        off_round = jnp.round(offset)
        off_int = off_round.astype(jnp.int32)
        disp = _displace(x.reshape(B, P, cpp, h, w), off_int).reshape(B, C, h, w)
        sub = offset - lax.stop_gradient(off_round)
        c = K // 2
        jj, ii = jnp.meshgrid(jnp.arange(K, dtype=jnp.float32) - c, jnp.arange(K, dtype=jnp.float32) - c, indexing='xy')
        field = jnp.stack([jj, ii], axis=-1)
        d = field[None] + sub[:, None, None, :]
        kernel = jnp.exp(-jnp.sum(d * d, axis=-1) / (2.0 * SIGMA ** 2))
        kernel = kernel / jnp.sum(kernel, axis=(1, 2), keepdims=True)
        kw = jnp.repeat(kernel, cpp, axis=0)[:, None]
        out = lax.conv_general_dilated(disp, kw, window_strides=(1, 1), padding=[(c, c), (c, c)], feature_group_count=C, dimension_numbers=('NCHW', 'OIHW', 'NCHW'))
        return out

    def _L3_conv_ref(x, wq, bq, wk, bk, wv, bv, w_proj, b_proj, bn_gamma, bn_beta, bn_mean, bn_var, w_se1, b_se1, w_se2, b_se2):
        import jax, jax.numpy as jnp
        import numpy as np
        DIM = 384
        QK_DIM = max(16, DIM // 2)
        SE_DIM = DIM // 4
        BN_EPS = 1e-05
        B, C, H, W = x.shape
        N = H * W
        scale = QK_DIM ** (-0.5)
        scale = 32.0 ** (-0.5)
        xf = x.reshape(B, C, N)
        q = jnp.einsum('oc,bcn->bno', wq, xf) + bq
        k = jnp.einsum('oc,bcn->bon', wk, xf) + bk[:, None]
        v = jnp.einsum('oc,bcn->bon', wv, xf) + bv[:, None]
        attn = jnp.einsum('bnd,bdm->bnm', q, k) * scale
        attn = jax.nn.softmax(attn, axis=-1)
        y = jnp.einsum('bcn,bmn->bcm', v, attn).reshape(B, C, H, W)
        pooled = jnp.mean(y, axis=(2, 3))
        h = jax.nn.relu(pooled @ w_se1.T + b_se1)
        gate = jax.nn.sigmoid(h @ w_se2.T + b_se2)
        y = y * gate[:, :, None, None]
        y = jnp.einsum('oc,bchw->bohw', w_proj, y) + b_proj[None, :, None, None]
        inv = bn_gamma / jnp.sqrt(bn_var + BN_EPS)
        out = (y - bn_mean[None, :, None, None]) * inv[None, :, None, None] + bn_beta[None, :, None, None]
        return out

    def _gn(v, G=32, eps=1e-5):
        B_, C_, H_, W_ = v.shape
        g = v.reshape(B_, G, C_ // G, H_, W_)
        m = jnp.mean(g, axis=(2, 3, 4), keepdims=True)
        s = jnp.var(g, axis=(2, 3, 4), keepdims=True)
        return ((g - m) / jnp.sqrt(s + eps)).reshape(v.shape)

    def _ln_c(v, eps=1e-6):
        m = jnp.mean(v, axis=1, keepdims=True)
        s = jnp.var(v, axis=1, keepdims=True)
        return (v - m) / jnp.sqrt(s + eps)

    def _ln_t(v, eps=1e-5):
        m = jnp.mean(v, axis=-1, keepdims=True)
        s = jnp.var(v, axis=-1, keepdims=True)
        return (v - m) / jnp.sqrt(s + eps)

    def _to_tokens(v):
        B_, C_, H_, W_ = v.shape
        return v.reshape(B_, C_, H_ * W_).transpose(0, 2, 1)
    def _from_tokens(t, like):
        B_, C_, H_, W_ = like.shape
        return t.transpose(0, 2, 1).reshape(B_, C_, H_, W_)

    x = x + _L0_conv_ref(_gn(x), L0_conv_qkvo_w, L0_conv_qkvo_b, L0_conv_lepe_w, L0_conv_lepe_b, L0_conv_proj_w, L0_conv_proj_b)
    x = x + _L1_conv_ref(_gn(x), L1_conv_x_proj_weight, L1_conv_dt_projs_weight, L1_conv_dt_projs_bias, L1_conv_A_logs, L1_conv_Ds, L1_conv_ln_weight, L1_conv_ln_bias)
    x = x + _L2_conv_ref(_gn(x), L2_conv_offset)
    x = x + _L3_conv_ref(_gn(x), L3_conv_wq, L3_conv_bq, L3_conv_wk, L3_conv_bk, L3_conv_wv, L3_conv_bv, L3_conv_w_proj, L3_conv_b_proj, L3_conv_bn_gamma, L3_conv_bn_beta, L3_conv_bn_mean, L3_conv_bn_var, L3_conv_w_se1, L3_conv_b_se1, L3_conv_w_se2, L3_conv_b_se2)
    return x


_drawn_inputs = setup_inputs


def setup_inputs(seed=0):
    import zlib

    import numpy as np

    out = dict(_drawn_inputs(seed))
    spreads = {'L1_conv_Ds': (1.0, 0.6),
     'L1_conv_ln_weight': (1.0, 0.2),
     'L1_conv_ln_bias': (0.0, 0.579),
     'L3_conv_bq': (0.0, 0.341),
     'L3_conv_bk': (0.0, 2.0),
     'L3_conv_bv': (0.0, 0.456),
     'L3_conv_b_proj': (0.0, 0.412),
     'L3_conv_bn_gamma': (1.0, 0.577),
     'L3_conv_bn_beta': (0.0, 0.427),
     'L3_conv_bn_mean': (0.0, 0.424),
     'L3_conv_bn_var': (1.0, 0.6),
     'L3_conv_b_se1': (0.0, 1.32),
     'L3_conv_b_se2': (0.0, 1.278)}
    factors = {'L0_conv_qkvo_w': 4.695,
     'L0_conv_qkvo_b': 8.0,
     'L0_conv_lepe_w': 5.998,
     'L0_conv_lepe_b': 8.0,
     'L0_conv_proj_w': 4.716,
     'L0_conv_proj_b': 8.0,
     'L1_conv_A_logs': 4.761,
     'L3_conv_w_se1': 4.551}
    for name, (base, spread) in spreads.items():
        noise = np.random.default_rng([zlib.crc32(name.encode()), seed]).standard_normal(out[name].shape)
        drawn = base * np.exp(spread * noise) if base else spread * noise
        out[name] = jnp.asarray(drawn.astype(out[name].dtype))
    for name, factor in factors.items():
        out[name] = (out[name] * factor).astype(out[name].dtype)
    return out
```

```python
import numpy as np
import concourse.bass as bass
from concourse import mybir
from contextlib import ExitStack

F32 = mybir.dt.float32
ACT = mybir.ActivationFunctionType
ALU = mybir.AluOpType
AX = mybir.AxisListType

B, C, HH, WW = 8, 384, 32, 32
L = HH * WW
P = 128
NC = C // P
LB = L // P
HALF = 512
HEADS, HD = 12, 32
SC0 = HD ** -0.5
STEPS0 = HEADS * LB
K, R, N = 4, 12, 16
XR = R + 2 * N
GN_ = 4
STEPS1 = K * NC * N
POS, CPP = 48, 8
PG = POS // 4
QK3 = 192
QC3 = QK3 // 2
SE = C // 4
SC3 = 32.0 ** -0.5
GROUPS = 32
EPS = 1e-5

VEC = {n: i for i, n in enumerate(
    ["bq", "bk", "bv", "bo", "lepe_b", "proj_b", "D0", "D1", "D2", "D3", "ln_w", "ln_b",
     "dtb0", "dtb1", "dtb2", "dtb3", "bv3", "bproj3", "gamma", "beta", "mean", "var", "bse2"])}
NV = len(VEC)


DIRS = [(1, 0), (1, 1), (0, 0), (0, 1)]


class Signal:

    def __init__(self, handle, per):
        self.h, self.per = handle, per

    def at(self, img, n):
        return img * self.per + (n + 1)


def build(nc, t):
    ctx = ExitStack()
    with ctx:
        def sb(name, cols, parts=P):
            return ctx.enter_context(nc.sbuf_tensor(name, [parts, cols], F32))

        signals = []

        def sem(name, per):
            s = Signal(ctx.enter_context(nc.semaphore(name)), per)
            if per:
                signals.append(s)
            return s

        ident = sb("ident", P)
        group_avg = sb("group_avg", NC * NC * P)
        vecs = sb("vecs", NV * NC)
        vec96 = sb("vec96", 5)
        lepe_w = sb("lepe_w", NC * 25)
        negA = sb("negA", K * NC * N)
        w_xproj = sb("w_xproj", NC * K * XR)
        w_dt = sb("w_dt", K * C)
        w_proj0 = sb("w_proj0", NC * C)
        shift_y = sb("shift_y", PG * P)
        derived = sb("derived", 32)
        half_neg = sb("half_neg", 8)
        gn_t = sb("gn_t", 64)
        ln_t = sb("ln_t", 64)
        se_t = sb("se_t", 64)
        stats = sb("stats", 48)
        ws = sb("ws", 6144)
        vpad = sb("vpad", 36 * 36)
        X = sb("X", NC * L)
        R_ = sb("R", 35 * 1024)
        ps = ctx.enter_context(nc.psum_tensor("ps", [P, 8, HALF], F32))

        ga = group_avg[:, :].rearrange("p (a b m) -> p a b m", a=NC, b=NC)
        X3 = X[:, :].rearrange("p (c l) -> p c l", c=NC)

        def reg(at, words):
            return R_[:, at:at + words]

        def vec(name, c):
            i = VEC[name] * NC + c
            return vecs[:, i:i + 1]

        def banks(b):
            return ps[:, b:b + 2, :].rearrange("p b n -> p (b n)")

        K1 = 1024
        xn0 = reg(0, 3 * K1).rearrange("p (c l) -> p c l", c=NC)
        vT = reg(3 * K1, 3 * K1).rearrange("p (b c) -> p b c", b=LB)
        stage = [reg((6 + i) * K1, K1) for i in range(2)]
        qh = [reg((8 + i) * K1, K1) for i in range(2)]
        kh = [reg((10 + i) * K1, K1) for i in range(2)]
        probs = [reg((12 + i) * K1, K1) for i in range(2)]
        probsT = [reg((14 + i) * K1, K1).rearrange("p (b q) -> p b q", b=LB) for i in range(2)]
        heads = reg(16 * K1, 3 * K1).rearrange("p (b c) -> p b c", b=LB)
        lep = reg(19 * K1, K1)
        gate0 = reg(20 * K1, K1)
        res = reg(21 * K1, 3 * K1).rearrange("p (c l) -> p c l", c=NC)
        small0 = reg(24 * K1, 64)
        negmax, rowsum, rowinv = small0[:, 0:8], small0[:, 8:16], small0[:, 16:24]
        w0 = ws[:, 0:NC * 4 * C].rearrange("p (c o) -> p c o", c=NC)
        U = reg(0, 3 * K1).rearrange("p (c l) -> p c l", c=NC)
        ysum = reg(3 * K1, 3 * K1).rearrange("p (b c) -> p b c", b=LB)
        dt = reg(6 * K1, 3 * K1).rearrange("p (c l) -> p c l", c=NC)
        dtu = reg(9 * K1, 3 * K1).rearrange("p (c l) -> p c l", c=NC)
        bc = reg(12 * K1, 16 * K1).rearrange("p (g t n l) -> p g t n l", g=2, t=2, n=GN_)
        decay = [reg((28 + i) * K1, K1) for i in range(2)]
        state = [reg((30 + i) * K1, K1) for i in range(4)]
        soft = [state[i] for i in range(2)]
        xdbl = reg(34 * K1, K1)
        gel = [decay[i] for i in range(2)]
        xn2 = reg(0, 3 * K1).rearrange("p (c l) -> p c l", c=NC)
        rows2 = reg(3 * K1, 3 * K1).rearrange("p (j s) -> p j s", s=32)
        mid2 = reg(6 * K1, 3 * K1).rearrange("p (g m) -> p g m", m=P)
        out2 = reg(9 * K1, 3 * K1).rearrange("p (j s) -> p j s", s=32)
        blur = reg(12 * K1, 3 * K1).rearrange("p (c l) -> p c l", c=NC)
        shift_x = ws[:, 0:POS * P].rearrange("p (q m) -> p q m", q=POS)
        xn3 = reg(0, 3 * K1).rearrange("p (c l) -> p c l", c=NC)
        q3 = reg(3 * K1, 2 * K1).rearrange("p (c l) -> p c l", c=2)
        k3 = reg(5 * K1, 2 * K1).rearrange("p (c l) -> p c l", c=2)
        vT3 = reg(7 * K1, 3 * K1).rearrange("p (b c) -> p b c", b=LB)
        prob3 = [reg((10 + i) * K1, K1) for i in range(2)]
        prT3 = [reg((12 + 4 * i) * K1, 4 * K1).rearrange("p (b q) -> p b q", b=LB) for i in range(2)]
        y3 = reg(20 * K1, 3 * K1).rearrange("p (c l) -> p c l", c=NC)
        wg3 = reg(23 * K1, NC * C).rearrange("p (c o) -> p c o", c=NC)
        o3 = 0
        wq3 = ws[:, 0:NC * QK3].rearrange("p (c o) -> p c o", c=NC)
        wk3 = ws[:, 576:576 + NC * QK3].rearrange("p (c o) -> p c o", c=NC)
        wv3 = ws[:, 1152:1152 + NC * C].rearrange("p (c o) -> p c o", c=NC)
        wp3 = ws[:, 2304:2304 + NC * C].rearrange("p (c o) -> p c o", c=NC)
        wse1 = ws[:, 3456:3456 + NC * SE].rearrange("p (c o) -> p c o", c=NC)
        wse2 = ws[0:SE, 3744:3744 + C]
        qb = derived[:, 0:3]
        dsum = derived[:, 3:6]
        inv3 = derived[:, 6:9]
        cst3 = derived[:, 9:12]
        qb3 = derived[:, 12:14]
        tmp_d = derived[:, 14:20]

        c_in = sem("consts_loaded", 0)
        pre_v = sem("pre_vector", 0)
        pre_a = sem("pre_scalar", 0)
        pre_g = sem("pre_gpsimd", 0)
        pre_st = sem("shift_x_stored", 0)
        x_in = sem("x_loaded", 16)
        w_in = sem("weights_loaded", 16 * 8)
        gn_stat = sem("gn_stats", 4)
        gn_mean = sem("gn_group_mean", 4)
        gn_dev = sem("gn_deviation", 4)
        gn_var = sem("gn_group_var", 4)
        gn_eps = sem("gn_var_eps", 4)
        gn_rstd = sem("gn_rstd", 4)
        gn_out = sem("gn_normalized", 4)
        qk_ps = sem("qk_projected", 6)
        qk_sb = sem("qk_evacuated", 6)
        qk_st = [sem(f"qk_stored{i}", 48) for i in range(2)]
        vt_ps = sem("vT_projected", LB)
        vt_sb = sem("vT_evacuated", LB)
        hd_in = [sem(f"head_loaded{i}", 32 * HEADS // 2) for i in range(2)]
        s_ps = sem("scores_ready", STEPS0)
        s_max = sem("rowmax_ready", STEPS0)
        s_exp = sem("probs_ready", STEPS0)
        t_ps = sem("probsT_in_psum", STEPS0)
        t_sb = sem("probsT_ready", STEPS0)
        pv_ps = sem("head_out_in_psum", STEPS0)
        o_sb = sem("head_out_ready", STEPS0)
        vo_ps = sem("v_and_gate_projected", 2 * NC)
        vo_sb = sem("v_and_gate_evacuated", 2 * NC)
        hT_ps = sem("heads_transposed", NC)
        r_sb = sem("gated_result_ready", NC)
        p0_ps = sem("proj0_in_psum", NC)
        x1 = sem("x1_ready", NC)
        xd_ps = sem("xproj_in_psum", K)
        xd_sb = sem("xproj_evacuated", K)
        bc_st = sem("bc_rows_stored", 16 * K)
        bc_ld = [sem(f"bc_rows_loaded{i}", 16 * 4 * K) for i in range(2)]
        dt_ps = sem("dt_in_psum", K * NC)
        dt_rel = sem("dt_relu_ready", K * NC)
        dt_abs = sem("dt_abs_read", K * NC)
        dt_ln = sem("dt_log_ready", K * NC)
        dt_sb = sem("dt_ready", K * NC)
        mg_ps = sem("column_sum_turned_back", NC)
        mg_sb = sem("column_sum_reordered", NC)
        mg_tp = sem("column_sum_turned", NC)
        mg_y = sem("column_sum_in_ysum", NC)
        a_sb = sem("decay_ready", STEPS1)
        b_sb = sem("drive_ready", STEPS1)
        h_sb = sem("state_ready", STEPS1)
        hc_sb = sem("state_times_c_ready", STEPS1)
        y_ps = sem("y_transposed", STEPS1)
        y_sb = sem("y_added", STEPS1 // GN_)
        ln_st = sem("ln_stats", 1)
        ln_r = sem("ln_rstd", 1)
        ln_o = sem("ln_normalized", 1)
        lt_ps = sem("ln_transposed", NC)
        g_sb = sem("gelu_ready", NC)
        x2 = sem("x2_ready", NC)
        s2_st = sem("xn2_stored", 16)
        s2_ld = sem("rows2_loaded", 64)
        m2_ps = sem("rows_shifted", 6)
        m2_sb = sem("rows_shifted_evacuated", 6)
        o2_ps = sem("cols_shifted", 6)
        o2_sb = sem("cols_shifted_evacuated", 6)
        o2_st = sem("blur_stored", 64)
        b2_ld = sem("blur_loaded", 16)
        x3 = sem("x3_ready", 1)
        p3_ps = sem("qk3_in_psum", 4)
        p3_sb = sem("qk3_evacuated", 4)
        v3_ps = sem("vT3_in_psum", LB)
        v3_sb = sem("vT3_evacuated", LB)
        s3_ps = sem("scores3_ready", LB)
        s3_mx = sem("rowmax3_ready", LB)
        s3_ex = sem("probs3_ready", LB)
        s3_nm = sem("probs3_normalized", LB)
        s3_tp = sem("probs3T_in_psum", LB)
        s3_ts = sem("probs3T_ready", LB)
        y3_ps = sem("y3_in_psum", 2 * NC)
        y3_sb = sem("y3_evacuated", 2 * NC)
        se_pool = sem("pooled_ready", 1)
        se_h = sem("se_hidden_in_psum", 1)
        se_hr = sem("se_hidden_ready", 1)
        se_z = sem("se_logits_in_psum", 1)
        se_zb = sem("se_logits_ready", 1)
        se_e = sem("se_exp_ready", 1)
        se_w = sem("gated_weights_ready", 1)
        f_ps = sem("proj3_in_psum", NC)
        f_sb = sem("out_ready", NC)
        out_st = sem("out_stored", 16)

        qk_d = t["qk_scratch"]
        bc_d = t["bc_scratch"]
        sx_d = t["shift_scratch"]
        s2_d = t["rows_scratch"]
        o2_d = t["blur_scratch"]

        block = ctx.enter_context(nc.Block())
        def img3(a, img):
            return a[img].rearrange("(c p) l -> p c l", p=P)

        def transposed(ap):
            return ap.rearrange("p (h w) -> p w h", w=WW)

        @block.sync
        def _(sp):
            for s in signals:
                sp.sem_inc(s.h, 1)
            for name, dst in [("ident", ident[:, :]), ("group_avg", group_avg[:, :]), ("vecs", vecs[:, :]),
                              ("vec96", vec96[0:QC3, :]), ("lepe_w", lepe_w[:, :]), ("A_logs", negA[:, :]),
                              ("w_xproj", w_xproj[:, :]), ("w_dt", w_dt[32:32 + R, :]),
                              ("w_proj0", w_proj0[:, :]),
                              ("row_index", R_[:, 0:1]), ("col_row", R_[:, 32:64])]:
                sp.dma_start(dst, t[name]).then_inc(c_in.h, 16)
            with nc.allow_non_contiguous_dma(reason="48 offsets, once"):
                for q in range(4):
                    src = t["offset"][q * PG:(q + 1) * PG, :].rearrange("g d -> (g d)")
                    sp.dma_start(R_[32 * q:32 * q + 32, 64:64 + 2 * PG],
                                 src[None, :].to_broadcast([32, 2 * PG])).then_inc(c_in.h, 16)
                src = t["offset"].rearrange("g d -> (g d)")
                sp.dma_start(R_[:, 96:96 + 2 * POS], src[None, :].to_broadcast([P, 2 * POS])).then_inc(c_in.h, 16)
            sp.wait_ge(pre_v.h, 2)
            sp.dma_start(sx_d, ws[:, 0:POS * P]).then_inc(pre_st.h, 16)
            sp.wait_ge(pre_st.h, 16)

            with sp.Fori(0, B) as img:
                sp.wait_ge(out_st.h, out_st.at(img, 0))
                sp.dma_start(X3, img3(t["x"], img)).then_inc(x_in.h, 16)
                sp.wait_ge(f_ps.h, f_ps.at(img, 0))
                sp.dma_start(w0, t["w_qkvo"]).then_inc(w_in.h, 16)
                for i in range(6):
                    sp.wait_ge(qk_sb.h, qk_sb.at(img, i + 1))
                    sp.dma_start(qk_d[i], stage[i % 2]).then_inc(qk_st[i % 2].h, 16)
                sp.wait_ge(qk_st[0].h, qk_st[0].at(img, 48))
                sp.wait_ge(qk_st[1].h, qk_st[1].at(img, 48))
                qrows = qk_d.rearrange("a p l -> (a p) l")

                def load_head(row, j):
                    sp.dma_start(qh[j][0:HD, :], qrows[bass.ds(row, HD), :]).then_inc(hd_in[j].h, 16)
                    sp.dma_start(kh[j][0:HD, :], qrows[bass.ds(row + C, HD), :]).then_inc(hd_in[j].h, 16)

                load_head(0, 0)
                load_head(HD, 1)
                with sp.Fori(0, HEADS // 2 - 1) as pair:
                    for j in range(2):
                        sp.wait_ge(s_ps.h, s_ps.at(img, pair * 16 + 8 * (j + 1)))
                        load_head(pair * 64 + 64 + 32 * j, j)
                for k in range(K):
                    sp.wait_ge(xd_sb.h, xd_sb.at(img, k + 1))
                    sp.dma_start(bc_d[k], xdbl[0:2 * N, :]).then_inc(bc_st.h, 16)
                    sp.wait_ge(bc_st.h, bc_st.at(img, 16 * (k + 1)))
                    for a in range(N // GN_):
                        if a >= 2:
                            sp.wait_ge(hc_sb.h, hc_sb.at(img, 48 * k + 12 * (a - 1)))
                        for j in range(2):
                            rows = bc_d[k, 16 * j + GN_ * a:16 * j + GN_ * (a + 1), :].rearrange("n l -> (n l)")
                            sp.dma_start(bc[:, a % 2, j, :, :].rearrange("p n l -> p (n l)"),
                                         rows[None, :].to_broadcast([P, GN_ * L])).then_inc(bc_ld[a % 2].h, 16)
                sp.wait_ge(vo_ps.h, vo_ps.at(img, 2 * NC))
                sp.dma_start(ws[:, 0:POS * P], sx_d).then_inc(w_in.h, 16)
                sp.wait_ge(gn_out.h, gn_out.at(img, 3))
                sp.dma_start(s2_d.rearrange("(c p) l -> p c l", p=P), xn2).then_inc(s2_st.h, 16)
                sp.wait_ge(s2_st.h, s2_st.at(img, 16))
                quads = s2_d.rearrange("(q j) (y x) -> q y j x", q=4, x=WW)
                for q in range(4):
                    sp.dma_start(rows2[32 * q:32 * q + 32, :, :], quads[q]).then_inc(s2_ld.h, 16)
                sp.wait_ge(o2_sb.h, o2_sb.at(img, 6))
                quads = o2_d.rearrange("(q j) (y x) -> q y j x", q=4, x=WW)
                for q in range(4):
                    sp.dma_start(quads[q], out2[32 * q:32 * q + 32, :, :]).then_inc(o2_st.h, 16)
                sp.wait_ge(o2_ps.h, o2_ps.at(img, 6))
                for name, dst in [("wq3", wq3), ("wk3", wk3), ("wv3", wv3), ("wp3", wp3), ("wse1", wse1), ("wse2", wse2)]:
                    sp.dma_start(dst, t[name]).then_inc(w_in.h, 16)
                sp.wait_ge(o2_st.h, o2_st.at(img, 64))
                sp.dma_start(blur, o2_d.rearrange("(c p) l -> p c l", p=P)).then_inc(b2_ld.h, 16)
                sp.wait_ge(f_sb.h, f_sb.at(img, NC))
                sp.dma_start(img3(t["out"], img), X3).then_inc(out_st.h, 16)
            sp.wait_ge(out_st.h, out_st.at(B - 1, 16))

        @block.tensor
        def _(pe):
            def group_norm(img, g):
                for src, sig_in, sig_out, col in ((gn_t[:, 0:3], gn_stat, gn_mean, 0), (gn_t[:, 16:19], gn_dev, gn_var, 8)):
                    pe.wait_ge(sig_in.h, sig_in.at(img, g + 1))
                    for m in range(NC):
                        near = [a for a in range(NC) if abs(a - m) < 2]
                        for a in near:
                            mm = pe.matmul(ps[:, 7, col + m:col + m + 1], ga[:, a, m, :], src[:, a:a + 1],
                                           start=a == near[0], stop=a == near[-1])
                    mm.then_inc(sig_out.h, 1)

            def project(dst, lhs, rhs, parts=P):
                for hf in range(2):
                    for c in range(NC):
                        mm = pe.matmul(dst[0:parts, hf * HALF:(hf + 1) * HALF], lhs[:, c], rhs(c, hf),
                                       start=c == 0, stop=c == NC - 1)
                return mm

            def rows_of(x):
                return lambda c, hf: x[:, c, hf * HALF:(hf + 1) * HALF]

            with pe.Fori(0, B) as img:
                pe.wait_ge(c_in.h, 16 * 16)
                group_norm(img, 0)
                pe.wait_ge(gn_out.h, gn_out.at(img, 1))
                pe.wait_ge(w_in.h, w_in.at(img, 16))
                for i in range(6):
                    if i >= 2:
                        pe.wait_ge(qk_sb.h, qk_sb.at(img, i - 1))
                    project(banks(2 * (i % 2)), w0[:, :, i * P:(i + 1) * P], rows_of(xn0)).then_inc(qk_ps.h, 1)
                for b in range(LB):
                    if b >= 2:
                        pe.wait_ge(vt_sb.h, vt_sb.at(img, b - 1))
                    for c in range(NC):
                        mm = pe.matmul(ps[:, 4 + b % 2, 0:C], xn0[:, c, b * P:(b + 1) * P], w0[:, c, 2 * C:3 * C],
                                       start=c == 0, stop=c == NC - 1)
                    mm.then_inc(vt_ps.h, 1)
                with pe.Fori(0, HEADS // 2) as pair:
                    base = pair * 16

                    def scores(u):
                        j, qc = u // LB, u % LB
                        if u == 0:
                            pe.wait_ge(qk_sb.h, qk_sb.at(img, 6))
                            pe.wait_ge(vt_sb.h, vt_sb.at(img, LB))
                        if qc == 0:
                            pe.wait_ge(hd_in[j].h, hd_in[j].at(img, pair * 32 + 32))
                        if u >= 2:
                            pe.wait_ge(s_exp.h, s_exp.at(img, base + (u - 1)))
                        for hf in range(2):
                            mm = pe.matmul(ps[:, 2 * (u % 2) + hf, :], qh[j][0:HD, qc * P:(qc + 1) * P],
                                           kh[j][0:HD, hf * HALF:(hf + 1) * HALF], start=True, stop=True)
                        mm.then_inc(s_ps.h, 1)

                    def turn(u):
                        pe.wait_ge(s_exp.h, s_exp.at(img, base + (u + 1)))
                        if u >= 1:
                            pe.wait_ge(t_sb.h, t_sb.at(img, base + u))
                        for b in range(LB):
                            mm = pe.matmul(ps[:, 4 + b // 4, (b % 4) * P:(b % 4 + 1) * P],
                                           probs[u % 2][:, b * P:(b + 1) * P], ident[:, :],
                                           start=True, stop=True, is_transpose=True)
                        mm.then_inc(t_ps.h, 1)

                    def values(u):
                        pe.wait_ge(t_sb.h, t_sb.at(img, base + (u + 1)))
                        pe.wait_ge(o_sb.h, o_sb.at(img, base + max(u - 1, 0)))
                        for b in range(LB):
                            mm = pe.matmul(ps[:, 6 + u % 2, 0:HD], probsT[u % 2][:, b, :],
                                           vT[:, b, bass.ds(pair * 64 + 32 * (u // LB), HD)],
                                           start=b == 0, stop=b == LB - 1)
                        mm.then_inc(pv_ps.h, 1)

                    for u in range(18):
                        if u < 16:
                            scores(u)
                        if 1 <= u < 17:
                            turn(u - 1)
                        if u >= 2:
                            values(u - 2)
                pe.wait_ge(o_sb.h, o_sb.at(img, STEPS0))
                for m in range(NC):
                    if m:
                        pe.wait_ge(vo_sb.h, vo_sb.at(img, 2 * m))
                    project(banks(0), w0[:, :, 2 * C + m * P:2 * C + (m + 1) * P], rows_of(xn0)).then_inc(vo_ps.h, 1)
                    project(banks(2), w0[:, :, 3 * C + m * P:3 * C + (m + 1) * P], rows_of(xn0)).then_inc(vo_ps.h, 1)
                    if m:
                        pe.wait_ge(r_sb.h, r_sb.at(img, m))
                    for b in range(LB):
                        mm = pe.matmul(ps[:, 4 + b // 4, (b % 4) * P:(b % 4 + 1) * P],
                                       heads[:, b, m * P:(m + 1) * P], ident[:, :],
                                       start=True, stop=True, is_transpose=True)
                    mm.then_inc(hT_ps.h, 1)
                pe.wait_ge(r_sb.h, r_sb.at(img, NC))
                wp0 = w_proj0[:, :].rearrange("p (c o) -> p c o", c=NC)
                for m in range(NC):
                    if m == 2:
                        pe.wait_ge(x1.h, x1.at(img, 1))
                    project(banks(2 * (m % 2)), wp0[:, :, m * P:(m + 1) * P], rows_of(res)).then_inc(p0_ps.h, 1)

                group_norm(img, 1)
                pe.wait_ge(gn_out.h, gn_out.at(img, 2))
                wx = w_xproj[:, :].rearrange("p (c k r) -> p c k r", c=NC, k=K)
                wd = w_dt[:, :].rearrange("p (k d) -> p k d", k=K)

                def merge():
                    pe.wait_ge(y_sb.h, y_sb.at(img, 2 * 12))
                    for c in range(NC):
                        if c:
                            pe.wait_ge(mg_sb.h, mg_sb.at(img, c))
                        for b in range(LB):
                            mm = pe.matmul(ps[:, 2 + b // 4, (b % 4) * P:(b % 4 + 1) * P], ysum[:, b, c * P:(c + 1) * P],
                                           ident[:, :], start=True, stop=True, is_transpose=True)
                        mm.then_inc(mg_ps.h, 1)
                        pe.wait_ge(mg_sb.h, mg_sb.at(img, c + 1))
                        if c:
                            pe.wait_ge(mg_y.h, mg_y.at(img, c))
                        for b in range(LB):
                            mm = pe.matmul(ps[:, 4 + b // 4, (b % 4) * P:(b % 4 + 1) * P],
                                           decay[c % 2][:, b * P:(b + 1) * P], ident[:, :], start=True, stop=True,
                                           is_transpose=True)
                        mm.then_inc(mg_tp.h, 1)
                    pe.wait_ge(mg_y.h, mg_y.at(img, NC))

                for k, (cols, back) in enumerate(DIRS):
                    if k == 2:
                        merge()
                    if not cols:
                        rhs = rows_of(U)
                    else:
                        rhs = lambda c, hf: transposed(U[:, c, :])[:, hf * 16:(hf + 1) * 16, :]
                    if k:
                        pe.wait_ge(dt_abs.h, dt_abs.at(img, k * NC))
                        pe.wait_ge(dt_rel.h, dt_rel.at(img, k * NC))
                    project(banks(6), wx[:, :, cols + 2 * back, :], rhs, XR).then_inc(xd_ps.h, 1)
                    pe.wait_ge(xd_sb.h, xd_sb.at(img, k + 1))
                    for c in range(NC):
                        if c:
                            pe.wait_ge(dt_abs.h, dt_abs.at(img, k * NC + c))
                            pe.wait_ge(dt_rel.h, dt_rel.at(img, k * NC + c))
                        for hf in range(2):
                            mm = pe.matmul(ps[:, 6 + hf, :], wd[32:32 + R, cols + 2 * back, c * P:(c + 1) * P],
                                           xdbl[32:32 + R, hf * HALF:(hf + 1) * HALF], start=True, stop=True)
                        mm.then_inc(dt_ps.h, 1)
                    with pe.Fori(0, 2) as gp:
                        for u in range(24):
                            run = u // GN_
                            yb = 4 - 2 * (run % 2)
                            pe.wait_ge(hc_sb.h, hc_sb.at(img, k * 48 + gp * 24 + (u + 1)))
                            if u % GN_ == 0:
                                pe.wait_ge(y_sb.h, y_sb.at(img, k * 12 + gp * 6 + max(run - 1, 0)))
                            for b in range(LB):
                                lhs = state[u % 4][:, b * P:(b + 1) * P]
                                mm = pe.matmul(ps[:, yb + b // 4, (b % 4) * P:(b % 4 + 1) * P], lhs, ident[:, :],
                                               start=u % GN_ == 0 and b % 4 == 0, stop=u % GN_ == GN_ - 1,
                                               is_transpose=True, skip_group_check=True)
                            mm.then_inc(y_ps.h, 1)
                pe.wait_ge(ln_o.h, ln_o.at(img, 1))
                for c in range(NC):
                    if c == 2:
                        pe.wait_ge(g_sb.h, g_sb.at(img, 1))
                    for b in range(LB):
                        mm = pe.matmul(ps[:, 2 * (c % 2) + b // 4, (b % 4) * P:(b % 4 + 1) * P],
                                       ysum[:, b, c * P:(c + 1) * P], ident[:, :], start=True, stop=True,
                                       is_transpose=True)
                    mm.then_inc(lt_ps.h, 1)

                group_norm(img, 2)
                pe.wait_ge(s2_ld.h, s2_ld.at(img, 64))
                pe.wait_ge(w_in.h, w_in.at(img, 32))
                sy = shift_y[:, :].rearrange("p (g m) -> p g m", g=PG)
                for r in range(6):
                    if r >= 2:
                        pe.wait_ge(m2_sb.h, m2_sb.at(img, r - 1))
                    for j in range(4):
                        gh = 4 * r + j
                        mm = pe.matmul(ps[:, r % 2, j * P:(j + 1) * P], rows2[:, 4 * gh:4 * gh + 4, :], sy[:, gh // 2, :],
                                       start=True, stop=True)
                    mm.then_inc(m2_ps.h, 1)
                for r in range(6):
                    pe.wait_ge(m2_sb.h, m2_sb.at(img, r + 1))
                    if r >= 2:
                        pe.wait_ge(o2_sb.h, o2_sb.at(img, r - 1))
                    for j in range(4):
                        gh = 4 * r + j
                        for q in range(4):
                            mm = pe.matmul(ps[32 * q:32 * q + 32, 2 + r % 2, j * P:(j + 1) * P],
                                           mid2[:, gh, 32 * q:32 * q + 32], shift_x[:, q * PG + gh // 2, :],
                                           start=True, stop=True)
                    mm.then_inc(o2_ps.h, 1)

                group_norm(img, 3)
                pe.wait_ge(gn_out.h, gn_out.at(img, 4))
                pe.wait_ge(w_in.h, w_in.at(img, 128))
                for i in range(4):
                    if i >= 2:
                        pe.wait_ge(p3_sb.h, p3_sb.at(img, i - 1))
                    w = (wq3, wk3)[i // 2]
                    project(banks(2 * (i % 2)), w[:, :, (i % 2) * QC3:(i % 2 + 1) * QC3], rows_of(xn3), QC3)\
                        .then_inc(p3_ps.h, 1)
                for b in range(LB):
                    if b >= 2:
                        pe.wait_ge(v3_sb.h, v3_sb.at(img, b - 1))
                    for c in range(NC):
                        mm = pe.matmul(ps[:, 4 + b % 2, 0:C], xn3[:, c, b * P:(b + 1) * P], wv3[:, c, :],
                                       start=c == 0, stop=c == NC - 1)
                    mm.then_inc(v3_ps.h, 1)
                pe.wait_ge(p3_sb.h, p3_sb.at(img, 4))
                pe.wait_ge(v3_sb.h, v3_sb.at(img, LB))

                def scores3(u):
                    if u >= 2:
                        pe.wait_ge(s3_ex.h, s3_ex.at(img, u - 1))
                    for hf in range(2):
                        for a in range(2):
                            mm = pe.matmul(ps[:, 2 * (u % 2) + hf, :], q3[0:QC3, a, u * P:(u + 1) * P],
                                           k3[0:QC3, a, hf * HALF:(hf + 1) * HALF], start=a == 0, stop=a == 1)
                    mm.then_inc(s3_ps.h, 1)

                def turn3(u):
                    pe.wait_ge(s3_nm.h, s3_nm.at(img, u + 1))
                    if u:
                        pe.wait_ge(s3_ts.h, s3_ts.at(img, u))
                    for b in range(LB):
                        mm = pe.matmul(ps[:, 4 + b // 4, (b % 4) * P:(b % 4 + 1) * P],
                                       prob3[u % 2][:, b * P:(b + 1) * P], ident[:, :],
                                       start=True, stop=True, is_transpose=True)
                    mm.then_inc(s3_tp.h, 1)

                def values3(hf):
                    pe.wait_ge(s3_ts.h, s3_ts.at(img, 4 * hf + 4))
                    for m in range(NC):
                        i = hf * NC + m
                        if i >= 2:
                            pe.wait_ge(y3_sb.h, y3_sb.at(img, i - 1))
                        for b in range(LB):
                            mm = pe.matmul(ps[:, 6 + i % 2, :], vT3[:, b, m * P:(m + 1) * P], prT3[hf][:, b, :],
                                           start=b == 0, stop=b == LB - 1)
                        mm.then_inc(y3_ps.h, 1)

                for u in range(LB + 1):
                    if u < LB:
                        scores3(u)
                    if u >= 1:
                        turn3(u - 1)
                    if u == 5:
                        values3(0)
                values3(1)
                pe.wait_ge(se_pool.h, se_pool.at(img, 1))
                for c in range(NC):
                    mm = pe.matmul(ps[0:SE, 0, 0:1], wse1[:, c, :], se_t[:, 8 + c:9 + c], start=c == 0, stop=c == NC - 1)
                mm.then_inc(se_h.h, 1)
                pe.wait_ge(se_hr.h, se_hr.at(img, 1))
                for c in range(NC):
                    mm = pe.matmul(ps[:, 1, c:c + 1], wse2[:, c * P:(c + 1) * P], se_t[0:SE, 12:13], start=True, stop=True)
                mm.then_inc(se_z.h, 1)
                pe.wait_ge(se_w.h, se_w.at(img, 1))
                pe.wait_ge(y3_sb.h, y3_sb.at(img, 2 * NC))
                for m in range(NC):
                    if m == 2:
                        pe.wait_ge(f_sb.h, f_sb.at(img, 1))
                    project(banks(2 * (m % 2)), wg3[:, :, m * P:(m + 1) * P], rows_of(y3)).then_inc(f_ps.h, 1)

        @block.scalar
        def _(act):
            act.wait_ge(c_in.h, 16 * 16)
            act.activation(negA[:, :], negA[:, :], ACT.Exp).then_inc(pre_a.h, 1)
            act.wait_ge(pre_v.h, 1)
            for which, n in enumerate((PG, POS)):
                at = 1024 + which * 8192
                for lo, wide in [(at, n * 32)] + [(at + 2048 + 64 * j, n) for j in range(5)]:
                    act.activation(R_[:, lo:lo + wide], R_[:, lo:lo + wide], ACT.Exp, scale=-2.0).then_inc(pre_a.h, 1)
            act.wait_ge(pre_v.h, 3)

            with act.Fori(0, B) as img:
                for i in range(6):
                    act.wait_ge(qk_ps.h, qk_ps.at(img, i + 1))
                    if i < 2:
                        act.wait_ge(qk_st[i].h, qk_st[i].at(img, 0))
                    else:
                        act.wait_ge(qk_st[i % 2].h, qk_st[i % 2].at(img, 16 * (i // 2)))
                    if i < 3:
                        act.activation(stage[i % 2], banks(2 * (i % 2)), ACT.Identity, bias=qb[:, i:i + 1], scale=SC0)\
                            .then_inc(qk_sb.h, 1)
                    else:
                        act.activation(stage[i % 2], banks(2 * (i % 2)), ACT.Identity, bias=vec("bk", i - 3))\
                            .then_inc(qk_sb.h, 1)
                with act.Fori(0, HEADS // 2) as pair:
                    base = pair * 16

                    def exps(u):
                        act.wait_ge(s_max.h, s_max.at(img, base + (u + 1)))
                        act.wait_ge(t_ps.h, t_ps.at(img, base + max(u - 1, 0)))
                        act.activation(probs[u % 2], banks(2 * (u % 2)), ACT.Exp, bias=negmax[:, u % 8:u % 8 + 1],
                                       accum_out=rowsum[:, u % 8:u % 8 + 1]).then_inc(s_exp.h, 1)

                    def turned(u):
                        act.wait_ge(t_ps.h, t_ps.at(img, base + (u + 1)))
                        act.wait_ge(pv_ps.h, pv_ps.at(img, base + max(u - 1, 0)))
                        act.activation(probsT[u % 2].rearrange("p b q -> p (b q)"), banks(4), ACT.Copy)\
                            .then_inc(t_sb.h, 1)

                    for u in range(17):
                        if u < 16:
                            exps(u)
                        if u >= 1:
                            turned(u - 1)
                for m in range(NC):
                    act.wait_ge(vo_ps.h, vo_ps.at(img, 2 * m + 1))
                    if m:
                        act.wait_ge(r_sb.h, r_sb.at(img, m))
                    inner = vpad[:, :].rearrange("p (h w) -> p h w", w=36)[:, 2:34, 2:34]
                    act.activation(inner, banks(0).rearrange("p (h w) -> p h w", w=WW), ACT.Identity, bias=vec("bv", m))\
                        .then_inc(vo_sb.h, 1)
                    act.wait_ge(vo_ps.h, vo_ps.at(img, 2 * m + 2))
                    act.activation(gate0, banks(2), ACT.Identity, bias=vec("bo", m)).then_inc(vo_sb.h, 1)
                for k, (cols, back) in enumerate(DIRS):
                    act.wait_ge(xd_ps.h, xd_ps.at(img, k + 1))
                    if k:
                        act.wait_ge(bc_st.h, bc_st.at(img, 16 * k))
                    act.activation(xdbl[0:XR, :], banks(6)[0:XR, :], ACT.Copy).then_inc(xd_sb.h, 1)
                    for c in range(NC):
                        i = k * NC + c
                        act.wait_ge(dt_rel.h, dt_rel.at(img, i + 1))
                        if c == 0 and k:
                            act.wait_ge(y_ps.h, y_ps.at(img, 48 * k))
                        if c == 2:
                            act.wait_ge(dt_sb.h, dt_sb.at(img, i - 1))
                        s = soft[c % 2]
                        act.activation(s, banks(6), ACT.Abs, bias=vec(f"dtb{cols + 2 * back}", c)).then_inc(dt_abs.h, 1)
                        act.drain()
                        act.activation(s, s, ACT.Exp, scale=-1.0)
                        act.drain()
                        act.activation(s, s, ACT.Ln, bias=1.0).then_inc(dt_ln.h, 1)
                    with act.Fori(0, 2) as gp:
                        for u in range(24):
                            g, c, n = u // 12, (u // 4) % 3, u % 4
                            if u < 12 and n == 0:
                                act.wait_ge(dt_sb.h, dt_sb.at(img, k * NC + c + 1))
                            act.wait_ge(h_sb.h, h_sb.at(img, k * 48 + gp * 24 + max(u - 1, 0)))
                            col = gp * 8 + ((cols + 2 * back) * NC * N + c * N + g * 4 + n)
                            act.activation(decay[u % 2], dt[:, c, :], ACT.Exp, scale=negA[:, bass.ds(col, 1)])\
                                .then_inc(a_sb.h, 1)
                for c in range(NC):
                    act.wait_ge(lt_ps.h, lt_ps.at(img, c + 1))
                    if c == 2:
                        act.wait_ge(x2.h, x2.at(img, 1))
                    act.activation(gel[c % 2], banks(2 * (c % 2)), ACT.Gelu, bias=vec("ln_b", c), scale=vec("ln_w", c))\
                        .then_inc(g_sb.h, 1)
                for r in range(6):
                    act.wait_ge(m2_ps.h, m2_ps.at(img, r + 1))
                    act.activation(mid2[:, 4 * r:4 * r + 4, :].rearrange("p a m -> p (a m)"), ps[:, r % 2, :], ACT.Copy)\
                        .then_inc(m2_sb.h, 1)
                for i in range(4):
                    act.wait_ge(p3_ps.h, p3_ps.at(img, i + 1))
                    if i < 2:
                        act.activation(q3[0:QC3, i, :], banks(2 * (i % 2))[0:QC3, :], ACT.Identity,
                                       bias=qb3[0:QC3, i:i + 1], scale=SC3).then_inc(p3_sb.h, 1)
                    else:
                        act.activation(k3[0:QC3, i - 2, :], banks(2 * (i % 2))[0:QC3, :], ACT.Identity,
                                       bias=vec96[0:QC3, i:i + 1]).then_inc(p3_sb.h, 1)

                def exps3(u):
                    act.wait_ge(s3_mx.h, s3_mx.at(img, u + 1))
                    if u >= 2:
                        act.wait_ge(s3_tp.h, s3_tp.at(img, u - 1))
                    act.activation(prob3[u % 2], banks(2 * (u % 2)), ACT.Exp, bias=se_t[:, 16 + u:17 + u],
                                   accum_out=se_t[:, 24 + u:25 + u]).then_inc(s3_ex.h, 1)

                def turned3(u):
                    act.wait_ge(s3_tp.h, s3_tp.at(img, u + 1))
                    hf, j = u // 4, u % 4
                    act.activation(prT3[hf][:, :, j * P:(j + 1) * P], banks(4).rearrange("p (b q) -> p b q", b=LB),
                                   ACT.Copy).then_inc(s3_ts.h, 1)

                def values3(hf):
                    for m in range(NC):
                        i = hf * NC + m
                        act.wait_ge(y3_ps.h, y3_ps.at(img, i + 1))
                        act.activation(y3[:, m, hf * HALF:(hf + 1) * HALF], ps[:, 6 + i % 2, :], ACT.Identity,
                                       bias=vec("bv3", m), accum_out=se_t[:, i:i + 1]).then_inc(y3_sb.h, 1)

                for u in range(LB + 1):
                    if u < LB:
                        exps3(u)
                    if u >= 1:
                        turned3(u - 1)
                    if u == 5:
                        values3(0)
                values3(1)
                act.wait_ge(se_zb.h, se_zb.at(img, 1))
                act.activation(se_t[:, 36:39], se_t[:, 33:36], ACT.Exp, scale=-1.0).then_inc(se_e.h, 1)

        @block.gpsimd
        def _(gp_):
            gp_.memset(half_neg[:, :], -0.5).then_inc(pre_g.h, 1)
            gp_.wait_ge(pre_g.h, 1)
            gp_.wait_ge(pre_v.h, 3)
            gp_.tensor_tensor(inv3, tmp_d[:, 0:3], half_neg[:, 0:3], ALU.pow).then_inc(pre_g.h, 1)
            with gp_.Fori(0, B) as img:
                def rstd(g):
                    gp_.wait_ge(gn_eps.h, gn_eps.at(img, g + 1))
                    gp_.tensor_tensor(gn_t[:, 32:35], gn_t[:, 24:27], half_neg[:, 0:3], ALU.pow).then_inc(gn_rstd.h, 1)
                rstd(0)
                rstd(1)
                for k, (cols, back) in enumerate(DIRS):
                    for c in range(NC):
                        i = k * NC + c
                        gp_.wait_ge(dt_ln.h, dt_ln.at(img, i + 1))
                        gp_.wait_ge(dt_rel.h, dt_rel.at(img, i + 1))
                        gp_.tensor_tensor(dt[:, c, :], dt[:, c, :], soft[c % 2], ALU.add)
                        gp_.drain()
                        u_in = transposed(U[:, c, :]) if cols else U[:, c, :]
                        d_in, d_out = dt[:, c, :], dtu[:, c, :]
                        if cols:
                            d_in = d_in.rearrange("p (w h) -> p w h", h=HH)
                            d_out = d_out.rearrange("p (w h) -> p w h", h=HH)
                        gp_.tensor_tensor(d_out, d_in, u_in, ALU.mult).then_inc(dt_sb.h, 1)
                    with gp_.Fori(0, 2) as gp:
                        for u in range(24):
                            g, n = u // 12, u % 4
                            gp_.wait_ge(h_sb.h, h_sb.at(img, k * 48 + gp * 24 + (u + 1)))
                            gp_.tensor_tensor(state[u % 4], state[u % 4], bc[:, g, 1, n, :], ALU.mult)\
                                .then_inc(hc_sb.h, 1)
                gp_.wait_ge(ln_st.h, ln_st.at(img, 1))
                gp_.tensor_tensor(ln_t[:, 16:24], ln_t[:, 24:32], half_neg[:, 0:8], ALU.pow).then_inc(ln_r.h, 1)
                rstd(2)
                rstd(3)

        @block.vector
        def _(v):
            v.memset(vpad[:, :], 0.0)
            v.wait_ge(c_in.h, 16 * 16)
            v.memset(ws[:, :], 0.0)
            v.memset(shift_y[:, :], 0.0)
            sidx, yrow = R_[:, 0:1], R_[:, 32:64]
            kinds = []
            for which, (n, off) in enumerate(((PG, R_[:, 64:64 + 2 * PG].rearrange("p (g d) -> p g d", d=2)[:, :, 1]),
                                              (POS, R_[:, 96:96 + 2 * POS].rearrange("p (g d) -> p g d", d=2)[:, :, 0]))):
                at = 1024 + which * 8192
                expo = R_[:, at:at + n * 32].rearrange("p (g y) -> p g y", y=32)
                band = R_[:, at + 4096:at + 4096 + n * 32].rearrange("p (g y) -> p g y", y=32)
                taps = [R_[:, at + 2048 + 64 * j:at + 2048 + 64 * j + n] for j in range(5)]
                rnd, sub, moved, keep, tot = (R_[:, at + 3072 + 64 * j:at + 3072 + 64 * j + n] for j in range(5))
                MAGIC = 12582912.0
                v.tensor_scalar(rnd, off, MAGIC, None, ALU.add)
                v.drain()
                v.tensor_scalar(rnd, rnd, MAGIC, None, ALU.subtract)
                v.drain()
                v.tensor_tensor(sub, off, rnd, ALU.subtract)
                v.drain()
                v.tensor_scalar(sub, sub, 0.5, -0.5, ALU.min, ALU.max)
                v.tensor_scalar(moved, rnd, sidx, None, ALU.add)
                v.drain()
                v.tensor_scalar(keep, moved, 0.0, None, ALU.is_ge)
                v.tensor_scalar(tot, moved, 31.0, None, ALU.is_le)
                v.drain()
                v.tensor_tensor(keep, keep, tot, ALU.mult)
                v.tensor_tensor(band, moved[:, :, None].to_broadcast([P, n, 32]),
                                yrow[:, None, :].to_broadcast([P, n, 32]), ALU.subtract)
                v.drain()
                v.tensor_tensor(expo, band, sub[:, :, None].to_broadcast([P, n, 32]), ALU.add)
                v.drain()
                v.tensor_tensor(expo, expo, expo, ALU.mult)
                v.tensor_tensor(band, band, band, ALU.mult)
                v.drain()
                v.tensor_scalar(band, band, 4.5, None, ALU.is_le)
                for j in range(5):
                    v.tensor_scalar(taps[j], sub, float(j - 2), None, ALU.add)
                v.drain()
                for j in range(5):
                    ins = v.tensor_tensor(taps[j], taps[j], taps[j], ALU.mult)
                kinds.append((n, expo, band, taps, keep, tot))
            ins.then_inc(pre_v.h, 1)
            v.wait_ge(pre_a.h, 1 + 2 * 6)
            for which, (n, expo, band, taps, keep, tot) in enumerate(kinds):
                v.tensor_tensor(tot, taps[0], taps[1], ALU.add)
                for j in range(2, 5):
                    v.drain()
                    v.tensor_tensor(tot, tot, taps[j], ALU.add)
                v.drain()
                v.reciprocal(tot, tot)
                v.drain()
                v.tensor_tensor(keep, keep, tot, ALU.mult)
                v.tensor_tensor(expo, expo, band, ALU.mult)
                v.drain()
                v.tensor_tensor(expo, expo, keep[:, :, None].to_broadcast([P, n, 32]), ALU.mult)
                v.drain()
                dst = (shift_y[:, :] if which == 0 else ws[:, 0:POS * P]).rearrange("p (g q y) -> p g q y", q=4, y=32)
                for q in range(4):
                    ins = v.tensor_copy(dst[32 * q:32 * q + 32, :, q, :], expo[32 * q:32 * q + 32, :, :])
            ins.then_inc(pre_v.h, 1)
            v.tensor_scalar(negA[:, :], negA[:, :], -1.0, None, ALU.mult)
            v.tensor_scalar(qb, vecs[:, VEC["bq"] * NC:VEC["bq"] * NC + NC], SC0, None, ALU.mult)
            v.tensor_scalar(qb3[0:QC3, :], vec96[0:QC3, 0:2], SC3, None, ALU.mult)

            def vec3(name):
                return vecs[:, VEC[name] * NC:VEC[name] * NC + NC]
            v.tensor_tensor(dsum, vec3("D0"), vec3("D1"), ALU.add)
            v.drain()
            v.tensor_tensor(dsum, dsum, vec3("D2"), ALU.add)
            v.drain()
            v.tensor_tensor(dsum, dsum, vec3("D3"), ALU.add)
            v.tensor_scalar(tmp_d[:, 0:3], vec3("var"), EPS, None, ALU.add).then_inc(pre_v.h, 1)
            v.wait_ge(pre_g.h, 2)
            v.tensor_tensor(inv3, inv3, vec3("gamma"), ALU.mult)
            v.tensor_tensor(cst3, vec3("bproj3"), vec3("mean"), ALU.subtract)
            v.drain()
            v.tensor_tensor(cst3, cst3, inv3, ALU.mult)
            v.drain()
            v.tensor_tensor(cst3, cst3, vec3("beta"), ALU.add)
            v.drain()

            def group_norm(img, g, dst):
                agg = gn_t[:, 6:12].rearrange("p (c s) -> p c s", s=2)
                bst = stats
                for c in range(NC):
                    for hf in range(2):
                        v.bn_stats(bst[:, c * 12 + hf * 6:c * 12 + hf * 6 + 6], X3[:, c, hf * HALF:(hf + 1) * HALF])
                v.drain()
                for c in range(NC):
                    v.bn_aggr(agg[:, c, :], bst[:, c * 12:c * 12 + 12])
                v.drain()
                v.tensor_copy(gn_t[:, 0:3], agg[:, :, 0]).then_inc(gn_stat.h, 1)
                v.wait_ge(gn_mean.h, gn_mean.at(img, g + 1))
                v.tensor_copy(gn_t[:, 3:6], ps[:, 7, 0:3])
                v.drain()
                v.tensor_tensor(gn_t[:, 12:15], gn_t[:, 0:3], gn_t[:, 3:6], ALU.subtract)
                v.drain()
                v.tensor_tensor(gn_t[:, 12:15], gn_t[:, 12:15], gn_t[:, 12:15], ALU.mult)
                v.drain()
                v.tensor_tensor(gn_t[:, 16:19], gn_t[:, 12:15], agg[:, :, 1], ALU.add).then_inc(gn_dev.h, 1)
                v.wait_ge(gn_var.h, gn_var.at(img, g + 1))
                v.tensor_scalar(gn_t[:, 24:27], ps[:, 7, 8:11], EPS, None, ALU.add).then_inc(gn_eps.h, 1)
                v.wait_ge(gn_rstd.h, gn_rstd.at(img, g + 1))
                for c in range(NC):
                    ins = v.tensor_scalar(dst[:, c, :], X3[:, c, :], gn_t[:, 3 + c:4 + c], gn_t[:, 32 + c:33 + c],
                                          ALU.subtract, ALU.mult)
                ins.then_inc(gn_out.h, 1)

            with v.Fori(0, B) as img:
                v.wait_ge(x_in.h, x_in.at(img, 16))
                v.wait_ge(f_ps.h, f_ps.at(img, 0))
                group_norm(img, 0, xn0)
                for b in range(LB):
                    v.wait_ge(vt_ps.h, vt_ps.at(img, b + 1))
                    v.tensor_copy(vT[:, b, :], ps[:, 4 + b % 2, 0:C]).then_inc(vt_sb.h, 1)
                with v.Fori(0, HEADS // 2) as pair:
                    base = pair * 16

                    def rowmax(u):
                        v.wait_ge(s_ps.h, s_ps.at(img, base + (u + 1)))
                        v.tensor_reduce(negmax[:, u % 8:u % 8 + 1], banks(2 * (u % 2)), AX.X, ALU.max, negate=True)\
                            .then_inc(s_max.h, 1)

                    def head_out(u):
                        v.wait_ge(s_exp.h, s_exp.at(img, base + (u + 1)))
                        v.reciprocal(rowinv[:, u % 8:u % 8 + 1], rowsum[:, u % 8:u % 8 + 1])
                        v.drain()
                        v.wait_ge(pv_ps.h, pv_ps.at(img, base + (u + 1)))
                        v.tensor_scalar(heads[:, u % LB, bass.ds(pair * 64 + 32 * (u // LB), HD)], ps[:, 6 + u % 2, 0:HD],
                                        rowinv[:, u % 8:u % 8 + 1], None, ALU.mult).then_inc(o_sb.h, 1)

                    for u in range(19):
                        if u < 16:
                            rowmax(u)
                        if u >= 3:
                            head_out(u - 3)
                vp = vpad[:, :].rearrange("p (h w) -> p h w", w=36)
                lep3 = lep.rearrange("p (h w) -> p h w", w=WW)
                for m in range(NC):
                    v.wait_ge(vo_sb.h, vo_sb.at(img, 2 * m + 1))
                    for j in range(25):
                        win = vp[:, j // 5:j // 5 + HH, j % 5:j % 5 + WW]
                        w = lepe_w[:, m * 25 + j:m * 25 + j + 1]
                        if j == 0:
                            v.tensor_scalar(lep3, win, w, vec("lepe_b", m), ALU.mult, ALU.add)
                        else:
                            v.drain()
                            v.scalar_tensor_tensor(lep3, win, w, lep3, ALU.mult, ALU.add)
                    v.drain()
                    v.wait_ge(hT_ps.h, hT_ps.at(img, m + 1))
                    v.scalar_tensor_tensor(lep, banks(4), vec("bv", m), lep, ALU.add, ALU.add)
                    v.drain()
                    v.wait_ge(vo_sb.h, vo_sb.at(img, 2 * m + 2))
                    v.tensor_tensor(res[:, m, :], lep, gate0, ALU.mult).then_inc(r_sb.h, 1)
                for m in range(NC):
                    v.wait_ge(p0_ps.h, p0_ps.at(img, m + 1))
                    v.scalar_tensor_tensor(X3[:, m, :], banks(2 * (m % 2)), vec("proj_b", m), X3[:, m, :],
                                           ALU.add, ALU.add).then_inc(x1.h, 1)
                v.drain()
                group_norm(img, 1, U)
                v.memset(R_[:, 3 * K1:6 * K1], 0.0)
                v.drain()
                for k, (cols, back) in enumerate(DIRS):
                    if k == 2:
                        for c in range(NC):
                            v.wait_ge(mg_ps.h, mg_ps.at(img, c + 1))
                            v.scalar_tensor_tensor(decay[c % 2].rearrange("p (h w) -> p h w", w=WW),
                                                   U[:, c, :].rearrange("p (h w) -> p h w", w=WW), dsum[:, c:c + 1],
                                                   banks(2).rearrange("p (w h) -> p h w", h=HH), ALU.mult, ALU.add)\
                                .then_inc(mg_sb.h, 1)
                            v.wait_ge(mg_tp.h, mg_tp.at(img, c + 1))
                            v.tensor_copy(ysum[:, :, c * P:(c + 1) * P], banks(4).rearrange("p (b c) -> p b c", b=LB))\
                                .then_inc(mg_y.h, 1)
                        v.drain()
                    for c in range(NC):
                        i = k * NC + c
                        v.wait_ge(dt_ps.h, dt_ps.at(img, i + 1))
                        if c == 0 and k:
                            v.wait_ge(a_sb.h, a_sb.at(img, 48 * k))
                        v.tensor_scalar(dt[:, c, :], banks(6), vec(f"dtb{cols + 2 * back}", c), 0.0, ALU.add, ALU.max)\
                            .then_inc(dt_rel.h, 1)
                    with v.Fori(0, 2) as gp:
                        base = gp * 24 + k * 48

                        def drive(u):
                            g, c, n = u // 12, (u // 4) % 3, u % 4
                            if u % 12 == 0:
                                v.wait_ge(bc_ld[g].h, bc_ld[g].at(img, gp * 32 + (64 * k + 32)))
                            if u == 0:
                                v.wait_ge(dt_sb.h, dt_sb.at(img, k * NC + NC))
                            v.wait_ge(y_ps.h, y_ps.at(img, base + max(u - 3, 0)))
                            v.tensor_tensor(state[u % 4], dtu[:, c, :], bc[:, g, 0, n, :], ALU.mult).then_inc(b_sb.h, 1)

                        def scan(u):
                            v.wait_ge(a_sb.h, a_sb.at(img, base + (u + 1)))
                            v.wait_ge(b_sb.h, b_sb.at(img, base + (u + 1)))
                            d, s = decay[u % 2], state[u % 4]
                            if back:
                                d, s = d[:, ::-1], s[:, ::-1]
                            v.tensor_tensor_scan(s, d, s, 0.0, ALU.mult, ALU.add).then_inc(h_sb.h, 1)

                        def add_y(run):
                            yb = 4 - 2 * (run % 2)
                            v.wait_ge(y_ps.h, y_ps.at(img, base + (4 * run + 4)))
                            ysl = ysum[:, :, (run % 3) * P:(run % 3 + 1) * P]
                            v.tensor_tensor(ysl, ysl, banks(yb).rearrange("p (b c) -> p b c", b=LB), ALU.add)\
                                .then_inc(y_sb.h, 1)

                        for u in range(25):
                            if u < 24:
                                drive(u)
                            if u >= 1:
                                scan(u - 1)
                            if u >= 6 and (u - 6) % 4 == 0:
                                add_y((u - 6) // 4)
                        add_y(5)
                v.drain()
                bst = stats[:, 0:48].rearrange("p (b s) -> p b s", s=6)
                for b in range(LB):
                    v.bn_stats(bst[:, b, :], ysum[:, b, :])
                v.drain()
                agg = ln_t[:, 0:16].rearrange("p (b s) -> p b s", s=2)
                for b in range(LB):
                    v.bn_aggr(agg[:, b, :], bst[:, b, :])
                v.drain()
                v.tensor_scalar(ln_t[:, 24:32], agg[:, :, 1], EPS, None, ALU.add).then_inc(ln_st.h, 1)
                v.wait_ge(ln_r.h, ln_r.at(img, 1))
                for b in range(LB):
                    ins = v.tensor_scalar(ysum[:, b, :], ysum[:, b, :], agg[:, b, 0:1], ln_t[:, 16 + b:17 + b],
                                          ALU.subtract, ALU.mult)
                ins.then_inc(ln_o.h, 1)
                for c in range(NC):
                    v.wait_ge(g_sb.h, g_sb.at(img, c + 1))
                    v.tensor_tensor(X3[:, c, :], X3[:, c, :], gel[c % 2], ALU.add).then_inc(x2.h, 1)
                v.drain()
                group_norm(img, 2, xn2)
                for r in range(6):
                    v.wait_ge(o2_ps.h, o2_ps.at(img, r + 1))
                    v.tensor_copy(out2[:, 16 * r:16 * r + 16, :].rearrange("p a s -> p (a s)"), ps[:, 2 + r % 2, :])\
                        .then_inc(o2_sb.h, 1)
                v.wait_ge(b2_ld.h, b2_ld.at(img, 16))
                ins = v.tensor_tensor(X[:, :], X[:, :], blur.rearrange("p c l -> p (c l)"), ALU.add)
                ins.then_inc(x3.h, 1)
                v.drain()
                group_norm(img, 3, xn3)
                for c in range(NC):
                    v.tensor_scalar(X3[:, c, :], X3[:, c, :], cst3[:, c:c + 1], None, ALU.add)
                for b in range(LB):
                    v.wait_ge(v3_ps.h, v3_ps.at(img, b + 1))
                    v.tensor_copy(vT3[:, b, :], ps[:, 4 + b % 2, 0:C]).then_inc(v3_sb.h, 1)

                def rowmax3(u):
                    v.wait_ge(s3_ps.h, s3_ps.at(img, u + 1))
                    v.tensor_reduce(se_t[:, 16 + u:17 + u], banks(2 * (u % 2)), AX.X, ALU.max, negate=True)\
                        .then_inc(s3_mx.h, 1)

                def normalize3(u):
                    v.wait_ge(s3_ex.h, s3_ex.at(img, u + 1))
                    v.reciprocal(se_t[:, 40 + u:41 + u], se_t[:, 24 + u:25 + u])
                    v.drain()
                    v.tensor_scalar(prob3[u % 2], prob3[u % 2], se_t[:, 40 + u:41 + u], None, ALU.mult)\
                        .then_inc(s3_nm.h, 1)

                for u in range(LB + 1):
                    if u < LB:
                        rowmax3(u)
                    if u >= 1:
                        normalize3(u - 1)
                v.wait_ge(y3_sb.h, y3_sb.at(img, 2 * NC))
                v.tensor_tensor(se_t[:, 8:11], se_t[:, 0:3], se_t[:, 3:6], ALU.add)
                v.drain()
                v.tensor_scalar(se_t[:, 8:11], se_t[:, 8:11], 1.0 / L, None, ALU.mult).then_inc(se_pool.h, 1)
                v.wait_ge(se_h.h, se_h.at(img, 1))
                v.tensor_scalar(se_t[0:SE, 12:13], ps[0:SE, 0, 0:1], vec96[0:SE, 4:5], 0.0, ALU.add, ALU.max)\
                    .then_inc(se_hr.h, 1)
                v.wait_ge(se_z.h, se_z.at(img, 1))
                v.tensor_tensor(se_t[:, 33:36], ps[:, 1, 0:3], vec3("bse2"), ALU.add).then_inc(se_zb.h, 1)
                v.wait_ge(se_e.h, se_e.at(img, 1))
                v.tensor_scalar(se_t[:, 50:53], se_t[:, 36:39], 1.0, None, ALU.add)
                v.drain()
                v.reciprocal(se_t[:, 54:57], se_t[:, 50:53])
                v.drain()
                for c in range(NC):
                    ins = v.tensor_scalar(wg3[:, c, :], wp3[:, c, :], se_t[:, 54 + c:55 + c], None, ALU.mult)
                ins.then_inc(se_w.h, 1)
                for m in range(NC):
                    v.wait_ge(f_ps.h, f_ps.at(img, m + 1))
                    v.scalar_tensor_tensor(X3[:, m, :], banks(2 * (m % 2)), inv3[:, m:m + 1], X3[:, m, :],
                                           ALU.mult, ALU.add).then_inc(f_sb.h, 1)


def _chunks(a):
    return np.ascontiguousarray(a.reshape(NC, P, -1).transpose(1, 0, 2).reshape(P, -1))


def kernel(**inputs):
    import concourse.bacc as bacc
    from concourse.bass_utils import run_bass_kernel_spmd
    a = {n: np.asarray(v) for n, v in inputs.items()}
    ds, dtb = a["L1_conv_Ds"].reshape(K, C), a["L1_conv_dt_projs_bias"]
    qb_ = a["L0_conv_qkvo_b"]
    cols = [qb_[0:C], qb_[C:2 * C], qb_[2 * C:3 * C], qb_[3 * C:], a["L0_conv_lepe_b"], a["L0_conv_proj_b"],
            ds[0], ds[1], ds[2], ds[3], a["L1_conv_ln_weight"], a["L1_conv_ln_bias"], dtb[0], dtb[1], dtb[2], dtb[3],
            a["L3_conv_bv"], a["L3_conv_b_proj"], a["L3_conv_bn_gamma"], a["L3_conv_bn_beta"], a["L3_conv_bn_mean"],
            a["L3_conv_bn_var"], a["L3_conv_b_se2"]]
    vecs = np.stack([v.reshape(NC, P) for v in cols]).transpose(2, 0, 1).reshape(P, NV * NC)
    bq3, bk3 = a["L3_conv_bq"].reshape(2, QC3), a["L3_conv_bk"].reshape(2, QC3)
    vec96 = np.stack([bq3[0], bq3[1], bk3[0], bk3[1], a["L3_conv_b_se1"]], axis=1)
    xw = a["L1_conv_x_proj_weight"]
    xw = np.concatenate([xw[:, R:], xw[:, :R]], axis=1)
    chan = np.arange(C) // (C // GROUPS)
    same = (chan[:, None] == chan[None, :]).astype(np.float32) / (C // GROUPS)
    ga = same.reshape(NC, P, NC, P).transpose(1, 0, 2, 3).reshape(P, -1)
    w3 = lambda w: _chunks(w.T).reshape(P, NC, -1)
    arrays = {
        "x": a["x"].reshape(B, C, L),
        "ident": np.eye(P, dtype=np.float32),
        "group_avg": ga,
        "vecs": vecs, "vec96": vec96,
        "lepe_w": _chunks(a["L0_conv_lepe_w"].reshape(C, 25)),
        "A_logs": a["L1_conv_A_logs"].reshape(K, NC, P, N).transpose(2, 0, 1, 3).reshape(P, -1),
        "w_xproj": _chunks(xw.transpose(2, 0, 1).reshape(C, K * XR)),
        "w_dt": a["L1_conv_dt_projs_weight"].transpose(2, 0, 1).reshape(R, K * C),
        "w_proj0": _chunks(a["L0_conv_proj_w"].reshape(C, C).T),
        "row_index": (np.arange(P) % 32).astype(np.float32).reshape(P, 1),
        "col_row": np.tile(np.arange(32, dtype=np.float32), (P, 1)),
        "offset": a["L2_conv_offset"],
        "w_qkvo": w3(a["L0_conv_qkvo_w"].reshape(4 * C, C)),
        "wq3": w3(a["L3_conv_wq"]), "wk3": w3(a["L3_conv_wk"]), "wv3": w3(a["L3_conv_wv"]),
        "wp3": w3(a["L3_conv_w_proj"]), "wse1": w3(a["L3_conv_w_se1"]), "wse2": a["L3_conv_w_se2"].T,
    }
    nc = bacc.Bacc("TRN2", target_bir_lowering=False, num_devices=1)
    t, feed = {}, {}
    for name, v in arrays.items():
        feed["in_" + name] = np.ascontiguousarray(v)
        t[name] = nc.dram_tensor("in_" + name, v.shape, F32, kind="ExternalInput").ap()
    t["out"] = nc.dram_tensor("out_0", (B, C, L), F32, kind="ExternalOutput").ap()
    for name, shape in [("qk_scratch", (6, P, L)), ("bc_scratch", (K, 2 * N, L)), ("shift_scratch", (P, POS * P)),
                        ("rows_scratch", (C, L)), ("blur_scratch", (C, L))]:
        t[name] = nc.dram_tensor(name, shape, F32, kind="Internal").ap()
    build(nc, t)
    r = run_bass_kernel_spmd(nc, [feed], core_ids=[0])
    return r.results[0]["out_0"].reshape(B, C, HH, WW)
```

```python
import numpy as np
import concourse.bass as bass
from concourse import mybir
from contextlib import ExitStack

F32 = mybir.dt.float32
ACT = mybir.ActivationFunctionType
ALU = mybir.AluOpType
AX = mybir.AxisListType

B, C, HH, WW = 8, 384, 32, 32
L = HH * WW
P = 128
NC = C // P
LB = L // P
HALF = 512
HEADS, HD = 12, 32
SC0 = HD ** -0.5
STEPS0 = HEADS * LB
K, R, N = 4, 12, 16
XR = R + 2 * N
GN_ = 4
SLOTS = 5
STEPS1 = K * NC * N
LAG = 3
POS, CPP = 48, 8
PG = POS // 4
QK3 = 192
QC3 = QK3 // 2
SE = C // 4
SC3 = 32.0 ** -0.5
GROUPS = 32
EPS = 1e-5

VEC = {n: i for i, n in enumerate(
    ["bq", "bk", "bv", "bo", "lepe_b", "proj_b", "D0", "D1", "D2", "D3", "ln_w", "ln_b",
     "dtb0", "dtb1", "dtb2", "dtb3", "bv3", "bproj3", "gamma", "beta", "mean", "var", "bse2"])}
NV = len(VEC)


DIRS = [(1, 0), (1, 1), (0, 0), (0, 1)]


def schedule(attention, scans):
    before = {}

    def put(u, *ev):
        before.setdefault(u, []).append(ev)

    per = STEPS1 // K
    for run in range(STEPS1 // GN_):
        u = GN_ * run + GN_ + LAG
        put(u, "y", run)
        if run >= 2 * per // GN_ - NC and run < 2 * per // GN_:
            put(u, "m", run - (2 * per // GN_ - NC))
    for k in range(1, K):
        for hf in range(2):
            put(per * k - 22 + 3 * hf, "x", k, hf)
        for c in range(NC):
            u = per * k - 6 + GN_ * c
            put(u, "d", k, 2 * c)
            put(u + 1, "d", k, 2 * c + 1)
            put(u + 2, "l", k, c)
            put(u + 4, "t", k, c)
    for a in range(STEPS0):
        put(2 * a + 1, "a", a)
    order = [("x", 0, hf) for hf in range(2)]
    for c in range(NC):
        order += [("d", 0, 2 * c), ("d", 0, 2 * c + 1)]
    for c in range(NC):
        order += [("l", 0, c), ("t", 0, c)]
    for u in range(STEPS1 + LAG + 1):
        order += before.get(u, [])
        if u < STEPS1 + LAG:
            order.append(("s", u))
    order += [("a", STEPS0 + i) for i in range(3)]
    return [ev for ev in order if (attention if ev[0] == "a" else scans)]


def place(i):
    k, u = i // (STEPS1 // K), i % (STEPS1 // K)
    return i, k, u // GN_ % NC, GN_ * (u // (NC * GN_)) + u % GN_


def slot_used(i):
    k, n = i // N, i % N
    return STEPS1 // K * k + NC * GN_ * (n // GN_) + (NC - 1) * GN_ + n % GN_ + 1


class Signal:

    def __init__(self, handle, per):
        self.h, self.per = handle, per

    def at(self, img, n):
        return img * self.per + (n + 1)


def build(nc, t):
    ctx = ExitStack()
    with ctx:
        def sb(name, cols, parts=P):
            return ctx.enter_context(nc.sbuf_tensor(name, [parts, cols], F32))

        signals = []

        def sem(name, per):
            s = Signal(ctx.enter_context(nc.semaphore(name)), per)
            if per:
                signals.append(s)
            return s

        ident = sb("ident", P)
        group_avg = sb("group_avg", NC * NC * P)
        vecs = sb("vecs", NV * NC)
        vec96 = sb("vec96", 5)
        lepe_w = sb("lepe_w", NC * 25)
        negA = sb("negA", K * NC * N)
        w_xproj = sb("w_xproj", NC * K * XR)
        w_dt = sb("w_dt", C)
        derived = sb("derived", 32)
        half_neg = sb("half_neg", 8)
        gn_t = sb("gn_t", 96)
        ln_t = sb("ln_t", 64)
        se_t = sb("se_t", 64)
        stats = sb("stats", 48)
        X = sb("X", NC * L)
        R_ = sb("R", 47 * 1024)
        gn0_t = sb("gn0_t", 40)
        ps = ctx.enter_context(nc.psum_tensor("ps", [P, 8, HALF], F32))

        ga = group_avg[:, :].rearrange("p (a b m) -> p a b m", a=NC, b=NC)
        X3 = X[:, :].rearrange("p (c l) -> p c l", c=NC)

        def reg(at, words):
            return R_[:, at:at + words]

        def vec(name, c):
            i = VEC[name] * NC + c
            return vecs[:, i:i + 1]

        def banks(b):
            return ps[:, b:b + 2, :].rearrange("p b n -> p (b n)")

        K1 = 1024

        def chunks(at):
            return reg(at, NC * L).rearrange("p (c l) -> p c l", c=NC)

        def blocks(at):
            return reg(at, NC * L).rearrange("p (b c) -> p b c", b=LB)

        def weights(at, cols):
            return reg(at, NC * cols).rearrange("p (c o) -> p c o", c=NC)

        q4, k4, vT, heads = chunks(0), chunks(3 * K1), blocks(6 * K1), blocks(9 * K1)
        probs = [reg((12 + i) * K1, K1) for i in range(2)]
        probsT = [reg((14 + i) * K1, K1).rearrange("p (b q) -> p b q", b=LB) for i in range(2)]
        xn0 = chunks(16 * K1)
        w0a = weights(28 * K1, 3 * C)
        w0b = weights(12 * K1, 2 * C)
        wp0 = weights(12 * K1 + NC * 2 * C, C)
        vpad = reg(26 * K1, 36 * 36)
        lep, gate0 = reg(40 * K1, K1), reg(41 * K1, K1)
        res = chunks(42 * K1)
        U, ysum, dt, dtu = chunks(16 * K1), blocks(19 * K1), chunks(22 * K1), chunks(25 * K1)
        bc = [reg((28 + 2 * i) * K1, 2 * K1).rearrange("p (t l) -> p t l", t=2) for i in range(SLOTS)]
        turned = reg(38 * K1, K1)
        decay = [reg((40 + i) * K1, K1) for i in range(2)]
        state = [reg((42 + i) * K1, K1) for i in range(4)]
        xdbl = reg(46 * K1, K1)
        gel = decay
        xn2 = chunks(16 * K1)
        rows2 = reg(19 * K1, 3 * K1).rearrange("p (j s) -> p j s", s=32)
        mid2 = reg(22 * K1, 3 * K1).rearrange("p (g m) -> p g m", m=P)
        out2 = reg(25 * K1, 3 * K1).rearrange("p (j s) -> p j s", s=32)
        shifts = reg(28 * K1, (POS + PG) * P)
        shift_x = shifts[:, 0:POS * P].rearrange("p (q m) -> p q m", q=POS)
        shift_y = shifts[:, POS * P:(POS + PG) * P].rearrange("p (g m) -> p g m", g=PG)
        blur = chunks(12 * K1)
        xn3 = chunks(16 * K1)
        q3 = reg(19 * K1, 2 * K1).rearrange("p (c l) -> p c l", c=2)
        k3 = reg(21 * K1, 2 * K1).rearrange("p (c l) -> p c l", c=2)
        vT3 = blocks(23 * K1)
        prob3 = [reg(i * K1, K1) for i in range(2)]
        prT3 = [reg((28 + 4 * i) * K1, 4 * K1).rearrange("p (b q) -> p b q", b=LB) for i in range(2)]
        y3 = chunks(3 * K1)
        wg3 = weights(6 * K1, C)
        at3 = 28 * K1 + (POS + PG) * P
        wq3, wk3 = weights(at3, QK3), weights(at3 + NC * QK3, QK3)
        wv3, wp3 = weights(at3 + 2 * NC * QK3, C), weights(at3 + NC * (2 * QK3 + C), C)
        wse1 = weights(at3 + NC * (2 * QK3 + 2 * C), SE)
        at3 += NC * (2 * QK3 + 2 * C + SE)
        wse2 = R_[0:SE, at3:at3 + C]
        negmax, rowsum, rowinv = (gn_t[:, i:i + 8] for i in (64, 72, 80))
        qb = derived[:, 0:3]
        dsum = derived[:, 3:6]
        inv3 = derived[:, 6:9]
        cst3 = derived[:, 9:12]
        qb3 = derived[:, 12:14]
        tmp_d = derived[:, 14:20]

        c_in = sem("consts_loaded", 0)
        pre_v = sem("pre_vector", 0)
        pre_a = sem("pre_scalar", 0)
        pre_g = sem("pre_gpsimd", 0)
        pre_st = sem("shift_x_stored", 0)
        xa_in = sem("x_loaded_for_attention", 16)
        xb_in = sem("x_loaded_for_gate", 16)
        xr_in = sem("x_loaded_as_residual", 16)
        wa_in = sem("qkv_weights_loaded", 16)
        wb_in = sem("gate_weights_loaded", 32)
        wd_in = sem("dt_weights_loaded", 16 * K)
        ws_in = sem("shifts_loaded", 16)
        w3_in = sem("layer3_weights_loaded", 96)
        g0_stat = sem("gn0_stats", 1)
        g0_mean = sem("gn0_group_mean", 1)
        g0_dev = sem("gn0_deviation", 1)
        g0_var = sem("gn0_group_var", 1)
        g0_eps = sem("gn0_var_eps", 1)
        g0_rstd = sem("gn0_rstd", 1)
        g0_out = sem("gn0_normalized", 1)
        g0_again = sem("gn0_normalized_again", 1)
        gn_stat = sem("gn_stats", 3)
        gn_mean = sem("gn_group_mean", 3)
        gn_dev = sem("gn_deviation", 3)
        gn_var = sem("gn_group_var", 3)
        gn_eps = sem("gn_var_eps", 3)
        gn_rstd = sem("gn_rstd", 3)
        gn_out = sem("gn_normalized", 3)
        qk_ps = sem("qk_projected", 6)
        qk_sb = sem("qk_evacuated", 6)
        vt_ps = sem("vT_projected", LB)
        vt_sb = sem("vT_evacuated", LB)
        s_ps = sem("scores_ready", STEPS0)
        s_max = sem("rowmax_ready", STEPS0)
        s_exp = sem("probs_ready", STEPS0)
        t_ps = sem("probsT_in_psum", STEPS0)
        t_sb = sem("probsT_ready", STEPS0)
        pv_ps = sem("head_out_in_psum", STEPS0)
        o_sb = sem("head_out_ready", STEPS0)
        vo_ps = sem("v_and_gate_projected", 2 * NC)
        vo_sb = sem("v_and_gate_evacuated", 2 * NC)
        hT_ps = sem("heads_transposed", NC)
        r_sb = sem("gated_result_ready", NC)
        p0_ps = sem("proj0_in_psum", NC)
        x1 = sem("x1_ready", NC)
        xd_ps = sem("xproj_in_psum", 2 * K)
        xd_sb = sem("xproj_evacuated", 2 * K)
        bc_st = sem("bc_rows_stored", 32 * K)
        bc_ld = [sem(f"bc_rows_loaded{i}", 16 * len(range(i, K * N, SLOTS))) for i in range(SLOTS)]
        dt_ps = sem("dt_in_psum", 2 * K * NC)
        dt_rel = sem("dt_relu_ready", 2 * K * NC)
        dt_abs = sem("dt_abs_read", 2 * K * NC)
        dt_ln = sem("dt_log_ready", K * NC)
        dt_sum = sem("dt_ready", K * NC)
        dt_sb = sem("dt_times_u_ready", K * NC)
        mg_ps = sem("column_sum_turned_back", NC)
        mg_sb = sem("column_sum_reordered", NC)
        mg_tp = sem("column_sum_turned", NC)
        mg_y = sem("column_sum_in_ysum", NC)
        a_sb = sem("decay_ready", STEPS1)
        b_sb = sem("drive_ready", STEPS1)
        h_sb = sem("state_ready", STEPS1)
        hc_sb = sem("state_times_c_ready", STEPS1)
        y_ps = sem("y_transposed", STEPS1)
        y_sb = sem("y_added", STEPS1 // GN_)
        ln_st = sem("ln_stats", 1)
        ln_r = sem("ln_rstd", 1)
        ln_o = sem("ln_normalized", 1)
        lt_ps = sem("ln_transposed", NC)
        g_sb = sem("gelu_ready", NC)
        x2 = sem("x2_ready", NC)
        s2_st = sem("xn2_stored", 16)
        s2_ld = sem("rows2_loaded", 64)
        m2_ps = sem("rows_shifted", 6)
        m2_sb = sem("rows_shifted_evacuated", 6)
        o2_ps = sem("cols_shifted", 6)
        o2_sb = sem("cols_shifted_evacuated", 6)
        o2_st = sem("blur_stored", 64)
        b2_ld = sem("blur_loaded", 16)
        x3 = sem("x3_ready", 1)
        p3_ps = sem("qk3_in_psum", 4)
        p3_sb = sem("qk3_evacuated", 4)
        v3_ps = sem("vT3_in_psum", LB)
        v3_sb = sem("vT3_evacuated", LB)
        s3_ps = sem("scores3_ready", LB)
        s3_mx = sem("rowmax3_ready", LB)
        s3_ex = sem("probs3_ready", LB)
        s3_nm = sem("probs3_normalized", LB)
        s3_tp = sem("probs3T_in_psum", LB)
        s3_ts = sem("probs3T_ready", LB)
        y3_ps = sem("y3_in_psum", 2 * NC)
        y3_sb = sem("y3_evacuated", 2 * NC)
        se_pool = sem("pooled_ready", 1)
        se_h = sem("se_hidden_in_psum", 1)
        se_hr = sem("se_hidden_ready", 1)
        se_z = sem("se_logits_in_psum", 1)
        se_zb = sem("se_logits_ready", 1)
        se_e = sem("se_exp_ready", 1)
        se_w = sem("gated_weights_ready", 1)
        f_ps = sem("proj3_in_psum", NC)
        f_sb = sem("out_ready", NC)
        out_st = sem("out_stored", 16)

        bc_d = t["bc_scratch"]
        sx_d = t["shift_scratch"]
        s2_d = t["rows_scratch"]
        o2_d = t["blur_scratch"]

        block = ctx.enter_context(nc.Block())
        def img3(a, img):
            return a[img].rearrange("(c p) l -> p c l", p=P)

        def transposed(ap):
            return ap.rearrange("p (h w) -> p w h", w=WW)

        @block.sync
        def _(sp):
            for s in signals:
                sp.sem_inc(s.h, 1)
            for name, dst in [("ident", ident[:, :]), ("group_avg", group_avg[:, :]), ("vecs", vecs[:, :]),
                              ("vec96", vec96[0:QC3, :]), ("lepe_w", lepe_w[:, :]), ("A_logs", negA[:, :]),
                              ("w_xproj", w_xproj[:, :]),
                              ("row_index", R_[:, 0:1]), ("col_row", R_[:, 32:64])]:
                sp.dma_start(dst, t[name]).then_inc(c_in.h, 16)
            with nc.allow_non_contiguous_dma(reason="48 offsets, once"):
                for q in range(4):
                    src = t["offset"][q * PG:(q + 1) * PG, :].rearrange("g d -> (g d)")
                    sp.dma_start(R_[32 * q:32 * q + 32, 64:64 + 2 * PG],
                                 src[None, :].to_broadcast([32, 2 * PG])).then_inc(c_in.h, 16)
                src = t["offset"].rearrange("g d -> (g d)")
                sp.dma_start(R_[:, 96:96 + 2 * POS], src[None, :].to_broadcast([P, 2 * POS])).then_inc(c_in.h, 16)
            sp.wait_ge(pre_v.h, 2)
            sp.dma_start(sx_d, shifts).then_inc(pre_st.h, 16)
            sp.wait_ge(pre_st.h, 16)


            def before_attention(img):
                sp.wait_ge(x1.h, x1.at(img, 0))
                sp.dma_start(xn0, img3(t["x"], img)).then_inc(xa_in.h, 16)
                sp.dma_start(w0a, t["w_qkvo"][:, :, 0:3 * C]).then_inc(wa_in.h, 16)

            def scans(img):
                for k in range(K):
                    at = 64 * (k % 2)
                    sp.wait_ge(dt_ps.h, dt_ps.at(img, 2 * NC * max(k - 1, 0)))
                    sp.dma_start(w_dt[at + 32:at + 32 + R, :], t["w_dt"][:, k * C:(k + 1) * C]).then_inc(wd_in.h, 16)
                    sp.wait_ge(xd_sb.h, xd_sb.at(img, 2 * k + 2))
                    sp.dma_start(bc_d[k, 0:N], xdbl[at:at + N, :]).then_inc(bc_st.h, 16)
                    if k:
                        sp.wait_ge(hc_sb.h, hc_sb.at(img, slot_used(k * N - SLOTS)))
                    sp.dma_start(bc_d[k, N:], xdbl[at + N:at + 2 * N, :]).then_inc(bc_st.h, 16)
                    sp.wait_ge(bc_st.h, bc_st.at(img, 32 * (k + 1)))
                    for n in range(N):
                        i = k * N + n
                        if i >= SLOTS and n:
                            sp.wait_ge(hc_sb.h, hc_sb.at(img, slot_used(i - SLOTS)))
                        rows = bc_d[k].rearrange("(t n) l -> n t l", t=2)[n]
                        sp.dma_start(bc[i % SLOTS], rows[None, :, :].to_broadcast([P, 2, L])).then_inc(bc_ld[i % SLOTS].h, 16)

            def after_scans(img):
                sp.wait_ge(hc_sb.h, hc_sb.at(img, STEPS1))
                sp.dma_start(shifts, sx_d).then_inc(ws_in.h, 16)
                for name, dst in [("wq3", wq3), ("wk3", wk3), ("wv3", wv3), ("wp3", wp3), ("wse1", wse1), ("wse2", wse2)]:
                    sp.dma_start(dst, t[name]).then_inc(w3_in.h, 16)
                sp.wait_ge(gn_out.h, gn_out.at(img, 2))
                sp.dma_start(s2_d.rearrange("(c p) l -> p c l", p=P), xn2).then_inc(s2_st.h, 16)
                sp.wait_ge(s2_st.h, s2_st.at(img, 16))
                quads = s2_d.rearrange("(q j) (y x) -> q y j x", q=4, x=WW)
                for q in range(4):
                    sp.dma_start(rows2[32 * q:32 * q + 32, :, :], quads[q]).then_inc(s2_ld.h, 16)
                sp.wait_ge(o2_sb.h, o2_sb.at(img, 6))
                quads = o2_d.rearrange("(q j) (y x) -> q y j x", q=4, x=WW)
                for q in range(4):
                    sp.dma_start(quads[q], out2[32 * q:32 * q + 32, :, :]).then_inc(o2_st.h, 16)
                sp.wait_ge(o2_st.h, o2_st.at(img, 64))
                sp.dma_start(blur, o2_d.rearrange("(c p) l -> p c l", p=P)).then_inc(b2_ld.h, 16)

            def store_out(img):
                sp.wait_ge(f_sb.h, f_sb.at(img, NC))
                sp.dma_start(img3(t["out"], img), X3).then_inc(out_st.h, 16)

            def load_gate(img):
                sp.dma_start(w0b, t["w_qkvo"][:, :, 2 * C:4 * C]).then_inc(wb_in.h, 16)
                sp.dma_start(wp0, t["w_proj0"]).then_inc(wb_in.h, 16)
                sp.dma_start(xn0, img3(t["x"], img)).then_inc(xb_in.h, 16)

            def load_residual(img):
                sp.dma_start(X3, img3(t["x"], img)).then_inc(xr_in.h, 16)

            before_attention(0)
            sp.wait_ge(pv_ps.h, pv_ps.at(0, STEPS0))
            load_gate(0)
            load_residual(0)
            with sp.Fori(0, B - 1) as img:
                before_attention(img + 1)
                scans(img)
                after_scans(img)
                sp.wait_ge(v3_ps.h, v3_ps.at(img, LB))
                load_gate(img + 1)
                store_out(img)
                sp.wait_ge(out_st.h, out_st.at(img, 16))
                load_residual(img + 1)
            scans(B - 1)
            after_scans(B - 1)
            store_out(B - 1)
            sp.wait_ge(out_st.h, out_st.at(B - 1, 16))

        @block.tensor
        def _(pe):
            def group_mean(src, col):
                for m in range(NC):
                    near = [a for a in range(NC) if abs(a - m) < 2]
                    for a in near:
                        mm = pe.matmul(ps[:, 7, col + m:col + m + 1], ga[:, a, m, :], src[:, a:a + 1],
                                       start=a == near[0], stop=a == near[-1])
                return mm

            def group_norm(img, g):
                pe.wait_ge(gn_stat.h, gn_stat.at(img, g + 1))
                group_mean(gn_t[:, 0:3], 0).then_inc(gn_mean.h, 1)
                pe.wait_ge(gn_dev.h, gn_dev.at(img, g + 1))
                group_mean(gn_t[:, 16:19], 8).then_inc(gn_var.h, 1)

            def project(dst, lhs, rhs, parts=P):
                for hf in range(2):
                    for c in range(NC):
                        mm = pe.matmul(dst[0:parts, hf * HALF:(hf + 1) * HALF], lhs[:, c], rhs(c, hf),
                                       start=c == 0, stop=c == NC - 1)
                return mm

            def rows_of(x):
                return lambda c, hf: x[:, c, hf * HALF:(hf + 1) * HALF]

            def turn_blocks(bank, src):
                for b in range(LB):
                    mm = pe.matmul(ps[:, bank + b // 4, (b % 4) * P:(b % 4 + 1) * P], src(b), ident[:, :],
                                   start=True, stop=True, is_transpose=True)
                return mm

            def before_attention(img):
                pe.wait_ge(g0_stat.h, g0_stat.at(img, 1))
                group_mean(gn0_t[:, 0:3], 0).then_inc(g0_mean.h, 1)
                pe.wait_ge(g0_dev.h, g0_dev.at(img, 1))
                group_mean(gn0_t[:, 16:19], 8).then_inc(g0_var.h, 1)
                pe.wait_ge(g0_out.h, g0_out.at(img, 1))
                pe.wait_ge(wa_in.h, wa_in.at(img, 16))
                for i in range(6):
                    if i >= 2:
                        pe.wait_ge(qk_sb.h, qk_sb.at(img, i - 1))
                    project(banks(2 * (i % 2)), w0a[:, :, i * P:(i + 1) * P], rows_of(xn0)).then_inc(qk_ps.h, 1)
                for b in range(LB):
                    if b >= 2:
                        pe.wait_ge(vt_sb.h, vt_sb.at(img, b - 1))
                    for c in range(NC):
                        mm = pe.matmul(ps[:, 4 + b % 2, 0:C], xn0[:, c, b * P:(b + 1) * P], w0a[:, c, 2 * C:3 * C],
                                       start=c == 0, stop=c == NC - 1)
                    mm.then_inc(vt_ps.h, 1)

            def attention(img, a):
                if a == 0:
                    pe.wait_ge(qk_sb.h, qk_sb.at(img, 6))
                    pe.wait_ge(vt_sb.h, vt_sb.at(img, LB))
                if a < STEPS0:
                    h, qc = a // LB, a % LB
                    row = 32 * (h % 4)
                    if a:
                        pe.wait_ge(s_exp.h, s_exp.at(img, a))
                    for hf in range(2):
                        mm = pe.matmul(ps[:, hf, :], q4[row:row + HD, h // 4, qc * P:(qc + 1) * P],
                                       k4[row:row + HD, h // 4, hf * HALF:(hf + 1) * HALF], start=True, stop=True)
                    mm.then_inc(s_ps.h, 1)
                if 1 <= a <= STEPS0:
                    u = a - 1
                    pe.wait_ge(s_exp.h, s_exp.at(img, u + 1))
                    if u >= 1:
                        pe.wait_ge(t_sb.h, t_sb.at(img, u))
                    turn_blocks(2, lambda b: probs[u % 2][:, b * P:(b + 1) * P]).then_inc(t_ps.h, 1)
                if 2 <= a <= STEPS0 + 1:
                    u = a - 2
                    h = u // LB
                    pe.wait_ge(t_sb.h, t_sb.at(img, u + 1))
                    if u >= 1:
                        pe.wait_ge(o_sb.h, o_sb.at(img, u))
                    for b in range(LB):
                        mm = pe.matmul(ps[:, 6, 0:HD], probsT[u % 2][:, b, :], vT[:, b, HD * h:HD * h + HD],
                                       start=b == 0, stop=b == LB - 1)
                    mm.then_inc(pv_ps.h, 1)

            def after_attention(img):
                pe.wait_ge(g0_again.h, g0_again.at(img, 1))
                pe.wait_ge(wb_in.h, wb_in.at(img, 32))
                pe.wait_ge(o_sb.h, o_sb.at(img, STEPS0))
                for m in range(NC):
                    if m:
                        pe.wait_ge(vo_sb.h, vo_sb.at(img, 2 * m))
                    project(banks(0), w0b[:, :, m * P:(m + 1) * P], rows_of(xn0)).then_inc(vo_ps.h, 1)
                    project(banks(2), w0b[:, :, C + m * P:C + (m + 1) * P], rows_of(xn0)).then_inc(vo_ps.h, 1)
                    if m:
                        pe.wait_ge(r_sb.h, r_sb.at(img, m))
                    turn_blocks(4, lambda b: heads[:, b, m * P:(m + 1) * P]).then_inc(hT_ps.h, 1)
                pe.wait_ge(r_sb.h, r_sb.at(img, NC))
                for m in range(NC):
                    if m == 2:
                        pe.wait_ge(x1.h, x1.at(img, 1))
                    project(banks(2 * (m % 2)), wp0[:, :, m * P:(m + 1) * P], rows_of(res)).then_inc(p0_ps.h, 1)

            wx = w_xproj[:, :].rearrange("p (c k r) -> p c k r", c=NC, k=K)

            def scan(img, kind, k, u=0):
                if kind in "xdlt":
                    cols, back = DIRS[k]
                if kind in "sym":
                    u = k
                if kind == "m":
                    c = u
                    pe.wait_ge(y_sb.h, y_sb.at(img, STEPS1 // 2 // GN_ - NC + c + 1))
                    turn_blocks(4, lambda b: ysum[:, b, c * P:(c + 1) * P]).then_inc(mg_ps.h, 1)
                    pe.wait_ge(mg_sb.h, mg_sb.at(img, c + 1))
                    turn_blocks(4, lambda b: turned[:, b * P:(b + 1) * P]).then_inc(mg_tp.h, 1)
                if kind == "x":
                    if k == 0 and u == 0:
                        pe.wait_ge(gn_out.h, gn_out.at(img, 1))
                    if u:
                        pe.wait_ge(xd_sb.h, xd_sb.at(img, 2 * k + 1))
                    elif k:
                        pe.wait_ge(dt_abs.h, dt_abs.at(img, 2 * NC * k))
                    for c in range(NC):
                        rhs = U[:, c, :]
                        rhs = transposed(rhs)[:, u * 16:u * 16 + 16, :] if cols else rhs[:, u * HALF:(u + 1) * HALF]
                        mm = pe.matmul(ps[0:XR, 7, :], wx[:, c, cols + 2 * back, :], rhs, start=c == 0, stop=c == NC - 1)
                    mm.then_inc(xd_ps.h, 1)
                if kind == "d":
                    c, hf = u // 2, u % 2
                    at = 64 * (k % 2) + 32
                    if u == 0:
                        pe.wait_ge(xd_sb.h, xd_sb.at(img, 2 * k + 2))
                        pe.wait_ge(wd_in.h, wd_in.at(img, 16 * (k + 1)))
                    else:
                        pe.wait_ge(dt_abs.h, dt_abs.at(img, 2 * NC * k + u))
                    pe.matmul(ps[:, 7, :], w_dt[at:at + R, c * P:(c + 1) * P], xdbl[at:at + R, hf * HALF:(hf + 1) * HALF],
                              start=True, stop=True).then_inc(dt_ps.h, 1)
                if kind == "s" and u >= LAG:
                    i = u - LAG
                    pe.wait_ge(hc_sb.h, hc_sb.at(img, i + 1))
                    if i % GN_ == 0:
                        if i == 0:
                            pe.wait_ge(gn_out.h, gn_out.at(img, 1))
                        elif 0 <= i // GN_ - (STEPS1 // 2 // GN_ - NC + 1) < NC:
                            pe.wait_ge(mg_y.h, mg_y.at(img, i // GN_ - (STEPS1 // 2 // GN_ - NC)))
                        else:
                            pe.wait_ge(y_sb.h, y_sb.at(img, i // GN_))
                    for b in range(LB):
                        mm = pe.matmul(ps[:, 4 + b // 4, (b % 4) * P:(b % 4 + 1) * P],
                                       state[i % 4][:, b * P:(b + 1) * P], ident[:, :],
                                       start=i % GN_ == 0 and b % 4 == 0, stop=i % GN_ == GN_ - 1,
                                       is_transpose=True, skip_group_check=True)
                    mm.then_inc(y_ps.h, 1)

            def layers_1_to_3(img):
                pe.wait_ge(ln_o.h, ln_o.at(img, 1))
                for c in range(NC):
                    if c == 2:
                        pe.wait_ge(g_sb.h, g_sb.at(img, 1))
                    for b in range(LB):
                        mm = pe.matmul(ps[:, 2 * (c % 2) + b // 4, (b % 4) * P:(b % 4 + 1) * P],
                                       ysum[:, b, c * P:(c + 1) * P], ident[:, :], start=True, stop=True,
                                       is_transpose=True)
                    mm.then_inc(lt_ps.h, 1)


                group_norm(img, 1)
                pe.wait_ge(s2_ld.h, s2_ld.at(img, 64))
                pe.wait_ge(ws_in.h, ws_in.at(img, 16))
                for r in range(6):
                    if r >= 2:
                        pe.wait_ge(m2_sb.h, m2_sb.at(img, r - 1))
                    for j in range(4):
                        gh = 4 * r + j
                        mm = pe.matmul(ps[:, r % 2, j * P:(j + 1) * P], rows2[:, 4 * gh:4 * gh + 4, :], shift_y[:, gh // 2, :],
                                       start=True, stop=True)
                    mm.then_inc(m2_ps.h, 1)
                for r in range(6):
                    pe.wait_ge(m2_sb.h, m2_sb.at(img, r + 1))
                    if r >= 2:
                        pe.wait_ge(o2_sb.h, o2_sb.at(img, r - 1))
                    for j in range(4):
                        gh = 4 * r + j
                        for q in range(4):
                            mm = pe.matmul(ps[32 * q:32 * q + 32, 2 + r % 2, j * P:(j + 1) * P],
                                           mid2[:, gh, 32 * q:32 * q + 32], shift_x[:, q * PG + gh // 2, :],
                                           start=True, stop=True)
                    mm.then_inc(o2_ps.h, 1)

                group_norm(img, 2)
                pe.wait_ge(gn_out.h, gn_out.at(img, 3))
                pe.wait_ge(w3_in.h, w3_in.at(img, 96))
                for i in range(4):
                    if i >= 2:
                        pe.wait_ge(p3_sb.h, p3_sb.at(img, i - 1))
                    w = (wq3, wk3)[i // 2]
                    project(banks(2 * (i % 2)), w[:, :, (i % 2) * QC3:(i % 2 + 1) * QC3], rows_of(xn3), QC3)\
                        .then_inc(p3_ps.h, 1)
                for b in range(LB):
                    if b >= 2:
                        pe.wait_ge(v3_sb.h, v3_sb.at(img, b - 1))
                    for c in range(NC):
                        mm = pe.matmul(ps[:, 4 + b % 2, 0:C], xn3[:, c, b * P:(b + 1) * P], wv3[:, c, :],
                                       start=c == 0, stop=c == NC - 1)
                    mm.then_inc(v3_ps.h, 1)
                pe.wait_ge(p3_sb.h, p3_sb.at(img, 4))
                pe.wait_ge(v3_sb.h, v3_sb.at(img, LB))

                def scores3(u):
                    if u >= 2:
                        pe.wait_ge(s3_ex.h, s3_ex.at(img, u - 1))
                    for hf in range(2):
                        for a in range(2):
                            mm = pe.matmul(ps[:, 2 * (u % 2) + hf, :], q3[0:QC3, a, u * P:(u + 1) * P],
                                           k3[0:QC3, a, hf * HALF:(hf + 1) * HALF], start=a == 0, stop=a == 1)
                    mm.then_inc(s3_ps.h, 1)

                def turn3(u):
                    pe.wait_ge(s3_nm.h, s3_nm.at(img, u + 1))
                    if u:
                        pe.wait_ge(s3_ts.h, s3_ts.at(img, u))
                    for b in range(LB):
                        mm = pe.matmul(ps[:, 4 + b // 4, (b % 4) * P:(b % 4 + 1) * P],
                                       prob3[u % 2][:, b * P:(b + 1) * P], ident[:, :],
                                       start=True, stop=True, is_transpose=True)
                    mm.then_inc(s3_tp.h, 1)

                def values3(hf):
                    pe.wait_ge(s3_ts.h, s3_ts.at(img, 4 * hf + 4))
                    for m in range(NC):
                        i = hf * NC + m
                        if i >= 2:
                            pe.wait_ge(y3_sb.h, y3_sb.at(img, i - 1))
                        for b in range(LB):
                            mm = pe.matmul(ps[:, 6 + i % 2, :], vT3[:, b, m * P:(m + 1) * P], prT3[hf][:, b, :],
                                           start=b == 0, stop=b == LB - 1)
                        mm.then_inc(y3_ps.h, 1)

                for u in range(LB + 1):
                    if u < LB:
                        scores3(u)
                    if u >= 1:
                        turn3(u - 1)
                    if u == 5:
                        values3(0)
                values3(1)
                pe.wait_ge(se_pool.h, se_pool.at(img, 1))
                for c in range(NC):
                    mm = pe.matmul(ps[0:SE, 0, 0:1], wse1[:, c, :], se_t[:, 8 + c:9 + c], start=c == 0, stop=c == NC - 1)
                mm.then_inc(se_h.h, 1)
                pe.wait_ge(se_hr.h, se_hr.at(img, 1))
                for c in range(NC):
                    mm = pe.matmul(ps[:, 1, c:c + 1], wse2[:, c * P:(c + 1) * P], se_t[0:SE, 12:13], start=True, stop=True)
                mm.then_inc(se_z.h, 1)
                pe.wait_ge(se_w.h, se_w.at(img, 1))
                pe.wait_ge(y3_sb.h, y3_sb.at(img, 2 * NC))
                for m in range(NC):
                    if m == 2:
                        pe.wait_ge(f_sb.h, f_sb.at(img, 1))
                    project(banks(2 * (m % 2)), wg3[:, :, m * P:(m + 1) * P], rows_of(y3)).then_inc(f_ps.h, 1)


            pe.wait_ge(c_in.h, 16 * 14)
            before_attention(0)
            for ev in schedule(True, False):
                attention(0, ev[1])
            after_attention(0)
            with pe.Fori(0, B - 1) as img:
                before_attention(img + 1)
                group_norm(img, 0)
                for ev in schedule(True, True):
                    if ev[0] == "a":
                        attention(img + 1, ev[1])
                    else:
                        scan(img, *ev)
                layers_1_to_3(img)
                after_attention(img + 1)
            group_norm(B - 1, 0)
            for ev in schedule(False, True):
                scan(B - 1, *ev)
            layers_1_to_3(B - 1)

        @block.scalar
        def _(act):
            act.wait_ge(c_in.h, 16 * 14)
            act.activation(negA[:, :], negA[:, :], ACT.Exp).then_inc(pre_a.h, 1)
            act.wait_ge(pre_v.h, 1)
            for which, n in enumerate((PG, POS)):
                at = 1024 + which * 8192
                for lo, wide in [(at, n * 32)] + [(at + 2048 + 64 * j, n) for j in range(5)]:
                    act.activation(R_[:, lo:lo + wide], R_[:, lo:lo + wide], ACT.Exp, scale=-2.0).then_inc(pre_a.h, 1)
            act.wait_ge(pre_v.h, 3)

            def before_attention(img):
                for i in range(6):
                    act.wait_ge(qk_ps.h, qk_ps.at(img, i + 1))
                    if i < 3:
                        act.activation(q4[:, i, :], banks(2 * (i % 2)), ACT.Identity, bias=qb[:, i:i + 1], scale=SC0)\
                            .then_inc(qk_sb.h, 1)
                    else:
                        act.activation(k4[:, i - 3, :], banks(2 * (i % 2)), ACT.Identity, bias=vec("bk", i - 3))\
                            .then_inc(qk_sb.h, 1)

            def attention(img, a):
                if a < STEPS0:
                    act.wait_ge(s_max.h, s_max.at(img, a + 1))
                    if a >= 2:
                        act.wait_ge(t_ps.h, t_ps.at(img, a - 1))
                    act.activation(probs[a % 2], banks(0), ACT.Exp, bias=negmax[:, a % 8:a % 8 + 1],
                                   accum_out=rowsum[:, a % 8:a % 8 + 1]).then_inc(s_exp.h, 1)
                if 1 <= a <= STEPS0:
                    u = a - 1
                    act.wait_ge(t_ps.h, t_ps.at(img, u + 1))
                    if u >= 2:
                        act.wait_ge(pv_ps.h, pv_ps.at(img, u - 1))
                    act.activation(probsT[u % 2].rearrange("p b q -> p (b q)"), banks(2), ACT.Copy)\
                        .then_inc(t_sb.h, 1)

            def after_attention(img):
                act.wait_ge(g0_again.h, g0_again.at(img, 1))
                for m in range(NC):
                    act.wait_ge(vo_ps.h, vo_ps.at(img, 2 * m + 1))
                    if m:
                        act.wait_ge(r_sb.h, r_sb.at(img, m))
                    inner = vpad.rearrange("p (h w) -> p h w", w=36)[:, 2:34, 2:34]
                    act.activation(inner, banks(0).rearrange("p (h w) -> p h w", w=WW), ACT.Identity, bias=vec("bv", m))\
                        .then_inc(vo_sb.h, 1)
                    act.wait_ge(vo_ps.h, vo_ps.at(img, 2 * m + 2))
                    act.activation(gate0, banks(2), ACT.Identity, bias=vec("bo", m)).then_inc(vo_sb.h, 1)

            def scan(img, kind, k, u=0):
                if kind in "xdlt":
                    cols, back = DIRS[k]
                if kind in "sym":
                    u = k
                if kind == "x":
                    act.wait_ge(xd_ps.h, xd_ps.at(img, 2 * k + u + 1))
                    at = 64 * (k % 2)
                    if k >= 2 and u == 0:
                        act.wait_ge(bc_st.h, bc_st.at(img, 32 * (k - 1)))
                    act.activation(xdbl[at:at + XR, u * HALF:(u + 1) * HALF], ps[0:XR, 7, :], ACT.Copy).then_inc(xd_sb.h, 1)
                if kind == "d":
                    c, hf = u // 2, u % 2
                    part = dtu[:, c, hf * HALF:(hf + 1) * HALF]
                    act.wait_ge(dt_rel.h, dt_rel.at(img, 2 * NC * k + u + 1))
                    act.activation(part, ps[:, 7, :], ACT.Abs, bias=vec(f"dtb{cols + 2 * back}", c)).then_inc(dt_abs.h, 1)
                    act.drain()
                    act.activation(part, part, ACT.Exp, scale=-1.0)
                if kind == "l":
                    act.drain()
                    act.activation(dtu[:, u, :], dtu[:, u, :], ACT.Ln, bias=1.0).then_inc(dt_ln.h, 1)
                if kind == "s" and u < STEPS1:
                    i, k, c, n = place(u)
                    cols, back = DIRS[k]
                    if n == 0:
                        act.wait_ge(dt_sum.h, dt_sum.at(img, k * NC + c + 1))
                    if i >= 2:
                        act.wait_ge(h_sb.h, h_sb.at(img, i - 1))
                    elif i == 0:
                        act.wait_ge(gn_out.h, gn_out.at(img, 1))
                    col = (cols + 2 * back) * NC * N + c * N + n
                    act.activation(decay[i % 2], dt[:, c, :], ACT.Exp, scale=negA[:, col:col + 1]).then_inc(a_sb.h, 1)

            def layers_1_to_3(img):
                for c in range(NC):
                    act.wait_ge(lt_ps.h, lt_ps.at(img, c + 1))
                    if c == 2:
                        act.wait_ge(x2.h, x2.at(img, 1))
                    act.activation(gel[c % 2], banks(2 * (c % 2)), ACT.Gelu, bias=vec("ln_b", c), scale=vec("ln_w", c))\
                        .then_inc(g_sb.h, 1)
                for r in range(6):
                    act.wait_ge(m2_ps.h, m2_ps.at(img, r + 1))
                    act.activation(mid2[:, 4 * r:4 * r + 4, :].rearrange("p a m -> p (a m)"), ps[:, r % 2, :], ACT.Copy)\
                        .then_inc(m2_sb.h, 1)
                for i in range(4):
                    act.wait_ge(p3_ps.h, p3_ps.at(img, i + 1))
                    if i < 2:
                        act.activation(q3[0:QC3, i, :], banks(2 * (i % 2))[0:QC3, :], ACT.Identity,
                                       bias=qb3[0:QC3, i:i + 1], scale=SC3).then_inc(p3_sb.h, 1)
                    else:
                        act.activation(k3[0:QC3, i - 2, :], banks(2 * (i % 2))[0:QC3, :], ACT.Identity,
                                       bias=vec96[0:QC3, i:i + 1]).then_inc(p3_sb.h, 1)

                def exps3(u):
                    act.wait_ge(s3_mx.h, s3_mx.at(img, u + 1))
                    if u >= 2:
                        act.wait_ge(s3_tp.h, s3_tp.at(img, u - 1))
                    act.activation(prob3[u % 2], banks(2 * (u % 2)), ACT.Exp, bias=se_t[:, 16 + u:17 + u],
                                   accum_out=se_t[:, 24 + u:25 + u]).then_inc(s3_ex.h, 1)

                def turned3(u):
                    act.wait_ge(s3_tp.h, s3_tp.at(img, u + 1))
                    hf, j = u // 4, u % 4
                    act.activation(prT3[hf][:, :, j * P:(j + 1) * P], banks(4).rearrange("p (b q) -> p b q", b=LB),
                                   ACT.Copy).then_inc(s3_ts.h, 1)

                def values3(hf):
                    for m in range(NC):
                        i = hf * NC + m
                        act.wait_ge(y3_ps.h, y3_ps.at(img, i + 1))
                        act.activation(y3[:, m, hf * HALF:(hf + 1) * HALF], ps[:, 6 + i % 2, :], ACT.Identity,
                                       bias=vec("bv3", m), accum_out=se_t[:, i:i + 1]).then_inc(y3_sb.h, 1)

                for u in range(LB + 1):
                    if u < LB:
                        exps3(u)
                    if u >= 1:
                        turned3(u - 1)
                    if u == 5:
                        values3(0)
                values3(1)
                act.wait_ge(se_zb.h, se_zb.at(img, 1))
                act.activation(se_t[:, 36:39], se_t[:, 33:36], ACT.Exp, scale=-1.0).then_inc(se_e.h, 1)

            before_attention(0)
            for ev in schedule(True, False):
                attention(0, ev[1])
            after_attention(0)
            with act.Fori(0, B - 1) as img:
                before_attention(img + 1)
                for ev in schedule(True, True):
                    if ev[0] == "a":
                        attention(img + 1, ev[1])
                    else:
                        scan(img, *ev)
                layers_1_to_3(img)
                after_attention(img + 1)
            for ev in schedule(False, True):
                scan(B - 1, *ev)
            layers_1_to_3(B - 1)

        @block.gpsimd
        def _(pool):
            pool.memset(half_neg[:, :], -0.5).then_inc(pre_g.h, 1)
            pool.wait_ge(pre_g.h, 1)
            pool.wait_ge(pre_v.h, 3)
            pool.tensor_tensor(inv3, tmp_d[:, 0:3], half_neg[:, 0:3], ALU.pow).then_inc(pre_g.h, 1)

            def before_attention(img):
                pool.wait_ge(g0_eps.h, g0_eps.at(img, 1))
                pool.tensor_tensor(gn0_t[:, 32:35], gn0_t[:, 24:27], half_neg[:, 0:3], ALU.pow).then_inc(g0_rstd.h, 1)

            def group_norm(img, g):
                pool.wait_ge(gn_eps.h, gn_eps.at(img, g + 1))
                pool.tensor_tensor(gn_t[:, 32:35], gn_t[:, 24:27], half_neg[:, 0:3], ALU.pow).then_inc(gn_rstd.h, 1)

            def scan(img, kind, k, u=0):
                if kind in "xdlt":
                    cols, back = DIRS[k]
                if kind in "sym":
                    u = k
                if kind == "t":
                    c = u
                    pool.wait_ge(dt_sum.h, dt_sum.at(img, k * NC + c + 1))
                    u_in, d_in, d_out = U[:, c, :], dt[:, c, :], dtu[:, c, :]
                    if cols:
                        u_in = transposed(u_in)
                        d_in, d_out = (a.rearrange("p (w h) -> p w h", h=HH) for a in (d_in, d_out))
                    pool.tensor_tensor(d_out, d_in, u_in, ALU.mult).then_inc(dt_sb.h, 1)
                if kind == "s" and 1 <= u <= STEPS1:
                    i, k, c, n = place(u - 1)
                    pool.wait_ge(h_sb.h, h_sb.at(img, i + 1))
                    pool.tensor_tensor(state[i % 4], state[i % 4], bc[(k * N + n) % SLOTS][:, 1, :], ALU.mult)\
                        .then_inc(hc_sb.h, 1)

            def layers_1_to_3(img):
                pool.wait_ge(ln_st.h, ln_st.at(img, 1))
                pool.tensor_tensor(ln_t[:, 16:24], ln_t[:, 24:32], half_neg[:, 0:8], ALU.pow).then_inc(ln_r.h, 1)
                group_norm(img, 1)
                group_norm(img, 2)

            before_attention(0)
            with pool.Fori(0, B - 1) as img:
                before_attention(img + 1)
                group_norm(img, 0)
                for ev in schedule(False, True):
                    scan(img, *ev)
                layers_1_to_3(img)
            group_norm(B - 1, 0)
            for ev in schedule(False, True):
                scan(B - 1, *ev)
            layers_1_to_3(B - 1)

        @block.vector
        def _(v):
            v.wait_ge(c_in.h, 16 * 14)
            v.memset(shifts, 0.0)
            sidx, yrow = R_[:, 0:1], R_[:, 32:64]
            kinds = []
            for which, (n, off) in enumerate(((PG, R_[:, 64:64 + 2 * PG].rearrange("p (g d) -> p g d", d=2)[:, :, 1]),
                                              (POS, R_[:, 96:96 + 2 * POS].rearrange("p (g d) -> p g d", d=2)[:, :, 0]))):
                at = 1024 + which * 8192
                expo = R_[:, at:at + n * 32].rearrange("p (g y) -> p g y", y=32)
                band = R_[:, at + 4096:at + 4096 + n * 32].rearrange("p (g y) -> p g y", y=32)
                taps = [R_[:, at + 2048 + 64 * j:at + 2048 + 64 * j + n] for j in range(5)]
                rnd, sub, moved, keep, tot = (R_[:, at + 3072 + 64 * j:at + 3072 + 64 * j + n] for j in range(5))
                MAGIC = 12582912.0
                v.tensor_scalar(rnd, off, MAGIC, None, ALU.add)
                v.drain()
                v.tensor_scalar(rnd, rnd, MAGIC, None, ALU.subtract)
                v.drain()
                v.tensor_tensor(sub, off, rnd, ALU.subtract)
                v.drain()
                v.tensor_scalar(sub, sub, 0.5, -0.5, ALU.min, ALU.max)
                v.tensor_scalar(moved, rnd, sidx, None, ALU.add)
                v.drain()
                v.tensor_scalar(keep, moved, 0.0, None, ALU.is_ge)
                v.tensor_scalar(tot, moved, 31.0, None, ALU.is_le)
                v.drain()
                v.tensor_tensor(keep, keep, tot, ALU.mult)
                v.tensor_tensor(band, moved[:, :, None].to_broadcast([P, n, 32]),
                                yrow[:, None, :].to_broadcast([P, n, 32]), ALU.subtract)
                v.drain()
                v.tensor_tensor(expo, band, sub[:, :, None].to_broadcast([P, n, 32]), ALU.add)
                v.drain()
                v.tensor_tensor(expo, expo, expo, ALU.mult)
                v.tensor_tensor(band, band, band, ALU.mult)
                v.drain()
                v.tensor_scalar(band, band, 4.5, None, ALU.is_le)
                for j in range(5):
                    v.tensor_scalar(taps[j], sub, float(j - 2), None, ALU.add)
                v.drain()
                for j in range(5):
                    ins = v.tensor_tensor(taps[j], taps[j], taps[j], ALU.mult)
                kinds.append((n, expo, band, taps, keep, tot))
            ins.then_inc(pre_v.h, 1)
            v.wait_ge(pre_a.h, 1 + 2 * 6)
            for which, (n, expo, band, taps, keep, tot) in enumerate(kinds):
                v.tensor_tensor(tot, taps[0], taps[1], ALU.add)
                for j in range(2, 5):
                    v.drain()
                    v.tensor_tensor(tot, tot, taps[j], ALU.add)
                v.drain()
                v.reciprocal(tot, tot)
                v.drain()
                v.tensor_tensor(keep, keep, tot, ALU.mult)
                v.tensor_tensor(expo, expo, band, ALU.mult)
                v.drain()
                v.tensor_tensor(expo, expo, keep[:, :, None].to_broadcast([P, n, 32]), ALU.mult)
                v.drain()
                dst = (shifts[:, POS * P:] if which == 0 else shifts[:, 0:POS * P]).rearrange("p (g q y) -> p g q y", q=4, y=32)
                for q in range(4):
                    ins = v.tensor_copy(dst[32 * q:32 * q + 32, :, q, :], expo[32 * q:32 * q + 32, :, :])
            ins.then_inc(pre_v.h, 1)
            v.tensor_scalar(negA[:, :], negA[:, :], -1.0, None, ALU.mult)
            v.tensor_scalar(qb, vecs[:, VEC["bq"] * NC:VEC["bq"] * NC + NC], SC0, None, ALU.mult)
            v.tensor_scalar(qb3[0:QC3, :], vec96[0:QC3, 0:2], SC3, None, ALU.mult)

            def vec3(name):
                return vecs[:, VEC[name] * NC:VEC[name] * NC + NC]
            v.tensor_tensor(dsum, vec3("D0"), vec3("D1"), ALU.add)
            v.drain()
            v.tensor_tensor(dsum, dsum, vec3("D2"), ALU.add)
            v.drain()
            v.tensor_tensor(dsum, dsum, vec3("D3"), ALU.add)
            v.tensor_scalar(tmp_d[:, 0:3], vec3("var"), EPS, None, ALU.add).then_inc(pre_v.h, 1)
            v.wait_ge(pre_g.h, 2)
            v.tensor_tensor(inv3, inv3, vec3("gamma"), ALU.mult)
            v.tensor_tensor(cst3, vec3("bproj3"), vec3("mean"), ALU.subtract)
            v.drain()
            v.tensor_tensor(cst3, cst3, inv3, ALU.mult)
            v.drain()
            v.tensor_tensor(cst3, cst3, vec3("beta"), ALU.add)
            v.drain()

            def channel_stats(src, t):
                for c in range(NC):
                    for hf in range(2):
                        v.bn_stats(stats[:, c * 12 + hf * 6:c * 12 + hf * 6 + 6], src[:, c, hf * HALF:(hf + 1) * HALF])
                v.drain()
                agg = t[:, 6:12].rearrange("p (c s) -> p c s", s=2)
                for c in range(NC):
                    v.bn_aggr(agg[:, c, :], stats[:, c * 12:c * 12 + 12])
                v.drain()
                return v.tensor_copy(t[:, 0:3], agg[:, :, 0])

            def deviation(t):
                v.tensor_copy(t[:, 3:6], ps[:, 7, 0:3])
                v.drain()
                v.tensor_tensor(t[:, 12:15], t[:, 0:3], t[:, 3:6], ALU.subtract)
                v.drain()
                v.tensor_tensor(t[:, 12:15], t[:, 12:15], t[:, 12:15], ALU.mult)
                v.drain()
                return v.tensor_tensor(t[:, 16:19], t[:, 12:15], t[:, 7:12:2], ALU.add)

            def normalize(dst, src, t):
                for c in range(NC):
                    ins = v.tensor_scalar(dst[:, c, :], src[:, c, :], t[:, 3 + c:4 + c], t[:, 32 + c:33 + c],
                                          ALU.subtract, ALU.mult)
                return ins

            def group_norm(img, g, dst):
                channel_stats(X3, gn_t).then_inc(gn_stat.h, 1)
                v.wait_ge(gn_mean.h, gn_mean.at(img, g + 1))
                deviation(gn_t).then_inc(gn_dev.h, 1)
                v.wait_ge(gn_var.h, gn_var.at(img, g + 1))
                v.tensor_scalar(gn_t[:, 24:27], ps[:, 7, 8:11], EPS, None, ALU.add).then_inc(gn_eps.h, 1)
                v.wait_ge(gn_rstd.h, gn_rstd.at(img, g + 1))
                normalize(dst, X3, gn_t).then_inc(gn_out.h, 1)

            def before_attention(img):
                v.wait_ge(xa_in.h, xa_in.at(img, 16))
                channel_stats(xn0, gn0_t).then_inc(g0_stat.h, 1)
                v.wait_ge(g0_mean.h, g0_mean.at(img, 1))
                deviation(gn0_t).then_inc(g0_dev.h, 1)
                v.wait_ge(g0_var.h, g0_var.at(img, 1))
                v.tensor_scalar(gn0_t[:, 24:27], ps[:, 7, 8:11], EPS, None, ALU.add).then_inc(g0_eps.h, 1)
                v.wait_ge(g0_rstd.h, g0_rstd.at(img, 1))
                normalize(xn0, xn0, gn0_t).then_inc(g0_out.h, 1)
                for b in range(LB):
                    v.wait_ge(vt_ps.h, vt_ps.at(img, b + 1))
                    v.tensor_copy(vT[:, b, :], ps[:, 4 + b % 2, 0:C]).then_inc(vt_sb.h, 1)

            def attention(img, a):
                if a >= 3:
                    u = a - 3
                    v.wait_ge(s_exp.h, s_exp.at(img, u + 1))
                    v.reciprocal(rowinv[:, u % 8:u % 8 + 1], rowsum[:, u % 8:u % 8 + 1])
                    v.drain()
                    v.wait_ge(pv_ps.h, pv_ps.at(img, u + 1))
                    v.tensor_scalar(heads[:, u % LB, HD * (u // LB):HD * (u // LB) + HD], ps[:, 6, 0:HD],
                                    rowinv[:, u % 8:u % 8 + 1], None, ALU.mult).then_inc(o_sb.h, 1)
                if a < STEPS0:
                    v.wait_ge(s_ps.h, s_ps.at(img, a + 1))
                    v.tensor_reduce(negmax[:, a % 8:a % 8 + 1], banks(0), AX.X, ALU.max, negate=True)\
                        .then_inc(s_max.h, 1)

            def after_attention(img):
                v.memset(vpad, 0.0)
                v.wait_ge(xb_in.h, xb_in.at(img, 16))
                normalize(xn0, xn0, gn0_t).then_inc(g0_again.h, 1)
                vp = vpad.rearrange("p (h w) -> p h w", w=36)
                lep3 = lep.rearrange("p (h w) -> p h w", w=WW)
                for m in range(NC):
                    v.wait_ge(vo_sb.h, vo_sb.at(img, 2 * m + 1))
                    for j in range(25):
                        win = vp[:, j // 5:j // 5 + HH, j % 5:j % 5 + WW]
                        w = lepe_w[:, m * 25 + j:m * 25 + j + 1]
                        if j == 0:
                            v.tensor_scalar(lep3, win, w, vec("lepe_b", m), ALU.mult, ALU.add)
                        else:
                            v.drain()
                            v.scalar_tensor_tensor(lep3, win, w, lep3, ALU.mult, ALU.add)
                    v.drain()
                    v.wait_ge(hT_ps.h, hT_ps.at(img, m + 1))
                    v.scalar_tensor_tensor(lep, banks(4), vec("bv", m), lep, ALU.add, ALU.add)
                    v.drain()
                    v.wait_ge(vo_sb.h, vo_sb.at(img, 2 * m + 2))
                    v.tensor_tensor(res[:, m, :], lep, gate0, ALU.mult).then_inc(r_sb.h, 1)
                v.wait_ge(xr_in.h, xr_in.at(img, 16))
                for m in range(NC):
                    v.wait_ge(p0_ps.h, p0_ps.at(img, m + 1))
                    v.scalar_tensor_tensor(X3[:, m, :], banks(2 * (m % 2)), vec("proj_b", m), X3[:, m, :],
                                           ALU.add, ALU.add).then_inc(x1.h, 1)
                v.drain()

            def scan(img, kind, k, u=0):
                if kind in "xdlt":
                    cols, back = DIRS[k]
                if kind in "sym":
                    u = k
                if kind == "m":
                    c = u
                    v.wait_ge(mg_ps.h, mg_ps.at(img, c + 1))
                    v.scalar_tensor_tensor(turned.rearrange("p (h w) -> p h w", w=WW),
                                           U[:, c, :].rearrange("p (h w) -> p h w", w=WW), dsum[:, c:c + 1],
                                           banks(4).rearrange("p (w h) -> p h w", h=HH), ALU.mult, ALU.add)\
                        .then_inc(mg_sb.h, 1)
                    v.wait_ge(mg_tp.h, mg_tp.at(img, c + 1))
                    v.tensor_copy(ysum[:, :, c * P:(c + 1) * P], banks(4).rearrange("p (b c) -> p b c", b=LB))\
                        .then_inc(mg_y.h, 1)
                    v.drain()
                if kind == "d":
                    c, hf = u // 2, u % 2
                    v.wait_ge(dt_ps.h, dt_ps.at(img, 2 * NC * k + u + 1))
                    v.tensor_scalar(dt[:, c, hf * HALF:(hf + 1) * HALF], ps[:, 7, :], vec(f"dtb{cols + 2 * back}", c), 0.0,
                                    ALU.add, ALU.max).then_inc(dt_rel.h, 1)
                if kind == "t":
                    v.wait_ge(dt_ln.h, dt_ln.at(img, k * NC + u + 1))
                    v.tensor_tensor(dt[:, u, :], dt[:, u, :], dtu[:, u, :], ALU.add).then_inc(dt_sum.h, 1)
                if kind == "s":
                    if u < STEPS1:
                        i, k, c, n = place(u)
                        slot = (k * N + n) % SLOTS
                        if c == 0:
                            v.wait_ge(bc_ld[slot].h, bc_ld[slot].at(img, 16 * ((k * N + n) // SLOTS + 1)))
                        if n == 0:
                            v.wait_ge(dt_sb.h, dt_sb.at(img, k * NC + c + 1))
                        if i >= 4:
                            v.wait_ge(y_ps.h, y_ps.at(img, i - 3))
                        v.tensor_tensor(state[i % 4], dtu[:, c, :], bc[slot][:, 0, :], ALU.mult).then_inc(b_sb.h, 1)
                    if 1 <= u <= STEPS1:
                        i, k, c, n = place(u - 1)
                        back = DIRS[k][1]
                        v.wait_ge(a_sb.h, a_sb.at(img, i + 1))
                        v.wait_ge(b_sb.h, b_sb.at(img, i + 1))
                        d, s = decay[i % 2], state[i % 4]
                        if back:
                            d, s = d[:, ::-1], s[:, ::-1]
                        v.tensor_tensor_scan(s, d, s, 0.0, ALU.mult, ALU.add).then_inc(h_sb.h, 1)
                if kind == "y":
                    v.wait_ge(y_ps.h, y_ps.at(img, GN_ * (u + 1)))
                    ysl = ysum[:, :, (u % NC) * P:(u % NC + 1) * P]
                    v.tensor_tensor(ysl, ysl, banks(4).rearrange("p (b c) -> p b c", b=LB), ALU.add)\
                        .then_inc(y_sb.h, 1)

            def layers_1_to_3(img):
                v.drain()
                bst = stats[:, 0:48].rearrange("p (b s) -> p b s", s=6)
                for b in range(LB):
                    v.bn_stats(bst[:, b, :], ysum[:, b, :])
                v.drain()
                agg = ln_t[:, 0:16].rearrange("p (b s) -> p b s", s=2)
                for b in range(LB):
                    v.bn_aggr(agg[:, b, :], bst[:, b, :])
                v.drain()
                v.tensor_scalar(ln_t[:, 24:32], agg[:, :, 1], EPS, None, ALU.add).then_inc(ln_st.h, 1)
                v.wait_ge(ln_r.h, ln_r.at(img, 1))
                for b in range(LB):
                    ins = v.tensor_scalar(ysum[:, b, :], ysum[:, b, :], agg[:, b, 0:1], ln_t[:, 16 + b:17 + b],
                                          ALU.subtract, ALU.mult)
                ins.then_inc(ln_o.h, 1)
                for c in range(NC):
                    v.wait_ge(g_sb.h, g_sb.at(img, c + 1))
                    v.tensor_tensor(X3[:, c, :], X3[:, c, :], gel[c % 2], ALU.add).then_inc(x2.h, 1)
                v.drain()
                group_norm(img, 1, xn2)
                for r in range(6):
                    v.wait_ge(o2_ps.h, o2_ps.at(img, r + 1))
                    v.tensor_copy(out2[:, 16 * r:16 * r + 16, :].rearrange("p a s -> p (a s)"), ps[:, 2 + r % 2, :])\
                        .then_inc(o2_sb.h, 1)
                v.wait_ge(b2_ld.h, b2_ld.at(img, 16))
                ins = v.tensor_tensor(X[:, :], X[:, :], blur.rearrange("p c l -> p (c l)"), ALU.add)
                ins.then_inc(x3.h, 1)
                v.drain()
                group_norm(img, 2, xn3)
                for c in range(NC):
                    v.tensor_scalar(X3[:, c, :], X3[:, c, :], cst3[:, c:c + 1], None, ALU.add)
                for b in range(LB):
                    v.wait_ge(v3_ps.h, v3_ps.at(img, b + 1))
                    v.tensor_copy(vT3[:, b, :], ps[:, 4 + b % 2, 0:C]).then_inc(v3_sb.h, 1)

                def rowmax3(u):
                    v.wait_ge(s3_ps.h, s3_ps.at(img, u + 1))
                    v.tensor_reduce(se_t[:, 16 + u:17 + u], banks(2 * (u % 2)), AX.X, ALU.max, negate=True)\
                        .then_inc(s3_mx.h, 1)

                def normalize3(u):
                    v.wait_ge(s3_ex.h, s3_ex.at(img, u + 1))
                    v.reciprocal(se_t[:, 40 + u:41 + u], se_t[:, 24 + u:25 + u])
                    v.drain()
                    v.tensor_scalar(prob3[u % 2], prob3[u % 2], se_t[:, 40 + u:41 + u], None, ALU.mult)\
                        .then_inc(s3_nm.h, 1)

                for u in range(LB + 1):
                    if u < LB:
                        rowmax3(u)
                    if u >= 1:
                        normalize3(u - 1)
                v.wait_ge(y3_sb.h, y3_sb.at(img, 2 * NC))
                v.tensor_tensor(se_t[:, 8:11], se_t[:, 0:3], se_t[:, 3:6], ALU.add)
                v.drain()
                v.tensor_scalar(se_t[:, 8:11], se_t[:, 8:11], 1.0 / L, None, ALU.mult).then_inc(se_pool.h, 1)
                v.wait_ge(se_h.h, se_h.at(img, 1))
                v.tensor_scalar(se_t[0:SE, 12:13], ps[0:SE, 0, 0:1], vec96[0:SE, 4:5], 0.0, ALU.add, ALU.max)\
                    .then_inc(se_hr.h, 1)
                v.wait_ge(se_z.h, se_z.at(img, 1))
                v.tensor_tensor(se_t[:, 33:36], ps[:, 1, 0:3], vec3("bse2"), ALU.add).then_inc(se_zb.h, 1)
                v.wait_ge(se_e.h, se_e.at(img, 1))
                v.tensor_scalar(se_t[:, 50:53], se_t[:, 36:39], 1.0, None, ALU.add)
                v.drain()
                v.reciprocal(se_t[:, 54:57], se_t[:, 50:53])
                v.drain()
                for c in range(NC):
                    ins = v.tensor_scalar(wg3[:, c, :], wp3[:, c, :], se_t[:, 54 + c:55 + c], None, ALU.mult)
                ins.then_inc(se_w.h, 1)
                for m in range(NC):
                    v.wait_ge(f_ps.h, f_ps.at(img, m + 1))
                    v.scalar_tensor_tensor(X3[:, m, :], banks(2 * (m % 2)), inv3[:, m:m + 1], X3[:, m, :],
                                           ALU.mult, ALU.add).then_inc(f_sb.h, 1)

            before_attention(0)
            for ev in schedule(True, False):
                attention(0, ev[1])
            after_attention(0)
            with v.Fori(0, B - 1) as img:
                before_attention(img + 1)
                group_norm(img, 0, U)
                v.memset(ysum.rearrange("p b c -> p (b c)"), 0.0)
                v.drain()
                for ev in schedule(True, True):
                    if ev[0] == "a":
                        attention(img + 1, ev[1])
                    else:
                        scan(img, *ev)
                layers_1_to_3(img)
                after_attention(img + 1)
            group_norm(B - 1, 0, U)
            v.memset(ysum.rearrange("p b c -> p (b c)"), 0.0)
            v.drain()
            for ev in schedule(False, True):
                scan(B - 1, *ev)
            layers_1_to_3(B - 1)


def _chunks(a):
    return np.ascontiguousarray(a.reshape(NC, P, -1).transpose(1, 0, 2).reshape(P, -1))


def kernel(**inputs):
    import concourse.bacc as bacc
    from concourse.bass_utils import run_bass_kernel_spmd
    a = {n: np.asarray(v) for n, v in inputs.items()}
    ds, dtb = a["L1_conv_Ds"].reshape(K, C), a["L1_conv_dt_projs_bias"]
    qb_ = a["L0_conv_qkvo_b"]
    cols = [qb_[0:C], qb_[C:2 * C], qb_[2 * C:3 * C], qb_[3 * C:], a["L0_conv_lepe_b"], a["L0_conv_proj_b"],
            ds[0], ds[1], ds[2], ds[3], a["L1_conv_ln_weight"], a["L1_conv_ln_bias"], dtb[0], dtb[1], dtb[2], dtb[3],
            a["L3_conv_bv"], a["L3_conv_b_proj"], a["L3_conv_bn_gamma"], a["L3_conv_bn_beta"], a["L3_conv_bn_mean"],
            a["L3_conv_bn_var"], a["L3_conv_b_se2"]]
    vecs = np.stack([v.reshape(NC, P) for v in cols]).transpose(2, 0, 1).reshape(P, NV * NC)
    bq3, bk3 = a["L3_conv_bq"].reshape(2, QC3), a["L3_conv_bk"].reshape(2, QC3)
    vec96 = np.stack([bq3[0], bq3[1], bk3[0], bk3[1], a["L3_conv_b_se1"]], axis=1)
    xw = a["L1_conv_x_proj_weight"]
    xw = np.concatenate([xw[:, R:], xw[:, :R]], axis=1)
    chan = np.arange(C) // (C // GROUPS)
    same = (chan[:, None] == chan[None, :]).astype(np.float32) / (C // GROUPS)
    ga = same.reshape(NC, P, NC, P).transpose(1, 0, 2, 3).reshape(P, -1)
    w3 = lambda w: _chunks(w.T).reshape(P, NC, -1)
    arrays = {
        "x": a["x"].reshape(B, C, L),
        "ident": np.eye(P, dtype=np.float32),
        "group_avg": ga,
        "vecs": vecs, "vec96": vec96,
        "lepe_w": _chunks(a["L0_conv_lepe_w"].reshape(C, 25)),
        "A_logs": a["L1_conv_A_logs"].reshape(K, NC, P, N).transpose(2, 0, 1, 3).reshape(P, -1),
        "w_xproj": _chunks(xw.transpose(2, 0, 1).reshape(C, K * XR)),
        "w_dt": a["L1_conv_dt_projs_weight"][[cols + 2 * back for cols, back in DIRS]].transpose(2, 0, 1).reshape(R, K * C),
        "w_proj0": w3(a["L0_conv_proj_w"].reshape(C, C)),
        "row_index": (np.arange(P) % 32).astype(np.float32).reshape(P, 1),
        "col_row": np.tile(np.arange(32, dtype=np.float32), (P, 1)),
        "offset": a["L2_conv_offset"],
        "w_qkvo": w3(a["L0_conv_qkvo_w"].reshape(4 * C, C)),
        "wq3": w3(a["L3_conv_wq"]), "wk3": w3(a["L3_conv_wk"]), "wv3": w3(a["L3_conv_wv"]),
        "wp3": w3(a["L3_conv_w_proj"]), "wse1": w3(a["L3_conv_w_se1"]), "wse2": a["L3_conv_w_se2"].T,
    }
    nc = bacc.Bacc("TRN2", target_bir_lowering=False, num_devices=1, dynamic_dma_scratch_size=8192)
    t, feed = {}, {}
    for name, v in arrays.items():
        feed["in_" + name] = np.ascontiguousarray(v)
        t[name] = nc.dram_tensor("in_" + name, v.shape, F32, kind="ExternalInput").ap()
    t["out"] = nc.dram_tensor("out_0", (B, C, L), F32, kind="ExternalOutput").ap()
    for name, shape in [("bc_scratch", (K, 2 * N, L)), ("shift_scratch", (P, (POS + PG) * P)),
                        ("rows_scratch", (C, L)), ("blur_scratch", (C, L))]:
        t[name] = nc.dram_tensor(name, shape, F32, kind="Internal").ap()
    build(nc, t)
    r = run_bass_kernel_spmd(nc, [feed], core_ids=[0])
    return r.results[0]["out_0"].reshape(B, C, HH, WW)
```

```python
import numpy as np
import concourse.bass as bass
from concourse import mybir
from contextlib import ExitStack

F32 = mybir.dt.float32
ACT = mybir.ActivationFunctionType
ALU = mybir.AluOpType
AX = mybir.AxisListType

B, C, HH, WW = 8, 384, 32, 32
L = HH * WW
P = 128
NC = C // P
LB = L // P
HALF = 512
HEADS, HD = 12, 32
SC0 = HD ** -0.5
STEPS0 = HEADS * LB
K, R, N = 4, 12, 16
XR = R + 2 * N
GN_ = 4
SLOTS = 5
STEPS1 = K * NC * N
HELD = 5
LAG = 3
POS, CPP = 48, 8
PG = POS // 4
QK3 = 192
QC3 = QK3 // 2
SE = C // 4
SC3 = 32.0 ** -0.5
GROUPS = 32
EPS = 1e-5

VEC = {n: i for i, n in enumerate(
    ["bq", "bk", "bv", "bo", "lepe_b", "proj_b", "D0", "D1", "D2", "D3", "ln_w", "ln_b",
     "dtb0", "dtb1", "dtb2", "dtb3", "bv3", "bproj3", "gamma", "beta", "mean", "var", "bse2"])}
NV = len(VEC)


DIRS = [(1, 0), (1, 1), (0, 0), (0, 1)]


def schedule(attention, scans):
    before = {}

    def put(u, *ev):
        before.setdefault(u, []).append(ev)

    per = STEPS1 // K
    for run in range(STEPS1 // GN_):
        u = GN_ * run + GN_ + LAG
        put(u, "y", run)
        if run >= 2 * per // GN_ - NC and run < 2 * per // GN_:
            put(u, "m", run - (2 * per // GN_ - NC))
    for k in range(1, K):
        for hf in range(2):
            put(per * k - 22 + 3 * hf, "x", k, hf)
        for c in range(NC):
            u = per * k - 6 + GN_ * c
            put(u, "d", k, 2 * c)
            put(u + 1, "d", k, 2 * c + 1)
            put(u + 2, "l", k, c)
            put(u + 4, "t", k, c)
    for a in range(STEPS0 + 1):
        put(2 * a + 1, "a", a)
        put(2 * a + 2, "o", a)
        put(2 * a + 2, "p", a)
        put(2 * a + 2, "e", a)
    order = [("x", 0, hf) for hf in range(2)]
    for c in range(NC):
        order += [("d", 0, 2 * c), ("d", 0, 2 * c + 1)]
    for c in range(NC):
        order += [("l", 0, c), ("t", 0, c)]
    for u in range(STEPS1 + LAG + 1):
        order += before.get(u, [])
        if u < STEPS1 + LAG:
            order.append(("s", u))
    order += [(kind, STEPS0 + i) for i in (1, 2) for kind in "oape"]
    return [ev for ev in order if (attention if ev[0] in "oape" else scans)]


def place(i):
    k, u = i // (STEPS1 // K), i % (STEPS1 // K)
    return i, k, u // GN_ % NC, GN_ * (u // (NC * GN_)) + u % GN_


def slot_used(i):
    k, n = i // N, i % N
    return STEPS1 // K * k + NC * GN_ * (n // GN_) + (NC - 1) * GN_ + n % GN_ + 1


class Signal:

    def __init__(self, handle, per):
        self.h, self.per = handle, per

    def at(self, img, n):
        return img * self.per + (n + 1)


def build(nc, t):
    ctx = ExitStack()
    with ctx:
        def sb(name, cols, parts=P):
            return ctx.enter_context(nc.sbuf_tensor(name, [parts, cols], F32))

        signals = []

        def sem(name, per):
            s = Signal(ctx.enter_context(nc.semaphore(name)), per)
            if per:
                signals.append(s)
            return s

        ident = sb("ident", P)
        group_avg = sb("group_avg", NC * NC * P)
        vecs = sb("vecs", NV * NC)
        vec96 = sb("vec96", 5)
        lepe_w = sb("lepe_w", NC * 25)
        negA = sb("negA", K * NC * N)
        w_xproj = sb("w_xproj", NC * K * XR)
        w_dt = sb("w_dt", C)
        derived = sb("derived", 32)
        half_neg = sb("half_neg", 8)
        gn_t = sb("gn_t", 96)
        ln_t = sb("ln_t", 64)
        se_t = sb("se_t", 64)
        stats = sb("stats", 48)
        X = sb("X", NC * L)
        R_ = sb("R", 47 * 1024)
        gn0_t = sb("gn0_t", 40)
        ps = ctx.enter_context(nc.psum_tensor("ps", [P, 8, HALF], F32))

        ga = group_avg[:, :].rearrange("p (a b m) -> p a b m", a=NC, b=NC)
        X3 = X[:, :].rearrange("p (c l) -> p c l", c=NC)

        def reg(at, words):
            return R_[:, at:at + words]

        def vec(name, c):
            i = VEC[name] * NC + c
            return vecs[:, i:i + 1]

        def banks(b):
            return ps[:, b:b + 2, :].rearrange("p b n -> p (b n)")

        K1 = 1024

        def chunks(at):
            return reg(at, NC * L).rearrange("p (c l) -> p c l", c=NC)

        def blocks(at):
            return reg(at, NC * L).rearrange("p (b c) -> p b c", b=LB)

        def weights(at, cols):
            return reg(at, NC * cols).rearrange("p (c o) -> p c o", c=NC)

        q4, k4, vT, heads = chunks(0), chunks(3 * K1), blocks(6 * K1), blocks(9 * K1)
        probs = [reg((12 + i) * K1, K1) for i in range(2)]
        probsT = [reg((14 + i) * K1, K1).rearrange("p (b q) -> p b q", b=LB) for i in range(2)]
        xn0 = chunks(16 * K1)
        xa0 = chunks(19 * K1)
        w0a = weights(28 * K1, 3 * C)
        wo0 = weights(12 * K1, C)
        wp0 = weights(12 * K1 + NC * C, C)
        gate0 = [reg((40 + i) * K1, K1) for i in range(2)]
        res = chunks(42 * K1)
        vpad = reg(45 * K1, 36 * 36)
        U, ysum, dt, dtu = chunks(16 * K1), blocks(19 * K1), chunks(22 * K1), chunks(25 * K1)
        bc = [reg((28 + 2 * i) * K1, 2 * K1).rearrange("p (t l) -> p t l", t=2) for i in range(SLOTS)]
        turned = reg(38 * K1, K1)
        decay = [reg((40 + i) * K1, K1) for i in range(2)]
        state = [reg(at * K1, K1) for at in (39, 42, 43, 44, 45)]
        xdbl = reg(46 * K1, K1)
        gel = decay
        xn2 = chunks(16 * K1)
        rows2 = reg(19 * K1, 3 * K1).rearrange("p (j s) -> p j s", s=32)
        mid2 = reg(22 * K1, 3 * K1).rearrange("p (g m) -> p g m", m=P)
        out2 = reg(25 * K1, 3 * K1).rearrange("p (j s) -> p j s", s=32)
        shifts = reg(28 * K1, (POS + PG) * P)
        shift_x = shifts[:, 0:POS * P].rearrange("p (q m) -> p q m", q=POS)
        shift_y = shifts[:, POS * P:(POS + PG) * P].rearrange("p (g m) -> p g m", g=PG)
        blur = chunks(12 * K1)
        xn3 = chunks(16 * K1)
        q3 = reg(19 * K1, 2 * K1).rearrange("p (c l) -> p c l", c=2)
        k3 = reg(21 * K1, 2 * K1).rearrange("p (c l) -> p c l", c=2)
        vT3 = blocks(23 * K1)
        prob3 = [reg(i * K1, K1) for i in range(2)]
        prT3 = [reg((28 + 4 * i) * K1, 4 * K1).rearrange("p (b q) -> p b q", b=LB) for i in range(2)]
        y3 = chunks(3 * K1)
        wg3 = weights(6 * K1, C)
        at3 = 28 * K1 + (POS + PG) * P
        wq3, wk3 = weights(at3, QK3), weights(at3 + NC * QK3, QK3)
        wv3, wp3 = weights(at3 + 2 * NC * QK3, C), weights(at3 + NC * (2 * QK3 + C), C)
        wse1 = weights(at3 + NC * (2 * QK3 + 2 * C), SE)
        at3 += NC * (2 * QK3 + 2 * C + SE)
        wse2 = R_[0:SE, at3:at3 + C]
        negmax, rowsum, rowinv = (gn_t[:, i:i + 8] for i in (64, 72, 80))
        qb = derived[:, 0:3]
        dsum = derived[:, 3:6]
        inv3 = derived[:, 6:9]
        cst3 = derived[:, 9:12]
        qb3 = derived[:, 12:14]
        tmp_d = derived[:, 14:20]

        c_in = sem("consts_loaded", 0)
        pre_v = sem("pre_vector", 0)
        pre_a = sem("pre_scalar", 0)
        pre_g = sem("pre_gpsimd", 0)
        pre_st = sem("shift_x_stored", 0)
        xa_in = sem("x_loaded_for_attention", 16)
        xb_in = sem("x_loaded_for_gate", 16)
        xr_in = sem("x_loaded_as_residual", 16)
        wa_in = sem("qkv_weights_loaded", 16)
        wb_in = sem("gate_weights_loaded", 32)
        wd_in = sem("dt_weights_loaded", 16 * K)
        ws_in = sem("shifts_loaded", 16)
        w3_in = sem("layer3_weights_loaded", 96)
        g0_stat = sem("gn0_stats", 1)
        g0_mean = sem("gn0_group_mean", 1)
        g0_dev = sem("gn0_deviation", 1)
        g0_var = sem("gn0_group_var", 1)
        g0_eps = sem("gn0_var_eps", 1)
        g0_rstd = sem("gn0_rstd", 1)
        g0_out = sem("gn0_normalized", 1)
        g0_again = sem("gn0_normalized_again", 1)
        gn_stat = sem("gn_stats", 3)
        gn_mean = sem("gn_group_mean", 3)
        gn_dev = sem("gn_deviation", 3)
        gn_var = sem("gn_group_var", 3)
        gn_eps = sem("gn_var_eps", 3)
        gn_rstd = sem("gn_rstd", 3)
        gn_out = sem("gn_normalized", 3)
        qk_ps = sem("qk_projected", 6)
        qk_sb = sem("qk_evacuated", 6)
        vt_ps = sem("vT_projected", LB)
        vt_sb = sem("vT_evacuated", LB)
        s_ps = sem("scores_ready", STEPS0)
        s_max = sem("rowmax_ready", STEPS0)
        s_exp = sem("probs_ready", STEPS0)
        t_ps = sem("probsT_in_psum", STEPS0)
        t_sb = sem("probsT_ready", STEPS0)
        pv_ps = sem("head_out_in_psum", STEPS0)
        o_sb = sem("head_out_ready", STEPS0)
        lv_ps = sem("v_transposed", NC)
        lv_sb = sem("v_padded", NC)
        lp_sb = sem("depthwise_term_ready", NC)
        vo_ps = sem("gate_projected", NC)
        vo_sb = sem("gate_evacuated", NC)
        hT_ps = sem("heads_transposed", NC)
        r_sb = sem("gated_result_ready", NC)
        p0_ps = sem("proj0_in_psum", NC)
        x1 = sem("x1_ready", NC)
        xd_ps = sem("xproj_in_psum", 2 * K)
        xd_sb = sem("xproj_evacuated", 2 * K)
        bc_st = sem("bc_rows_stored", 32 * K)
        bc_ld = [sem(f"bc_rows_loaded{i}", 16 * len(range(i, K * N, SLOTS))) for i in range(SLOTS)]
        dt_ps = sem("dt_in_psum", 2 * K * NC)
        dt_abs = sem("dt_abs_read", 2 * K * NC)
        dt_ln = sem("dt_log_ready", K * NC)
        dt_sum = sem("dt_ready", K * NC)
        dt_sb = sem("dt_times_u_ready", K * NC)
        mg_ps = sem("column_sum_turned_back", NC)
        mg_sb = sem("column_sum_reordered", NC)
        mg_tp = sem("column_sum_turned", NC)
        mg_y = sem("column_sum_in_ysum", NC)
        a_sb = sem("decay_ready", STEPS1)
        b_sb = sem("drive_ready", STEPS1)
        h_sb = sem("state_ready", STEPS1)
        hc_sb = sem("state_times_c_ready", STEPS1)
        y_ps = sem("y_transposed", STEPS1)
        y_sb = sem("y_sum_ready", STEPS1 // GN_)
        ln_st = sem("ln_stats", 1)
        ln_r = sem("ln_rstd", 1)
        ln_o = sem("ln_normalized", 1)
        lt_ps = sem("ln_transposed", NC)
        g_sb = sem("gelu_ready", NC)
        x2 = sem("x2_ready", NC)
        s2_st = sem("xn2_stored", 16)
        s2_ld = sem("rows2_loaded", 64)
        m2_ps = sem("rows_shifted", 6)
        m2_sb = sem("rows_shifted_evacuated", 6)
        o2_ps = sem("cols_shifted", 6)
        o2_sb = sem("cols_shifted_evacuated", 6)
        o2_st = sem("blur_stored", 64)
        b2_ld = sem("blur_loaded", 16)
        x3 = sem("x3_ready", 1)
        p3_ps = sem("qk3_in_psum", 4)
        p3_sb = sem("qk3_evacuated", 4)
        v3_ps = sem("vT3_in_psum", LB)
        v3_sb = sem("vT3_evacuated", LB)
        s3_ps = sem("scores3_ready", LB)
        s3_mx = sem("rowmax3_ready", LB)
        s3_ex = sem("probs3_ready", LB)
        s3_nm = sem("probs3_normalized", LB)
        s3_tp = sem("probs3T_in_psum", LB)
        s3_ts = sem("probs3T_ready", LB)
        y3_ps = sem("y3_in_psum", 2 * NC)
        y3_sb = sem("y3_evacuated", 2 * NC)
        se_pool = sem("pooled_ready", 1)
        se_h = sem("se_hidden_in_psum", 1)
        se_hr = sem("se_hidden_ready", 1)
        se_z = sem("se_logits_in_psum", 1)
        se_zb = sem("se_logits_ready", 1)
        se_e = sem("se_exp_ready", 1)
        se_w = sem("gated_weights_ready", 1)
        f_ps = sem("proj3_in_psum", NC)
        f_sb = sem("out_ready", NC)
        out_st = sem("out_stored", 16)

        bc_d = t["bc_scratch"]
        sx_d = t["shift_scratch"]
        s2_d = t["rows_scratch"]
        o2_d = t["blur_scratch"]

        block = ctx.enter_context(nc.Block())
        def img3(a, img):
            return a[img].rearrange("(c p) l -> p c l", p=P)

        def transposed(ap):
            return ap.rearrange("p (h w) -> p w h", w=WW)

        @block.sync
        def _(sp):
            for s in signals:
                sp.sem_inc(s.h, 1)
            for name, dst in [("ident", ident[:, :]), ("group_avg", group_avg[:, :]), ("vecs", vecs[:, :]),
                              ("vec96", vec96[0:QC3, :]), ("lepe_w", lepe_w[:, :]), ("A_logs", negA[:, :]),
                              ("w_xproj", w_xproj[:, :]),
                              ("row_index", R_[:, 0:1]), ("col_row", R_[:, 32:64])]:
                sp.dma_start(dst, t[name]).then_inc(c_in.h, 16)
            with nc.allow_non_contiguous_dma(reason="48 offsets, once"):
                for q in range(4):
                    src = t["offset"][q * PG:(q + 1) * PG, :].rearrange("g d -> (g d)")
                    sp.dma_start(R_[32 * q:32 * q + 32, 64:64 + 2 * PG],
                                 src[None, :].to_broadcast([32, 2 * PG])).then_inc(c_in.h, 16)
                src = t["offset"].rearrange("g d -> (g d)")
                sp.dma_start(R_[:, 96:96 + 2 * POS], src[None, :].to_broadcast([P, 2 * POS])).then_inc(c_in.h, 16)
            sp.wait_ge(pre_v.h, 2)
            sp.dma_start(sx_d, shifts).then_inc(pre_st.h, 16)
            sp.wait_ge(pre_st.h, 16)


            def before_attention(img):
                sp.dma_start(xa0, img3(t["x"], img)).then_inc(xa_in.h, 16)
                sp.dma_start(w0a, t["w_qkvo"][:, :, 0:3 * C]).then_inc(wa_in.h, 16)

            def scans(img):
                for k in range(K):
                    at = 64 * (k % 2)
                    sp.wait_ge(dt_ps.h, dt_ps.at(img, 2 * NC * max(k - 1, 0)))
                    sp.dma_start(w_dt[at + 32:at + 32 + R, :], t["w_dt"][:, k * C:(k + 1) * C]).then_inc(wd_in.h, 16)
                    sp.wait_ge(xd_sb.h, xd_sb.at(img, 2 * k + 2))
                    sp.dma_start(bc_d[k, 0:N], xdbl[at:at + N, :]).then_inc(bc_st.h, 16)
                    if k:
                        sp.wait_ge(hc_sb.h, hc_sb.at(img, slot_used(k * N - SLOTS)))
                    sp.dma_start(bc_d[k, N:], xdbl[at + N:at + 2 * N, :]).then_inc(bc_st.h, 16)
                    sp.wait_ge(bc_st.h, bc_st.at(img, 32 * (k + 1)))
                    for n in range(N):
                        i = k * N + n
                        if i >= SLOTS and n:
                            sp.wait_ge(hc_sb.h, hc_sb.at(img, slot_used(i - SLOTS)))
                        rows = bc_d[k].rearrange("(t n) l -> n t l", t=2)[n]
                        sp.dma_start(bc[i % SLOTS], rows[None, :, :].to_broadcast([P, 2, L])).then_inc(bc_ld[i % SLOTS].h, 16)

            def after_scans(img):
                sp.wait_ge(y_ps.h, y_ps.at(img, STEPS1))
                sp.dma_start(shifts, sx_d).then_inc(ws_in.h, 16)
                for name, dst in [("wq3", wq3), ("wk3", wk3), ("wv3", wv3), ("wp3", wp3), ("wse1", wse1), ("wse2", wse2)]:
                    sp.dma_start(dst, t[name]).then_inc(w3_in.h, 16)
                sp.wait_ge(gn_out.h, gn_out.at(img, 2))
                sp.dma_start(s2_d.rearrange("(c p) l -> p c l", p=P), xn2).then_inc(s2_st.h, 16)
                sp.wait_ge(s2_st.h, s2_st.at(img, 16))
                quads = s2_d.rearrange("(q j) (y x) -> q y j x", q=4, x=WW)
                for q in range(4):
                    sp.dma_start(rows2[32 * q:32 * q + 32, :, :], quads[q]).then_inc(s2_ld.h, 16)
                sp.wait_ge(o2_sb.h, o2_sb.at(img, 6))
                quads = o2_d.rearrange("(q j) (y x) -> q y j x", q=4, x=WW)
                for q in range(4):
                    sp.dma_start(quads[q], out2[32 * q:32 * q + 32, :, :]).then_inc(o2_st.h, 16)
                sp.wait_ge(o2_st.h, o2_st.at(img, 64))
                sp.dma_start(blur, o2_d.rearrange("(c p) l -> p c l", p=P)).then_inc(b2_ld.h, 16)

            def store_out(img):
                sp.wait_ge(f_sb.h, f_sb.at(img, NC))
                sp.dma_start(img3(t["out"], img), X3).then_inc(out_st.h, 16)

            def load_gate(img):
                sp.dma_start(wo0, t["w_qkvo"][:, :, 3 * C:4 * C]).then_inc(wb_in.h, 16)
                sp.dma_start(wp0, t["w_proj0"]).then_inc(wb_in.h, 16)
                sp.dma_start(xn0, img3(t["x"], img)).then_inc(xb_in.h, 16)

            def load_residual(img):
                sp.dma_start(X3, img3(t["x"], img)).then_inc(xr_in.h, 16)

            before_attention(0)
            sp.wait_ge(pv_ps.h, pv_ps.at(0, STEPS0))
            load_gate(0)
            load_residual(0)
            with sp.Fori(0, B - 1) as img:
                sp.wait_ge(y3_ps.h, y3_ps.at(img, 0))
                before_attention(img + 1)
                scans(img)
                after_scans(img)
                sp.wait_ge(v3_ps.h, v3_ps.at(img, LB))
                load_gate(img + 1)
                store_out(img)
                sp.wait_ge(out_st.h, out_st.at(img, 16))
                load_residual(img + 1)
            scans(B - 1)
            after_scans(B - 1)
            store_out(B - 1)
            sp.wait_ge(out_st.h, out_st.at(B - 1, 16))

        @block.tensor
        def _(pe):
            def group_mean(src, col):
                for m in range(NC):
                    near = [a for a in range(NC) if abs(a - m) < 2]
                    for a in near:
                        mm = pe.matmul(ps[:, 7, col + m:col + m + 1], ga[:, a, m, :], src[:, a:a + 1],
                                       start=a == near[0], stop=a == near[-1])
                return mm

            def group_mean_of(img, g):
                pe.wait_ge(gn_stat.h, gn_stat.at(img, g + 1))
                group_mean(gn_t[:, 0:3], 0).then_inc(gn_mean.h, 1)

            def group_var_of(img, g):
                pe.wait_ge(gn_dev.h, gn_dev.at(img, g + 1))
                group_mean(gn_t[:, 16:19], 8).then_inc(gn_var.h, 1)

            def group_norm(img, g):
                group_mean_of(img, g)
                group_var_of(img, g)

            def project(dst, lhs, rhs, parts=P):
                for hf in range(2):
                    for c in range(NC):
                        mm = pe.matmul(dst[0:parts, hf * HALF:(hf + 1) * HALF], lhs[:, c], rhs(c, hf),
                                       start=c == 0, stop=c == NC - 1)
                return mm

            def rows_of(x):
                return lambda c, hf: x[:, c, hf * HALF:(hf + 1) * HALF]

            def turn_blocks(bank, src):
                for b in range(LB):
                    mm = pe.matmul(ps[:, bank + b // 4, (b % 4) * P:(b % 4 + 1) * P], src(b), ident[:, :],
                                   start=True, stop=True, is_transpose=True)
                return mm

            def before_attention(img, norm=None):
                pe.wait_ge(g0_stat.h, g0_stat.at(img, 1))
                group_mean(gn0_t[:, 0:3], 0).then_inc(g0_mean.h, 1)
                pe.wait_ge(g0_dev.h, g0_dev.at(img, 1))
                group_mean(gn0_t[:, 16:19], 8).then_inc(g0_var.h, 1)
                pe.wait_ge(g0_out.h, g0_out.at(img, 1))
                pe.wait_ge(wa_in.h, wa_in.at(img, 16))
                for i in range(6):
                    if i >= 2:
                        pe.wait_ge(qk_sb.h, qk_sb.at(img, i - 1))
                    project(banks(2 * (i % 2)), w0a[:, :, i * P:(i + 1) * P], rows_of(xa0)).then_inc(qk_ps.h, 1)
                    if i == 3 and norm is not None:
                        group_mean_of(norm, 0)
                    if i == 4 and norm is not None:
                        group_var_of(norm, 0)
                for b in range(LB):
                    if b >= 2:
                        pe.wait_ge(vt_sb.h, vt_sb.at(img, b - 1))
                    for c in range(NC):
                        mm = pe.matmul(ps[:, 4 + b % 2, 0:C], xa0[:, c, b * P:(b + 1) * P], w0a[:, c, 2 * C:3 * C],
                                       start=c == 0, stop=c == NC - 1)
                    mm.then_inc(vt_ps.h, 1)

            def attention(img, kind, a, alone=False):
                if kind not in "ap":
                    return
                if kind == "a" and a == 0:
                    pe.wait_ge(qk_sb.h, qk_sb.at(img, 6))
                    pe.wait_ge(vt_sb.h, vt_sb.at(img, LB))
                if kind == "a" and a < STEPS0:
                    h, qc = a // LB, a % LB
                    row = 32 * (h % 4)
                    bank = 4 * (a % 2) if alone else 0
                    if alone and a >= 2:
                        pe.wait_ge(s_exp.h, s_exp.at(img, a - 1))
                    if a and not alone:
                        pe.wait_ge(s_exp.h, s_exp.at(img, a))
                    for hf in range(2):
                        mm = pe.matmul(ps[:, bank + hf, :], q4[row:row + HD, h // 4, qc * P:(qc + 1) * P],
                                       k4[row:row + HD, h // 4, hf * HALF:(hf + 1) * HALF], start=True, stop=True)
                    mm.then_inc(s_ps.h, 1)
                if kind == "a" and 1 <= a <= STEPS0:
                    u = a - 1
                    pe.wait_ge(s_exp.h, s_exp.at(img, u + 1))
                    if u >= 1:
                        pe.wait_ge(t_sb.h, t_sb.at(img, u))
                    if alone and a >= 2:
                        products_ready(img, a)
                    for b in range(LB):
                        mm = pe.matmul(ps[:, 2 + b // 4, (b % 4) * P:(b % 4 + 1) * P], probs[u % 2][:, b * P:(b + 1) * P],
                                       ident[:, :], start=True, stop=True, is_transpose=True)
                        if alone and a >= 2:
                            pv = product(a, b)
                    mm.then_inc(t_ps.h, 1)
                    if alone and a >= 2:
                        pv.then_inc(pv_ps.h, 1)
                if kind == "p" and a == STEPS0 + 1:
                    products_ready(img, a)
                    for b in range(LB):
                        pv = product(a, b)
                    pv.then_inc(pv_ps.h, 1)

            def products_ready(img, a):
                pe.wait_ge(t_sb.h, t_sb.at(img, a - 1))
                if a > 2:
                    pe.wait_ge(o_sb.h, o_sb.at(img, a - 2))

            def product(a, b):
                h = (a - 2) // LB
                return pe.matmul(ps[:, 6, 0:HD], probsT[a % 2][:, b, :], vT[:, b, HD * h:HD * h + HD],
                                 start=b == 0, stop=b == LB - 1)

            def turn_v(img, m):
                if m:
                    pe.wait_ge(lv_sb.h, lv_sb.at(img, m))
                turn_blocks(4, lambda b: vT[:, b, m * P:(m + 1) * P]).then_inc(lv_ps.h, 1)

            def after_attention(img):
                pe.wait_ge(g0_again.h, g0_again.at(img, 1))
                pe.wait_ge(wb_in.h, wb_in.at(img, 32))
                pe.wait_ge(o_sb.h, o_sb.at(img, STEPS0))
                for m in range(NC):
                    if m == 2:
                        pe.wait_ge(vo_sb.h, vo_sb.at(img, 1))
                    project(banks(2 * (m % 2)), wo0[:, :, m * P:(m + 1) * P], rows_of(xn0)).then_inc(vo_ps.h, 1)
                    if m == 2:
                        pe.wait_ge(r_sb.h, r_sb.at(img, 1))
                    turn_blocks(4 + 2 * (m % 2), lambda b: heads[:, b, m * P:(m + 1) * P]).then_inc(hT_ps.h, 1)
                pe.wait_ge(r_sb.h, r_sb.at(img, NC))
                for m in range(NC):
                    if m == 2:
                        pe.wait_ge(x1.h, x1.at(img, 1))
                    project(banks(2 * (m % 2)), wp0[:, :, m * P:(m + 1) * P], rows_of(res)).then_inc(p0_ps.h, 1)

            wx = w_xproj[:, :].rearrange("p (c k r) -> p c k r", c=NC, k=K)

            def scan(img, kind, k, u=0, beside=0):
                if kind in "xdlt":
                    cols, back = DIRS[k]
                if kind in "sym":
                    u = k
                if kind == "m":
                    c = u
                    pe.wait_ge(y_sb.h, y_sb.at(img, STEPS1 // 2 // GN_ - NC + c + 1))
                    turn_blocks(4, lambda b: ysum[:, b, c * P:(c + 1) * P]).then_inc(mg_ps.h, 1)
                    pe.wait_ge(mg_sb.h, mg_sb.at(img, c + 1))
                    turn_blocks(4, lambda b: turned[:, b * P:(b + 1) * P]).then_inc(mg_tp.h, 1)
                if kind == "x":
                    if k == 0 and u == 0:
                        pe.wait_ge(gn_out.h, gn_out.at(img, 1))
                    if u:
                        pe.wait_ge(xd_sb.h, xd_sb.at(img, 2 * k + 1))
                    elif k:
                        pe.wait_ge(dt_abs.h, dt_abs.at(img, 2 * NC * k))
                    for c in range(NC):
                        rhs = U[:, c, :]
                        rhs = transposed(rhs)[:, u * 16:u * 16 + 16, :] if cols else rhs[:, u * HALF:(u + 1) * HALF]
                        mm = pe.matmul(ps[0:XR, 7, :], wx[:, c, cols + 2 * back, :], rhs, start=c == 0, stop=c == NC - 1)
                    mm.then_inc(xd_ps.h, 1)
                if kind == "d":
                    c, hf = u // 2, u % 2
                    at = 64 * (k % 2) + 32
                    if u == 0:
                        pe.wait_ge(xd_sb.h, xd_sb.at(img, 2 * k + 2))
                        pe.wait_ge(wd_in.h, wd_in.at(img, 16 * (k + 1)))
                    else:
                        pe.wait_ge(dt_abs.h, dt_abs.at(img, 2 * NC * k + u))
                    pe.matmul(ps[:, 7, :], w_dt[at:at + R, c * P:(c + 1) * P], xdbl[at:at + R, hf * HALF:(hf + 1) * HALF],
                              start=True, stop=True).then_inc(dt_ps.h, 1)
                if kind == "s" and u >= LAG:
                    i = u - LAG
                    pe.wait_ge(hc_sb.h, hc_sb.at(img, i + 1))
                    if i % GN_ == 0:
                        if i == 0:
                            pe.wait_ge(gn_out.h, gn_out.at(img, 1))
                        elif 0 <= i // GN_ - (STEPS1 // 2 // GN_ - NC + 1) < NC:
                            pe.wait_ge(mg_y.h, mg_y.at(img, i // GN_ - (STEPS1 // 2 // GN_ - NC)))
                        else:
                            pe.wait_ge(y_sb.h, y_sb.at(img, i // GN_))
                        if i >= NC * GN_:
                            c = i // GN_ % NC
                            for b in range(0, LB, 4):
                                pe.matmul(ps[:, 4 + b // 4, :], ident[:, :], ysum[:, b:b + 4, c * P:(c + 1) * P],
                                          start=True, stop=False, skip_group_check=True)
                    if beside >= 2:
                        products_ready(img + 1, beside)
                    for b in range(LB):
                        mm = pe.matmul(ps[:, 4 + b // 4, (b % 4) * P:(b % 4 + 1) * P],
                                       state[i % HELD][:, b * P:(b + 1) * P], ident[:, :],
                                       start=i < NC * GN_ and i % GN_ == 0 and b % 4 == 0, stop=i % GN_ == GN_ - 1,
                                       is_transpose=True, skip_group_check=True)
                        if beside >= 2:
                            pv = product(beside, b)
                    mm.then_inc(y_ps.h, 1)
                    if beside >= 2:
                        pv.then_inc(pv_ps.h, 1)

            def layers_1_to_3(img, ahead=True):
                pe.wait_ge(ln_o.h, ln_o.at(img, 1))
                for c in range(NC):
                    if c == 2:
                        pe.wait_ge(g_sb.h, g_sb.at(img, 1))
                    for b in range(LB):
                        mm = pe.matmul(ps[:, 2 * (c % 2) + b // 4, (b % 4) * P:(b % 4 + 1) * P],
                                       ysum[:, b, c * P:(c + 1) * P], ident[:, :], start=True, stop=True,
                                       is_transpose=True)
                    mm.then_inc(lt_ps.h, 1)
                if ahead:
                    turn_v(img + 1, 0)
                group_norm(img, 1)
                pe.wait_ge(s2_ld.h, s2_ld.at(img, 64))
                pe.wait_ge(ws_in.h, ws_in.at(img, 16))
                for r in range(6):
                    if r >= 2:
                        pe.wait_ge(m2_sb.h, m2_sb.at(img, r - 1))
                    for j in range(4):
                        gh = 4 * r + j
                        mm = pe.matmul(ps[:, r % 2, j * P:(j + 1) * P], rows2[:, 4 * gh:4 * gh + 4, :], shift_y[:, gh // 2, :],
                                       start=True, stop=True)
                    mm.then_inc(m2_ps.h, 1)
                for r in range(6):
                    pe.wait_ge(m2_sb.h, m2_sb.at(img, r + 1))
                    if r >= 2:
                        pe.wait_ge(o2_sb.h, o2_sb.at(img, r - 1))
                    for j in range(4):
                        gh = 4 * r + j
                        for q in range(4):
                            mm = pe.matmul(ps[32 * q:32 * q + 32, 2 + r % 2, j * P:(j + 1) * P],
                                           mid2[:, gh, 32 * q:32 * q + 32], shift_x[:, q * PG + gh // 2, :],
                                           start=True, stop=True)
                    mm.then_inc(o2_ps.h, 1)

                if ahead:
                    turn_v(img + 1, 1)
                group_norm(img, 2)
                if ahead:
                    turn_v(img + 1, 2)
                pe.wait_ge(gn_out.h, gn_out.at(img, 3))
                pe.wait_ge(w3_in.h, w3_in.at(img, 96))
                for i in range(4):
                    if i >= 2:
                        pe.wait_ge(p3_sb.h, p3_sb.at(img, i - 1))
                    w = (wq3, wk3)[i // 2]
                    project(banks(2 * (i % 2)), w[:, :, (i % 2) * QC3:(i % 2 + 1) * QC3], rows_of(xn3), QC3)\
                        .then_inc(p3_ps.h, 1)
                if ahead:
                    pe.wait_ge(lv_sb.h, lv_sb.at(img + 1, NC))
                for b in range(LB):
                    if b >= 2:
                        pe.wait_ge(v3_sb.h, v3_sb.at(img, b - 1))
                    for c in range(NC):
                        mm = pe.matmul(ps[:, 4 + b % 2, 0:C], xn3[:, c, b * P:(b + 1) * P], wv3[:, c, :],
                                       start=c == 0, stop=c == NC - 1)
                    mm.then_inc(v3_ps.h, 1)
                pe.wait_ge(p3_sb.h, p3_sb.at(img, 4))
                pe.wait_ge(v3_sb.h, v3_sb.at(img, LB))

                def scores3(u):
                    if u >= 2:
                        pe.wait_ge(s3_ex.h, s3_ex.at(img, u - 1))
                    for hf in range(2):
                        for a in range(2):
                            mm = pe.matmul(ps[:, 2 * (u % 2) + hf, :], q3[0:QC3, a, u * P:(u + 1) * P],
                                           k3[0:QC3, a, hf * HALF:(hf + 1) * HALF], start=a == 0, stop=a == 1)
                    mm.then_inc(s3_ps.h, 1)

                def turn3(u):
                    pe.wait_ge(s3_nm.h, s3_nm.at(img, u + 1))
                    if u:
                        pe.wait_ge(s3_ts.h, s3_ts.at(img, u))
                    for b in range(LB):
                        mm = pe.matmul(ps[:, 4 + b // 4, (b % 4) * P:(b % 4 + 1) * P],
                                       prob3[u % 2][:, b * P:(b + 1) * P], ident[:, :],
                                       start=True, stop=True, is_transpose=True)
                    mm.then_inc(s3_tp.h, 1)

                def values3(hf):
                    pe.wait_ge(s3_ts.h, s3_ts.at(img, 4 * hf + 4))
                    for m in range(NC):
                        i = hf * NC + m
                        if i >= 2:
                            pe.wait_ge(y3_sb.h, y3_sb.at(img, i - 1))
                        for b in range(LB):
                            mm = pe.matmul(ps[:, 6 + i % 2, :], vT3[:, b, m * P:(m + 1) * P], prT3[hf][:, b, :],
                                           start=b == 0, stop=b == LB - 1)
                        mm.then_inc(y3_ps.h, 1)

                for u in range(LB + 1):
                    if u < LB:
                        scores3(u)
                    if u >= 1:
                        turn3(u - 1)
                    if u == 5:
                        values3(0)
                values3(1)
                pe.wait_ge(se_pool.h, se_pool.at(img, 1))
                for c in range(NC):
                    mm = pe.matmul(ps[0:SE, 0, 0:1], wse1[:, c, :], se_t[:, 8 + c:9 + c], start=c == 0, stop=c == NC - 1)
                mm.then_inc(se_h.h, 1)
                pe.wait_ge(se_hr.h, se_hr.at(img, 1))
                for c in range(NC):
                    mm = pe.matmul(ps[:, 1, c:c + 1], wse2[:, c * P:(c + 1) * P], se_t[0:SE, 12:13], start=True, stop=True)
                mm.then_inc(se_z.h, 1)
                pe.wait_ge(se_w.h, se_w.at(img, 1))
                pe.wait_ge(y3_sb.h, y3_sb.at(img, 2 * NC))
                for m in range(NC):
                    if m == 2:
                        pe.wait_ge(f_sb.h, f_sb.at(img, 1))
                    project(banks(2 * (m % 2)), wg3[:, :, m * P:(m + 1) * P], rows_of(y3)).then_inc(f_ps.h, 1)


            pe.wait_ge(c_in.h, 16 * 14)
            before_attention(0)
            for ev in schedule(True, False):
                attention(0, *ev, alone=True)
            for m in range(NC):
                turn_v(0, m)
            after_attention(0)
            with pe.Fori(0, B - 1) as img:
                before_attention(img + 1, norm=img)
                beside = 0
                for ev in schedule(True, True):
                    if ev[0] == "p" and ev[1] <= STEPS0:
                        beside = ev[1]
                    elif ev[0] in "oape":
                        attention(img + 1, *ev)
                    elif ev[0] == "s":
                        scan(img, *ev, beside=beside)
                        beside = 0
                    else:
                        scan(img, *ev)
                layers_1_to_3(img)
                after_attention(img + 1)
            group_norm(B - 1, 0)
            for ev in schedule(False, True):
                scan(B - 1, *ev)
            layers_1_to_3(B - 1, ahead=False)

        @block.scalar
        def _(act):
            act.wait_ge(c_in.h, 16 * 14)
            act.activation(negA[:, :], negA[:, :], ACT.Exp).then_inc(pre_a.h, 1)
            act.wait_ge(pre_v.h, 1)
            for which, n in enumerate((PG, POS)):
                at = 1024 + which * 8192
                for lo, wide in [(at, n * 32)] + [(at + 2048 + 64 * j, n) for j in range(5)]:
                    act.activation(R_[:, lo:lo + wide], R_[:, lo:lo + wide], ACT.Exp, scale=-2.0).then_inc(pre_a.h, 1)
            act.wait_ge(pre_v.h, 3)

            def before_attention(img):
                for i in range(6):
                    act.wait_ge(qk_ps.h, qk_ps.at(img, i + 1))
                    if i < 3:
                        act.activation(q4[:, i, :], banks(2 * (i % 2)), ACT.Identity, bias=qb[:, i:i + 1], scale=SC0)\
                            .then_inc(qk_sb.h, 1)
                    else:
                        act.activation(k4[:, i - 3, :], banks(2 * (i % 2)), ACT.Identity, bias=vec("bk", i - 3))\
                            .then_inc(qk_sb.h, 1)

            def attention(img, kind, a, alone=False):
                if kind != "e":
                    return
                if a < STEPS0:
                    act.wait_ge(s_max.h, s_max.at(img, a + 1))
                    if a >= 2:
                        act.wait_ge(t_ps.h, t_ps.at(img, a - 1))
                    act.activation(probs[a % 2], banks(4 * (a % 2) if alone else 0), ACT.Exp, bias=negmax[:, a % 8:a % 8 + 1],
                                   accum_out=rowsum[:, a % 8:a % 8 + 1]).then_inc(s_exp.h, 1)
                if 1 <= a <= STEPS0:
                    u = a - 1
                    act.wait_ge(t_ps.h, t_ps.at(img, u + 1))
                    if u >= 2:
                        act.wait_ge(pv_ps.h, pv_ps.at(img, u - 1))
                    act.activation(probsT[u % 2].rearrange("p b q -> p (b q)"), banks(2), ACT.Copy)\
                        .then_inc(t_sb.h, 1)

            def pad_v(img, m):
                act.wait_ge(lv_ps.h, lv_ps.at(img, m + 1))
                if m:
                    act.wait_ge(lp_sb.h, lp_sb.at(img, m))
                inner = vpad.rearrange("p (h w) -> p h w", w=36)[:, 2:34, 2:34]
                act.activation(inner, banks(4).rearrange("p (h w) -> p h w", w=WW), ACT.Identity, bias=vec("bv", m))\
                    .then_inc(lv_sb.h, 1)

            def after_attention(img):
                for m in range(NC):
                    act.wait_ge(vo_ps.h, vo_ps.at(img, m + 1))
                    if m == 2:
                        act.wait_ge(r_sb.h, r_sb.at(img, 1))
                    act.activation(gate0[m % 2], banks(2 * (m % 2)), ACT.Identity, bias=vec("bo", m)).then_inc(vo_sb.h, 1)

            def scan(img, kind, k, u=0):
                if kind in "xdlt":
                    cols, back = DIRS[k]
                if kind in "sym":
                    u = k
                if kind == "x":
                    act.wait_ge(xd_ps.h, xd_ps.at(img, 2 * k + u + 1))
                    at = 64 * (k % 2)
                    if k >= 2 and u == 0:
                        act.wait_ge(bc_st.h, bc_st.at(img, 32 * (k - 1)))
                    act.activation(xdbl[at:at + XR, u * HALF:(u + 1) * HALF], ps[0:XR, 7, :], ACT.Copy).then_inc(xd_sb.h, 1)
                if kind == "d":
                    c, hf = u // 2, u % 2
                    part = dtu[:, c, hf * HALF:(hf + 1) * HALF]
                    act.wait_ge(dt_ps.h, dt_ps.at(img, 2 * NC * k + u + 1))
                    act.activation(dt[:, c, hf * HALF:(hf + 1) * HALF], ps[:, 7, :], ACT.Relu,
                                   bias=vec(f"dtb{cols + 2 * back}", c))
                    act.activation(part, ps[:, 7, :], ACT.Abs, bias=vec(f"dtb{cols + 2 * back}", c)).then_inc(dt_abs.h, 1)
                    act.drain()
                    act.activation(part, part, ACT.Exp, scale=-1.0)
                if kind == "l":
                    act.drain()
                    act.activation(dtu[:, u, :], dtu[:, u, :], ACT.Ln, bias=1.0).then_inc(dt_ln.h, 1)
                if kind == "y":
                    act.wait_ge(y_ps.h, y_ps.at(img, GN_ * (u + 1)))
                    act.activation(ysum[:, :, (u % NC) * P:(u % NC + 1) * P], banks(4).rearrange("p (b c) -> p b c", b=LB),
                                   ACT.Copy).then_inc(y_sb.h, 1)
                if kind == "s" and u < STEPS1:
                    i, k, c, n = place(u)
                    cols, back = DIRS[k]
                    if n == 0:
                        act.wait_ge(dt_sum.h, dt_sum.at(img, k * NC + c + 1))
                    if i >= 2:
                        act.wait_ge(h_sb.h, h_sb.at(img, i - 1))
                    elif i == 0:
                        act.wait_ge(gn_out.h, gn_out.at(img, 1))
                    col = (cols + 2 * back) * NC * N + c * N + n
                    act.activation(decay[i % 2], dt[:, c, :], ACT.Exp, scale=negA[:, col:col + 1]).then_inc(a_sb.h, 1)

            def layers_1_to_3(img, ahead=True):
                for c in range(NC):
                    act.wait_ge(lt_ps.h, lt_ps.at(img, c + 1))
                    if c == 2:
                        act.wait_ge(x2.h, x2.at(img, 1))
                    act.activation(gel[c % 2], banks(2 * (c % 2)), ACT.Gelu, bias=vec("ln_b", c), scale=vec("ln_w", c))\
                        .then_inc(g_sb.h, 1)
                if ahead:
                    pad_v(img + 1, 0)
                for r in range(6):
                    act.wait_ge(m2_ps.h, m2_ps.at(img, r + 1))
                    act.activation(mid2[:, 4 * r:4 * r + 4, :].rearrange("p a m -> p (a m)"), ps[:, r % 2, :], ACT.Copy)\
                        .then_inc(m2_sb.h, 1)
                if ahead:
                    pad_v(img + 1, 1)
                    pad_v(img + 1, 2)
                for i in range(4):
                    act.wait_ge(p3_ps.h, p3_ps.at(img, i + 1))
                    if i < 2:
                        act.activation(q3[0:QC3, i, :], banks(2 * (i % 2))[0:QC3, :], ACT.Identity,
                                       bias=qb3[0:QC3, i:i + 1], scale=SC3).then_inc(p3_sb.h, 1)
                    else:
                        act.activation(k3[0:QC3, i - 2, :], banks(2 * (i % 2))[0:QC3, :], ACT.Identity,
                                       bias=vec96[0:QC3, i:i + 1]).then_inc(p3_sb.h, 1)

                def exps3(u):
                    act.wait_ge(s3_mx.h, s3_mx.at(img, u + 1))
                    if u >= 2:
                        act.wait_ge(s3_tp.h, s3_tp.at(img, u - 1))
                    act.activation(prob3[u % 2], banks(2 * (u % 2)), ACT.Exp, bias=se_t[:, 16 + u:17 + u],
                                   accum_out=se_t[:, 24 + u:25 + u]).then_inc(s3_ex.h, 1)

                def turned3(u):
                    act.wait_ge(s3_tp.h, s3_tp.at(img, u + 1))
                    hf, j = u // 4, u % 4
                    act.activation(prT3[hf][:, :, j * P:(j + 1) * P], banks(4).rearrange("p (b q) -> p b q", b=LB),
                                   ACT.Copy).then_inc(s3_ts.h, 1)

                def values3(hf):
                    for m in range(NC):
                        i = hf * NC + m
                        act.wait_ge(y3_ps.h, y3_ps.at(img, i + 1))
                        act.activation(y3[:, m, hf * HALF:(hf + 1) * HALF], ps[:, 6 + i % 2, :], ACT.Identity,
                                       bias=vec("bv3", m), accum_out=se_t[:, i:i + 1]).then_inc(y3_sb.h, 1)

                for u in range(LB + 1):
                    if u < LB:
                        exps3(u)
                    if u >= 1:
                        turned3(u - 1)
                    if u == 5:
                        values3(0)
                values3(1)
                act.wait_ge(se_zb.h, se_zb.at(img, 1))
                act.activation(se_t[:, 36:39], se_t[:, 33:36], ACT.Exp, scale=-1.0).then_inc(se_e.h, 1)

            before_attention(0)
            for ev in schedule(True, False):
                attention(0, *ev, alone=True)
            for m in range(NC):
                pad_v(0, m)
            after_attention(0)
            with act.Fori(0, B - 1) as img:
                before_attention(img + 1)
                for ev in schedule(True, True):
                    if ev[0] in "oape":
                        attention(img + 1, *ev)
                    else:
                        scan(img, *ev)
                layers_1_to_3(img)
                after_attention(img + 1)
            for ev in schedule(False, True):
                scan(B - 1, *ev)
            layers_1_to_3(B - 1, ahead=False)

        @block.gpsimd
        def _(pool):
            pool.memset(half_neg[:, :], -0.5).then_inc(pre_g.h, 1)
            pool.wait_ge(pre_g.h, 1)
            pool.wait_ge(pre_v.h, 3)
            pool.tensor_tensor(inv3, tmp_d[:, 0:3], half_neg[:, 0:3], ALU.pow).then_inc(pre_g.h, 1)

            def before_attention(img):
                pool.wait_ge(g0_eps.h, g0_eps.at(img, 1))
                pool.tensor_tensor(gn0_t[:, 32:35], gn0_t[:, 24:27], half_neg[:, 0:3], ALU.pow).then_inc(g0_rstd.h, 1)

            def group_norm(img, g):
                pool.wait_ge(gn_eps.h, gn_eps.at(img, g + 1))
                pool.tensor_tensor(gn_t[:, 32:35], gn_t[:, 24:27], half_neg[:, 0:3], ALU.pow).then_inc(gn_rstd.h, 1)

            def scan(img, kind, k, u=0):
                if kind in "xdlt":
                    cols, back = DIRS[k]
                if kind in "sym":
                    u = k
                if kind == "t":
                    c = u
                    pool.wait_ge(dt_sum.h, dt_sum.at(img, k * NC + c + 1))
                    u_in, d_in, d_out = U[:, c, :], dt[:, c, :], dtu[:, c, :]
                    if cols:
                        u_in = transposed(u_in)
                        d_in, d_out = (a.rearrange("p (w h) -> p w h", h=HH) for a in (d_in, d_out))
                    pool.tensor_tensor(d_out, d_in, u_in, ALU.mult).then_inc(dt_sb.h, 1)
                if kind == "s" and 1 <= u <= STEPS1:
                    i, k, c, n = place(u - 1)
                    pool.wait_ge(h_sb.h, h_sb.at(img, i + 1))
                    pool.tensor_tensor(state[i % HELD], state[i % HELD], bc[(k * N + n) % SLOTS][:, 1, :], ALU.mult)\
                        .then_inc(hc_sb.h, 1)

            def layers_1_to_3(img, ahead=True):
                pool.wait_ge(ln_st.h, ln_st.at(img, 1))
                pool.tensor_tensor(ln_t[:, 16:24], ln_t[:, 24:32], half_neg[:, 0:8], ALU.pow).then_inc(ln_r.h, 1)
                group_norm(img, 1)
                group_norm(img, 2)

            before_attention(0)
            with pool.Fori(0, B - 1) as img:
                before_attention(img + 1)
                group_norm(img, 0)
                for ev in schedule(False, True):
                    scan(img, *ev)
                layers_1_to_3(img)
            group_norm(B - 1, 0)
            for ev in schedule(False, True):
                scan(B - 1, *ev)
            layers_1_to_3(B - 1, ahead=False)

        @block.vector
        def _(v):
            v.wait_ge(c_in.h, 16 * 14)
            v.memset(shifts, 0.0)
            sidx, yrow = R_[:, 0:1], R_[:, 32:64]
            kinds = []
            for which, (n, off) in enumerate(((PG, R_[:, 64:64 + 2 * PG].rearrange("p (g d) -> p g d", d=2)[:, :, 1]),
                                              (POS, R_[:, 96:96 + 2 * POS].rearrange("p (g d) -> p g d", d=2)[:, :, 0]))):
                at = 1024 + which * 8192
                expo = R_[:, at:at + n * 32].rearrange("p (g y) -> p g y", y=32)
                band = R_[:, at + 4096:at + 4096 + n * 32].rearrange("p (g y) -> p g y", y=32)
                taps = [R_[:, at + 2048 + 64 * j:at + 2048 + 64 * j + n] for j in range(5)]
                rnd, sub, moved, keep, tot = (R_[:, at + 3072 + 64 * j:at + 3072 + 64 * j + n] for j in range(5))
                MAGIC = 12582912.0
                v.tensor_scalar(rnd, off, MAGIC, None, ALU.add)
                v.drain()
                v.tensor_scalar(rnd, rnd, MAGIC, None, ALU.subtract)
                v.drain()
                v.tensor_tensor(sub, off, rnd, ALU.subtract)
                v.drain()
                v.tensor_scalar(sub, sub, 0.5, -0.5, ALU.min, ALU.max)
                v.tensor_scalar(moved, rnd, sidx, None, ALU.add)
                v.drain()
                v.tensor_scalar(keep, moved, 0.0, None, ALU.is_ge)
                v.tensor_scalar(tot, moved, 31.0, None, ALU.is_le)
                v.drain()
                v.tensor_tensor(keep, keep, tot, ALU.mult)
                v.tensor_tensor(band, moved[:, :, None].to_broadcast([P, n, 32]),
                                yrow[:, None, :].to_broadcast([P, n, 32]), ALU.subtract)
                v.drain()
                v.tensor_tensor(expo, band, sub[:, :, None].to_broadcast([P, n, 32]), ALU.add)
                v.drain()
                v.tensor_tensor(expo, expo, expo, ALU.mult)
                v.tensor_tensor(band, band, band, ALU.mult)
                v.drain()
                v.tensor_scalar(band, band, 4.5, None, ALU.is_le)
                for j in range(5):
                    v.tensor_scalar(taps[j], sub, float(j - 2), None, ALU.add)
                v.drain()
                for j in range(5):
                    ins = v.tensor_tensor(taps[j], taps[j], taps[j], ALU.mult)
                kinds.append((n, expo, band, taps, keep, tot))
            ins.then_inc(pre_v.h, 1)
            v.wait_ge(pre_a.h, 1 + 2 * 6)
            for which, (n, expo, band, taps, keep, tot) in enumerate(kinds):
                v.tensor_tensor(tot, taps[0], taps[1], ALU.add)
                for j in range(2, 5):
                    v.drain()
                    v.tensor_tensor(tot, tot, taps[j], ALU.add)
                v.drain()
                v.reciprocal(tot, tot)
                v.drain()
                v.tensor_tensor(keep, keep, tot, ALU.mult)
                v.tensor_tensor(expo, expo, band, ALU.mult)
                v.drain()
                v.tensor_tensor(expo, expo, keep[:, :, None].to_broadcast([P, n, 32]), ALU.mult)
                v.drain()
                dst = (shifts[:, POS * P:] if which == 0 else shifts[:, 0:POS * P]).rearrange("p (g q y) -> p g q y", q=4, y=32)
                for q in range(4):
                    ins = v.tensor_copy(dst[32 * q:32 * q + 32, :, q, :], expo[32 * q:32 * q + 32, :, :])
            ins.then_inc(pre_v.h, 1)
            v.tensor_scalar(negA[:, :], negA[:, :], -1.0, None, ALU.mult)
            v.tensor_scalar(qb, vecs[:, VEC["bq"] * NC:VEC["bq"] * NC + NC], SC0, None, ALU.mult)
            v.tensor_scalar(qb3[0:QC3, :], vec96[0:QC3, 0:2], SC3, None, ALU.mult)

            def vec3(name):
                return vecs[:, VEC[name] * NC:VEC[name] * NC + NC]
            v.tensor_tensor(dsum, vec3("D0"), vec3("D1"), ALU.add)
            v.drain()
            v.tensor_tensor(dsum, dsum, vec3("D2"), ALU.add)
            v.drain()
            v.tensor_tensor(dsum, dsum, vec3("D3"), ALU.add)
            v.tensor_scalar(tmp_d[:, 0:3], vec3("var"), EPS, None, ALU.add).then_inc(pre_v.h, 1)
            v.wait_ge(pre_g.h, 2)
            v.tensor_tensor(inv3, inv3, vec3("gamma"), ALU.mult)
            v.tensor_tensor(cst3, vec3("bproj3"), vec3("mean"), ALU.subtract)
            v.drain()
            v.tensor_tensor(cst3, cst3, inv3, ALU.mult)
            v.drain()
            v.tensor_tensor(cst3, cst3, vec3("beta"), ALU.add)
            v.drain()

            def channel_stats(src, t):
                for c in range(NC):
                    for hf in range(2):
                        v.bn_stats(stats[:, c * 12 + hf * 6:c * 12 + hf * 6 + 6], src[:, c, hf * HALF:(hf + 1) * HALF])
                v.drain()
                agg = t[:, 6:12].rearrange("p (c s) -> p c s", s=2)
                for c in range(NC):
                    v.bn_aggr(agg[:, c, :], stats[:, c * 12:c * 12 + 12])
                v.drain()
                return v.tensor_copy(t[:, 0:3], agg[:, :, 0])

            def deviation(t):
                v.tensor_copy(t[:, 3:6], ps[:, 7, 0:3])
                v.drain()
                v.tensor_tensor(t[:, 12:15], t[:, 0:3], t[:, 3:6], ALU.subtract)
                v.drain()
                v.tensor_tensor(t[:, 12:15], t[:, 12:15], t[:, 12:15], ALU.mult)
                v.drain()
                return v.tensor_tensor(t[:, 16:19], t[:, 12:15], t[:, 7:12:2], ALU.add)

            def normalize(dst, src, t):
                for c in range(NC):
                    ins = v.tensor_scalar(dst[:, c, :], src[:, c, :], t[:, 3 + c:4 + c], t[:, 32 + c:33 + c],
                                          ALU.subtract, ALU.mult)
                return ins

            def group_norm(img, g, dst):
                channel_stats(X3, gn_t).then_inc(gn_stat.h, 1)
                v.wait_ge(gn_mean.h, gn_mean.at(img, g + 1))
                deviation(gn_t).then_inc(gn_dev.h, 1)
                v.wait_ge(gn_var.h, gn_var.at(img, g + 1))
                v.tensor_scalar(gn_t[:, 24:27], ps[:, 7, 8:11], EPS, None, ALU.add).then_inc(gn_eps.h, 1)
                v.wait_ge(gn_rstd.h, gn_rstd.at(img, g + 1))
                normalize(dst, X3, gn_t).then_inc(gn_out.h, 1)

            def before_attention(img, norm=None):
                v.wait_ge(xa_in.h, xa_in.at(img, 16))
                channel_stats(xa0, gn0_t).then_inc(g0_stat.h, 1)
                v.wait_ge(g0_mean.h, g0_mean.at(img, 1))
                deviation(gn0_t).then_inc(g0_dev.h, 1)
                v.wait_ge(g0_var.h, g0_var.at(img, 1))
                v.tensor_scalar(gn0_t[:, 24:27], ps[:, 7, 8:11], EPS, None, ALU.add).then_inc(g0_eps.h, 1)
                v.wait_ge(g0_rstd.h, g0_rstd.at(img, 1))
                normalize(xa0, xa0, gn0_t).then_inc(g0_out.h, 1)
                if norm is not None:
                    group_norm(norm, 0, U)
                for b in range(LB):
                    v.wait_ge(vt_ps.h, vt_ps.at(img, b + 1))
                    v.tensor_copy(vT[:, b, :], ps[:, 4 + b % 2, 0:C]).then_inc(vt_sb.h, 1)

            def attention(img, kind, a, alone=False):
                if kind == "o" and a >= 3:
                    u = a - 3
                    v.wait_ge(s_exp.h, s_exp.at(img, u + 1))
                    v.reciprocal(rowinv[:, u % 8:u % 8 + 1], rowsum[:, u % 8:u % 8 + 1])
                    v.drain()
                    v.wait_ge(pv_ps.h, pv_ps.at(img, u + 1))
                    v.tensor_scalar(heads[:, u % LB, HD * (u // LB):HD * (u // LB) + HD], ps[:, 6, 0:HD],
                                    rowinv[:, u % 8:u % 8 + 1], None, ALU.mult).then_inc(o_sb.h, 1)
                if kind == "e" and a < STEPS0:
                    v.wait_ge(s_ps.h, s_ps.at(img, a + 1))
                    v.tensor_reduce(negmax[:, a % 8:a % 8 + 1], banks(4 * (a % 2) if alone else 0), AX.X, ALU.max, negate=True)\
                        .then_inc(s_max.h, 1)

            def depthwise(img, m):
                vp = vpad.rearrange("p (h w) -> p h w", w=36)
                sum3 = res[:, m, :].rearrange("p (h w) -> p h w", w=WW)
                v.wait_ge(lv_sb.h, lv_sb.at(img, m + 1))
                for j in range(25):
                    win = vp[:, j // 5:j // 5 + HH, j % 5:j % 5 + WW]
                    w = lepe_w[:, m * 25 + j:m * 25 + j + 1]
                    if j == 0:
                        v.tensor_scalar(sum3, win, w, vec("lepe_b", m), ALU.mult, ALU.add)
                    else:
                        v.drain()
                        ins = v.scalar_tensor_tensor(sum3, win, w, sum3, ALU.mult, ALU.add)
                ins.then_inc(lp_sb.h, 1)

            def after_attention(img):
                v.wait_ge(xb_in.h, xb_in.at(img, 16))
                normalize(xn0, xn0, gn0_t).then_inc(g0_again.h, 1)
                for m in range(NC):
                    v.wait_ge(hT_ps.h, hT_ps.at(img, m + 1))
                    v.scalar_tensor_tensor(res[:, m, :], banks(4 + 2 * (m % 2)), vec("bv", m), res[:, m, :], ALU.add, ALU.add)
                    v.drain()
                    v.wait_ge(vo_sb.h, vo_sb.at(img, m + 1))
                    v.tensor_tensor(res[:, m, :], res[:, m, :], gate0[m % 2], ALU.mult).then_inc(r_sb.h, 1)
                v.wait_ge(xr_in.h, xr_in.at(img, 16))
                for m in range(NC):
                    v.wait_ge(p0_ps.h, p0_ps.at(img, m + 1))
                    v.scalar_tensor_tensor(X3[:, m, :], banks(2 * (m % 2)), vec("proj_b", m), X3[:, m, :],
                                           ALU.add, ALU.add).then_inc(x1.h, 1)
                v.drain()

            def scan(img, kind, k, u=0):
                if kind in "xdlt":
                    cols, back = DIRS[k]
                if kind in "sym":
                    u = k
                if kind == "m":
                    c = u
                    v.wait_ge(mg_ps.h, mg_ps.at(img, c + 1))
                    v.scalar_tensor_tensor(turned.rearrange("p (h w) -> p h w", w=WW),
                                           U[:, c, :].rearrange("p (h w) -> p h w", w=WW), dsum[:, c:c + 1],
                                           banks(4).rearrange("p (w h) -> p h w", h=HH), ALU.mult, ALU.add)\
                        .then_inc(mg_sb.h, 1)
                    v.wait_ge(mg_tp.h, mg_tp.at(img, c + 1))
                    v.tensor_copy(ysum[:, :, c * P:(c + 1) * P], banks(4).rearrange("p (b c) -> p b c", b=LB))\
                        .then_inc(mg_y.h, 1)
                    v.drain()
                if kind == "t":
                    v.wait_ge(dt_ln.h, dt_ln.at(img, k * NC + u + 1))
                    v.tensor_tensor(dt[:, u, :], dt[:, u, :], dtu[:, u, :], ALU.add).then_inc(dt_sum.h, 1)
                if kind == "s":
                    if u < STEPS1:
                        i, k, c, n = place(u)
                        slot = (k * N + n) % SLOTS
                        if c == 0:
                            v.wait_ge(bc_ld[slot].h, bc_ld[slot].at(img, 16 * ((k * N + n) // SLOTS + 1)))
                        if n == 0:
                            v.wait_ge(dt_sb.h, dt_sb.at(img, k * NC + c + 1))
                        if i >= HELD:
                            v.wait_ge(y_ps.h, y_ps.at(img, i - HELD + 1))
                        v.tensor_tensor(state[i % HELD], dtu[:, c, :], bc[slot][:, 0, :], ALU.mult).then_inc(b_sb.h, 1)
                    if 1 <= u <= STEPS1:
                        i, k, c, n = place(u - 1)
                        back = DIRS[k][1]
                        v.wait_ge(a_sb.h, a_sb.at(img, i + 1))
                        v.wait_ge(b_sb.h, b_sb.at(img, i + 1))
                        d, s = decay[i % 2], state[i % HELD]
                        if back:
                            d, s = d[:, ::-1], s[:, ::-1]
                        v.tensor_tensor_scan(s, d, s, 0.0, ALU.mult, ALU.add).then_inc(h_sb.h, 1)

            def layers_1_to_3(img, ahead=True):
                v.wait_ge(y_sb.h, y_sb.at(img, STEPS1 // GN_))
                if ahead:
                    v.memset(vpad, 0.0)
                bst = stats[:, 0:48].rearrange("p (b s) -> p b s", s=6)
                for b in range(LB):
                    v.bn_stats(bst[:, b, :], ysum[:, b, :])
                v.drain()
                agg = ln_t[:, 0:16].rearrange("p (b s) -> p b s", s=2)
                for b in range(LB):
                    v.bn_aggr(agg[:, b, :], bst[:, b, :])
                v.drain()
                v.tensor_scalar(ln_t[:, 24:32], agg[:, :, 1], EPS, None, ALU.add).then_inc(ln_st.h, 1)
                v.wait_ge(ln_r.h, ln_r.at(img, 1))
                for b in range(LB):
                    ins = v.tensor_scalar(ysum[:, b, :], ysum[:, b, :], agg[:, b, 0:1], ln_t[:, 16 + b:17 + b],
                                          ALU.subtract, ALU.mult)
                ins.then_inc(ln_o.h, 1)
                for c in range(NC):
                    v.wait_ge(g_sb.h, g_sb.at(img, c + 1))
                    v.tensor_tensor(X3[:, c, :], X3[:, c, :], gel[c % 2], ALU.add).then_inc(x2.h, 1)
                v.drain()
                group_norm(img, 1, xn2)
                if ahead:
                    depthwise(img + 1, 0)
                for r in range(6):
                    v.wait_ge(o2_ps.h, o2_ps.at(img, r + 1))
                    v.tensor_copy(out2[:, 16 * r:16 * r + 16, :].rearrange("p a s -> p (a s)"), ps[:, 2 + r % 2, :])\
                        .then_inc(o2_sb.h, 1)
                if ahead:
                    depthwise(img + 1, 1)
                v.wait_ge(b2_ld.h, b2_ld.at(img, 16))
                ins = v.tensor_tensor(X[:, :], X[:, :], blur.rearrange("p c l -> p (c l)"), ALU.add)
                ins.then_inc(x3.h, 1)
                v.drain()
                group_norm(img, 2, xn3)
                for c in range(NC):
                    v.tensor_scalar(X3[:, c, :], X3[:, c, :], cst3[:, c:c + 1], None, ALU.add)
                if ahead:
                    depthwise(img + 1, 2)
                for b in range(LB):
                    v.wait_ge(v3_ps.h, v3_ps.at(img, b + 1))
                    v.tensor_copy(vT3[:, b, :], ps[:, 4 + b % 2, 0:C]).then_inc(v3_sb.h, 1)

                def rowmax3(u):
                    v.wait_ge(s3_ps.h, s3_ps.at(img, u + 1))
                    v.tensor_reduce(se_t[:, 16 + u:17 + u], banks(2 * (u % 2)), AX.X, ALU.max, negate=True)\
                        .then_inc(s3_mx.h, 1)

                def normalize3(u):
                    v.wait_ge(s3_ex.h, s3_ex.at(img, u + 1))
                    v.reciprocal(se_t[:, 40 + u:41 + u], se_t[:, 24 + u:25 + u])
                    v.drain()
                    v.tensor_scalar(prob3[u % 2], prob3[u % 2], se_t[:, 40 + u:41 + u], None, ALU.mult)\
                        .then_inc(s3_nm.h, 1)

                for u in range(LB + 1):
                    if u < LB:
                        rowmax3(u)
                    if u >= 1:
                        normalize3(u - 1)
                v.wait_ge(y3_sb.h, y3_sb.at(img, 2 * NC))
                v.tensor_tensor(se_t[:, 8:11], se_t[:, 0:3], se_t[:, 3:6], ALU.add)
                v.drain()
                v.tensor_scalar(se_t[:, 8:11], se_t[:, 8:11], 1.0 / L, None, ALU.mult).then_inc(se_pool.h, 1)
                v.wait_ge(se_h.h, se_h.at(img, 1))
                v.tensor_scalar(se_t[0:SE, 12:13], ps[0:SE, 0, 0:1], vec96[0:SE, 4:5], 0.0, ALU.add, ALU.max)\
                    .then_inc(se_hr.h, 1)
                v.wait_ge(se_z.h, se_z.at(img, 1))
                v.tensor_tensor(se_t[:, 33:36], ps[:, 1, 0:3], vec3("bse2"), ALU.add).then_inc(se_zb.h, 1)
                v.wait_ge(se_e.h, se_e.at(img, 1))
                v.tensor_scalar(se_t[:, 50:53], se_t[:, 36:39], 1.0, None, ALU.add)
                v.drain()
                v.reciprocal(se_t[:, 54:57], se_t[:, 50:53])
                v.drain()
                for c in range(NC):
                    ins = v.tensor_scalar(wg3[:, c, :], wp3[:, c, :], se_t[:, 54 + c:55 + c], None, ALU.mult)
                ins.then_inc(se_w.h, 1)
                for m in range(NC):
                    v.wait_ge(f_ps.h, f_ps.at(img, m + 1))
                    v.scalar_tensor_tensor(X3[:, m, :], banks(2 * (m % 2)), inv3[:, m:m + 1], X3[:, m, :],
                                           ALU.mult, ALU.add).then_inc(f_sb.h, 1)

            before_attention(0)
            v.memset(vpad, 0.0)
            for ev in schedule(True, False):
                attention(0, *ev, alone=True)
            for m in range(NC):
                depthwise(0, m)
            after_attention(0)
            with v.Fori(0, B - 1) as img:
                before_attention(img + 1, norm=img)
                for ev in schedule(True, True):
                    if ev[0] in "oape":
                        attention(img + 1, *ev)
                    else:
                        scan(img, *ev)
                layers_1_to_3(img)
                after_attention(img + 1)
            group_norm(B - 1, 0, U)
            for ev in schedule(False, True):
                scan(B - 1, *ev)
            layers_1_to_3(B - 1, ahead=False)


def _chunks(a):
    return np.ascontiguousarray(a.reshape(NC, P, -1).transpose(1, 0, 2).reshape(P, -1))


def kernel(**inputs):
    import concourse.bacc as bacc
    from concourse.bass_utils import run_bass_kernel_spmd
    a = {n: np.asarray(v) for n, v in inputs.items()}
    ds, dtb = a["L1_conv_Ds"].reshape(K, C), a["L1_conv_dt_projs_bias"]
    qb_ = a["L0_conv_qkvo_b"]
    cols = [qb_[0:C], qb_[C:2 * C], qb_[2 * C:3 * C], qb_[3 * C:], a["L0_conv_lepe_b"], a["L0_conv_proj_b"],
            ds[0], ds[1], ds[2], ds[3], a["L1_conv_ln_weight"], a["L1_conv_ln_bias"], dtb[0], dtb[1], dtb[2], dtb[3],
            a["L3_conv_bv"], a["L3_conv_b_proj"], a["L3_conv_bn_gamma"], a["L3_conv_bn_beta"], a["L3_conv_bn_mean"],
            a["L3_conv_bn_var"], a["L3_conv_b_se2"]]
    vecs = np.stack([v.reshape(NC, P) for v in cols]).transpose(2, 0, 1).reshape(P, NV * NC)
    bq3, bk3 = a["L3_conv_bq"].reshape(2, QC3), a["L3_conv_bk"].reshape(2, QC3)
    vec96 = np.stack([bq3[0], bq3[1], bk3[0], bk3[1], a["L3_conv_b_se1"]], axis=1)
    xw = a["L1_conv_x_proj_weight"]
    xw = np.concatenate([xw[:, R:], xw[:, :R]], axis=1)
    chan = np.arange(C) // (C // GROUPS)
    same = (chan[:, None] == chan[None, :]).astype(np.float32) / (C // GROUPS)
    ga = same.reshape(NC, P, NC, P).transpose(1, 0, 2, 3).reshape(P, -1)
    w3 = lambda w: _chunks(w.T).reshape(P, NC, -1)
    arrays = {
        "x": a["x"].reshape(B, C, L),
        "ident": np.eye(P, dtype=np.float32),
        "group_avg": ga,
        "vecs": vecs, "vec96": vec96,
        "lepe_w": _chunks(a["L0_conv_lepe_w"].reshape(C, 25)),
        "A_logs": a["L1_conv_A_logs"].reshape(K, NC, P, N).transpose(2, 0, 1, 3).reshape(P, -1),
        "w_xproj": _chunks(xw.transpose(2, 0, 1).reshape(C, K * XR)),
        "w_dt": a["L1_conv_dt_projs_weight"][[cols + 2 * back for cols, back in DIRS]].transpose(2, 0, 1).reshape(R, K * C),
        "w_proj0": w3(a["L0_conv_proj_w"].reshape(C, C)),
        "row_index": (np.arange(P) % 32).astype(np.float32).reshape(P, 1),
        "col_row": np.tile(np.arange(32, dtype=np.float32), (P, 1)),
        "offset": a["L2_conv_offset"],
        "w_qkvo": w3(a["L0_conv_qkvo_w"].reshape(4 * C, C)),
        "wq3": w3(a["L3_conv_wq"]), "wk3": w3(a["L3_conv_wk"]), "wv3": w3(a["L3_conv_wv"]),
        "wp3": w3(a["L3_conv_w_proj"]), "wse1": w3(a["L3_conv_w_se1"]), "wse2": a["L3_conv_w_se2"].T,
    }
    nc = bacc.Bacc("TRN2", target_bir_lowering=False, num_devices=1, dynamic_dma_scratch_size=8192)
    t, feed = {}, {}
    for name, v in arrays.items():
        feed["in_" + name] = np.ascontiguousarray(v)
        t[name] = nc.dram_tensor("in_" + name, v.shape, F32, kind="ExternalInput").ap()
    t["out"] = nc.dram_tensor("out_0", (B, C, L), F32, kind="ExternalOutput").ap()
    for name, shape in [("bc_scratch", (K, 2 * N, L)), ("shift_scratch", (P, (POS + PG) * P)),
                        ("rows_scratch", (C, L)), ("blur_scratch", (C, L))]:
        t[name] = nc.dram_tensor(name, shape, F32, kind="Internal").ap()
    build(nc, t)
    r = run_bass_kernel_spmd(nc, [feed], core_ids=[0])
    return r.results[0]["out_0"].reshape(B, C, HH, WW)
```
